# Optimizing a Trainium2 kernel written in Bass

```python
import numpy as np
import jax
import jax.numpy as jnp

def _softmax(x, axis=-1):
    return jax.nn.softmax(x, axis=axis)

def _gelu(x):
    return jax.nn.gelu(x, approximate=True)

def _silu(x):
    return jax.nn.silu(x)

def _sigmoid(x):
    return jax.nn.sigmoid(x)

def _layernorm(x, axis=-1, eps=1e-05):
    m = jnp.mean(x, axis=axis, keepdims=True)
    v = jnp.var(x, axis=axis, keepdims=True)
    return (x - m) / jnp.sqrt(v + eps)

def _scatter_add(tgt, idx, src, axis=0):
    return tgt.at[idx].add(src)

def _segment_sum(src, seg, n):
    return jax.ops.segment_sum(src, seg, n)
kernel_name = 'mk_decoder_postln_d1_seqx_r4_a0d9e4'

def setup_inputs(seed: int=0):
    np.random.seed(seed)
    _w = jnp.asarray

    def _rec_inputs():
        import jax
        import jax.numpy as jnp
        _rk = jax.random.key(seed)
        x = -0.000125 + 0.9999 * jax.random.normal(jax.random.fold_in(_rk, 1), (4, 512, 512), jnp.float32)
        _lenS = 512 - jax.random.randint(jax.random.fold_in(_rk, 7), (4,), 0, max(1, 512 // 4) + 1, jnp.int32)
        _lenS2 = 512 - jax.random.randint(jax.random.fold_in(_rk, 8), (4,), 0, max(1, 512 // 4) + 1, jnp.int32)
        itok_BxS_13_99985 = jax.random.randint(jax.random.fold_in(_rk, 11), (4, 512), 13, 99986, jnp.int32)
        _ctx_2048P = jax.random.normal(jax.random.fold_in(_rk, 12), (4, 16, 512), jnp.float32)
        _ctx_2048c = jax.random.dirichlet(jax.random.fold_in(_rk, 512), 0.3 * jnp.ones((16,), jnp.float32), (4, 512))
        _ctx_2048t = jnp.einsum('bsk,bkd->bsd', _ctx_2048c, _ctx_2048P)
        _ctx_2048t = _ctx_2048t * jax.lax.rsqrt(jnp.mean(jnp.square(_ctx_2048t)) + 1e-12) * 0.953939
        ctx_2048 = 6.82029e-06 + 0.0200006 * (_ctx_2048t + 0.3 * jax.random.normal(jax.random.fold_in(_rk, 612), (4, 512, 512), jnp.float32))
        return (x, itok_BxS_13_99985, ctx_2048)
    x, itok_BxS_13_99985, ctx_2048 = _rec_inputs()

    def _L0_attn_setup():
        import jax, jax.numpy as jnp
        import numpy as np
        EMBED_DIM = 256
        NUM_HEADS = 16
        HEAD_SIZE = EMBED_DIM // NUM_HEADS
        MAX_EMBED_DIM = 512
        MAX_HEAD_SIZE = 128
        B, T = (4, 512)
        key = jax.random.key(seed)
        kx, kq, kk, kv = jax.random.split(key, 4)
        x = jax.random.normal(kx, (B, T, MAX_EMBED_DIM), dtype=jnp.float32)
        Wq = jax.random.normal(kq, (NUM_HEADS, MAX_HEAD_SIZE, MAX_EMBED_DIM), dtype=jnp.float32) * 0.02
        Wk = jax.random.normal(kk, (NUM_HEADS, MAX_HEAD_SIZE, MAX_EMBED_DIM), dtype=jnp.float32) * 0.02
        Wv = jax.random.normal(kv, (NUM_HEADS, MAX_HEAD_SIZE, MAX_EMBED_DIM), dtype=jnp.float32) * 0.02
        return {'x': x, 'Wq': Wq, 'Wk': Wk, 'Wv': Wv}
    _L0_attn_all = _L0_attn_setup()
    _L0_attn_in = {k: v for k, v in _L0_attn_all.items() if k in ('Wq', 'Wk', 'Wv')}
    del _L0_attn_all

    def _L0_xattn_setup():
        import jax, jax.numpy as jnp
        import numpy as np
        B, S, D = (4, 1024, 512)
        E = 4
        F = 2048 // E
        VOCAB = 25000
        key = jax.random.key(seed)
        k1, k2, k3, k4, k5 = jax.random.split(key, 5)
        hidden_states = jax.random.normal(k1, (B, S, D), dtype=jnp.float32)
        token_ids = jax.random.randint(k2, (B, S), 0, VOCAB, dtype=jnp.int64)
        Wg = jax.random.normal(k3, (E, F, D), dtype=jnp.float32) * 0.02
        Wu = jax.random.normal(k4, (E, F, D), dtype=jnp.float32) * 0.02
        Wd = jax.random.normal(k5, (E, D, F), dtype=jnp.float32) * 0.02
        return {'hidden_states': hidden_states, 'token_ids': token_ids, 'Wg': Wg, 'Wu': Wu, 'Wd': Wd}
    _L0_xattn_all = _L0_xattn_setup()
    _L0_xattn_in = {k: v for k, v in _L0_xattn_all.items() if k in ()}
    del _L0_xattn_all

    def _L0_ffn_setup():
        import jax, jax.numpy as jnp
        import numpy as np
        NUM_EXPERTS = 32
        TOP_K = 4
        HIDDEN = 512
        INTER = 192
        key = jax.random.key(seed)
        k1, k2, k3, k4 = jax.random.split(key, 4)
        hidden_states = jax.random.normal(k1, (4, 128, HIDDEN), dtype=jnp.float32)
        gate = jax.random.normal(k2, (HIDDEN, NUM_EXPERTS), dtype=jnp.float32) * 0.02
        gate_up_proj = jax.random.normal(k3, (NUM_EXPERTS, HIDDEN, 2 * INTER), dtype=jnp.float32) * 0.02
        down_proj = jax.random.normal(k4, (NUM_EXPERTS, INTER, HIDDEN), dtype=jnp.float32) * 0.02
        return {'hidden_states': hidden_states, 'gate': gate, 'gate_up_proj': gate_up_proj, 'down_proj': down_proj}
    _L0_ffn_all = _L0_ffn_setup()
    _L0_ffn_in = {k: v for k, v in _L0_ffn_all.items() if k in ('gate', 'gate_up_proj', 'down_proj')}
    del _L0_ffn_all
    return {'x': x, 'itok_BxS_13_99985': itok_BxS_13_99985, 'ctx_2048': ctx_2048, 'L0_attn_Wq': _L0_attn_in['Wq'], 'L0_attn_Wk': _L0_attn_in['Wk'], 'L0_attn_Wv': _L0_attn_in['Wv'], 'L0_ffn_gate': _L0_ffn_in['gate'], 'L0_ffn_gate_up_proj': _L0_ffn_in['gate_up_proj'], 'L0_ffn_down_proj': _L0_ffn_in['down_proj']}

def reference(x, itok_BxS_13_99985, ctx_2048, L0_attn_Wq, L0_attn_Wk, L0_attn_Wv, L0_ffn_gate, L0_ffn_gate_up_proj, L0_ffn_down_proj):
    import jax
    import jax.numpy as jnp

    def _L0_attn_ref(x, Wq, Wk, Wv):
        import jax, jax.numpy as jnp
        import numpy as np
        EMBED_DIM = 256
        NUM_HEADS = 16
        HEAD_SIZE = EMBED_DIM // NUM_HEADS
        MAX_EMBED_DIM = 512
        MAX_HEAD_SIZE = 128
        B, T = (4, 512)
        Bx, Tx, _ = x.shape
        xs = x[:, :, :EMBED_DIM]
        wq = Wq[:, :HEAD_SIZE, :EMBED_DIM]
        wk = Wk[:, :HEAD_SIZE, :EMBED_DIM]
        wv = Wv[:, :HEAD_SIZE, :EMBED_DIM]
        q = jnp.einsum('bte,hde->bhtd', xs, wq)
        k = jnp.einsum('bte,hde->bhtd', xs, wk)
        v = jnp.einsum('bte,hde->bhtd', xs, wv)
        scale = jnp.asarray(HEAD_SIZE, x.dtype) ** (-0.5)
        wei = jnp.einsum('bhtd,bhsd->bhts', q, k) * scale
        causal = jnp.tril(jnp.ones((Tx, Tx), dtype=bool))
        wei = jnp.where(causal, wei, jnp.asarray(-jnp.inf, wei.dtype))
        wei = jax.nn.softmax(wei, axis=-1)
        out = jnp.einsum('bhts,bhsd->bhtd', wei, v)
        out = out.transpose(0, 2, 1, 3).reshape(Bx, Tx, NUM_HEADS * HEAD_SIZE)
        pad = MAX_EMBED_DIM - NUM_HEADS * HEAD_SIZE
        return jnp.pad(out, ((0, 0), (0, 0), (0, pad)))

    def _L0_xattn_ref(hidden_states, token_ids, Wg, Wu, Wd):
        import jax, jax.numpy as jnp
        import numpy as np
        B, S, D = (4, 1024, 512)
        E = 4
        F = 2048 // E
        VOCAB = 25000
        tokens_per_expert = VOCAB // E
        tid = jnp.clip(token_ids, 0, VOCAB - 1)
        expert_ids = jnp.minimum(tid // tokens_per_expert, E - 1)
        out = jnp.zeros_like(hidden_states)
        for e in range(E):
            g = jax.nn.silu(jnp.einsum('bsd,fd->bsf', hidden_states, Wg[e]))
            u = jnp.einsum('bsd,fd->bsf', hidden_states, Wu[e])
            y = jnp.einsum('bsf,df->bsd', g * u, Wd[e])
            out = jnp.where((expert_ids == e)[..., None], y, out)
        return out

    def _L0_ffn_ref(hidden_states, gate, gate_up_proj, down_proj):
        import jax, jax.numpy as jnp
        import numpy as np
        NUM_EXPERTS = 32
        TOP_K = 4
        HIDDEN = 512
        INTER = 192
        batch_size = hidden_states.shape[0]
        x = hidden_states.reshape(-1, HIDDEN)
        num_tokens = x.shape[0]
        router_logits = jnp.einsum('TD,DE->TE', x, gate)
        routing_weights = jax.nn.softmax(router_logits.astype(jnp.float32), axis=-1)
        top_k_weights, top_k_indices = jax.lax.top_k(routing_weights, TOP_K)
        top_k_weights = top_k_weights / top_k_weights.sum(axis=-1, keepdims=True)
        top_k_weights = top_k_weights.astype(x.dtype)
        router_weights = jnp.zeros((num_tokens, NUM_EXPERTS), dtype=x.dtype)
        token_indices = jnp.broadcast_to(jnp.arange(num_tokens)[:, None], top_k_indices.shape)
        router_weights = router_weights.at[token_indices, top_k_indices].set(top_k_weights)
        gate_up = jnp.einsum('TD,EDF->TEF', x, gate_up_proj)
        g, u = jnp.split(gate_up, 2, axis=-1)
        gated = u * jax.nn.silu(g)
        next_states = jnp.einsum('TEF,EFD->TED', gated, down_proj)
        next_states = (next_states * router_weights[..., None]).sum(axis=1)
        return next_states.reshape(batch_size, -1, HIDDEN)
    x = _layernorm(x + _L0_attn_ref(x, L0_attn_Wq, L0_attn_Wk, L0_attn_Wv), axis=-1)
    x = _layernorm(x + _L0_xattn_ref(x, itok_BxS_13_99985, ctx_2048, ctx_2048, ctx_2048), axis=-1)
    x = _layernorm(x + _L0_ffn_ref(x, L0_ffn_gate, L0_ffn_gate_up_proj, L0_ffn_down_proj), axis=-1)
    return x

_drawn_inputs = setup_inputs


def setup_inputs(seed=0):
    import zlib

    import numpy as np

    out = dict(_drawn_inputs(seed))
    spreads = {}
    factors = {'L0_attn_Wq': 8.0,
     'L0_attn_Wk': 8.0,
     'L0_ffn_gate': 3.949,
     'L0_ffn_gate_up_proj': 3.704,
     'L0_ffn_down_proj': 3.714}
    for name, (base, spread) in spreads.items():
        noise = np.random.default_rng([zlib.crc32(name.encode()), seed]).standard_normal(out[name].shape)
        drawn = base * np.exp(spread * noise) if base else spread * noise
        out[name] = jnp.asarray(drawn.astype(out[name].dtype))
    for name, factor in factors.items():
        out[name] = (out[name] * factor).astype(out[name].dtype)
    return out
```

```python
from contextlib import ExitStack

import concourse.bass as bass
from concourse import mybir

P = 128
ALU = mybir.AluOpType
ACT = mybir.ActivationFunctionType
AX = mybir.AxisListType
F32 = mybir.dt.float32
F32R = mybir.dt.float32r
BF16 = mybir.dt.bfloat16
I32 = mybir.dt.int32
U32 = mybir.dt.uint32

B, T, D = 4, 512, 512
N_TOK = B * T
TOK_TILES = N_TOK // P
DC = D // P
EPS = 1e-5

VOCAB, HASHES = 25000, 4
HASH_SPAN = VOCAB // HASHES
SORT_TILES = TOK_TILES + HASHES - 1
SLOTS = SORT_TILES * P

EXPERTS, TOP_K, INTER = 32, 4, 192
IC = 2
IW = INTER // IC
PAIR_TILES = N_TOK * TOP_K // P + EXPERTS - 1
PLAN = PAIR_TILES + 1
WEIGHT_SLOTS = 4


class Tensors:
    pass


def sequence(eng, sem):
    done = [0]

    def link(instruction):
        done[0] += 1
        instruction.then_inc(sem, 1)
        eng.wait_ge(sem, done[0])

    return link


def slots_of_groups(nc, link, w, groups, tiles, ones_sum, ranks):
    v = nc.vector
    flat = "p g t -> p (g t)"
    link(v.memset(w.keep[:], 1.0))
    link(v.memset(w.keep[:, :, 0:1], 0.0))
    for part, ps in ones_sum:
        link(v.tensor_copy(w.sums[:, part], ps))
    link(v.tensor_tensor_scan(w.upto[:].rearrange(flat), w.keep[:].rearrange(flat),
                              w.sums[:].rearrange(flat), 0.0, ALU.mult, ALU.add))
    link(v.tensor_scalar(w.n_tiles_i[:], w.upto[:, :, tiles - 1], P / 2 - 0.5, 1.0 / P, ALU.add, ALU.mult))
    link(v.tensor_copy(w.n_tiles[:], w.n_tiles_i[:]))
    link(v.memset(w.ones_g[:], 1.0))
    link(v.tensor_tensor_scan(w.tiles_end[:], w.ones_g[:], w.n_tiles[:], 0.0, ALU.mult, ALU.add))
    link(v.tensor_tensor(w.first[:], w.tiles_end[:], w.n_tiles[:], ALU.subtract))
    link(v.tensor_scalar(w.first[:], w.first[:], float(P), None, ALU.mult))
    link(v.tensor_tensor(w.slot[:], w.upto[:], w.sums[:], ALU.subtract))
    for part, ps in ranks:
        link(v.tensor_tensor(w.slot[:, part], ps, w.slot[:, part], ALU.add))
    link(v.tensor_tensor(w.slot[:], w.slot[:], w.first[:].unsqueeze(2).to_broadcast([P, groups, tiles]), ALU.add))


def sort_buffers(sb, name, groups, tiles):
    w = Tensors()
    w.member, w.keep, w.sums, w.upto, w.slot = (
        sb(f"{name}_{n}", [P, groups, tiles], F32) for n in ("member", "keep", "sums", "upto", "slot"))
    w.n_tiles, w.ones_g, w.tiles_end, w.first = (
        sb(f"{name}_{n}", [P, groups], F32) for n in ("n_tiles", "ones_g", "tiles_end", "first"))
    w.n_tiles_i = sb(f"{name}_n_tiles_i", [P, groups], I32)
    return w


def split_slot(nc, link, tile_of, place_of, tmp_i, slots):
    v = nc.vector
    link(v.tensor_scalar(tmp_i, slots, -(P / 2 - 0.5), 1.0 / P, ALU.add, ALU.mult))
    link(v.tensor_copy(tile_of, tmp_i))
    link(v.scalar_tensor_tensor(out=place_of, in0=tile_of, scalar=-float(P), in1=slots,
                                op0=ALU.mult, op1=ALU.add))


def stage_sort(nc, g):
    with ExitStack() as ctx:
        def sb(name, shape, dt=F32):
            return ctx.enter_context(nc.sbuf_tensor(f"sort_{name}", shape, dt))

        def sem(name):
            return ctx.enter_context(nc.semaphore(f"sort_{name}"))

        ids_i = sb("ids_i", [TOK_TILES, P], I32)
        ids_f = sb("ids_f", [TOK_TILES, P])
        ids = sb("ids", [P, TOK_TILES])
        at_least = sb("at_least", [P, HASHES + 1, TOK_TILES])
        w = sort_buffers(sb, "hash", HASHES, TOK_TILES)
        picked = sb("picked", [P, HASHES, TOK_TILES])
        tok_i = sb("tok_i", [P, TOK_TILES], I32)
        tile_of = sb("tile_of", [P, TOK_TILES])
        place_of = sb("place_of", [P, TOK_TILES])
        slot_of = sb("slot_of", [P, TOK_TILES])
        at_place = sb("at_place", [P, TOK_TILES, P])
        at_tile = sb("at_tile", [P, TOK_TILES, SORT_TILES])
        token_up = sb("token_up", [P, TOK_TILES])
        token_no = sb("token_no", [P, TOK_TILES])
        count_p = sb("count_p", [P, P])
        count_t = sb("count_t", [P, SORT_TILES])
        ones = sb("ones", [P, P])
        below = sb("below", [P, P])
        table = sb("table", [P, SORT_TILES])
        ctx_rows = sb("ctx_rows", [P, HASHES * DC, D])
        plan = sb("plan", [1, SORT_TILES, HASHES])
        plan_f = sb("plan_f", [1, SORT_TILES])
        plan_no = sb("plan_no", [1, SORT_TILES, HASHES])
        ps = ctx.enter_context(nc.psum_tensor("sort_ps", [P, 4, 512], F32))
        ps_ct = ctx.enter_context(nc.psum_tensor("ct_ps", [P, 4, 512], F32))

        ids_in, ctx_in, gate_in = sem("ids_in"), sem("ctx_in"), sem("gate_in")
        cleared, constants = sem("cleared"), sem("constants")
        ids_float, ids_turned = sem("ids_float"), sem("ids_turned")
        members, ranked, v_chain, v_chain2 = sem("members"), sem("ranked"), sem("v_chain"), sem("v_chain2")
        placed, tabled = sem("placed"), sem("tabled")
        ct_turned, ct_copied = sem("ct_turned"), sem("ct_copied")

        with nc.Block() as block:
            @block.sync
            def _(sp):
                sp.dma_start(ids_i[:], g.tokens.rearrange("b (j p) -> (b j) p", p=P)).then_inc(ids_in, 16)
                sp.dma_start(ctx_rows[:], g.context.rearrange("e (c p) d -> p (e c) d", p=P)).then_inc(ctx_in, 16)
                with nc.allow_non_contiguous_dma(reason="the gate's rows are 32 elements"):
                    sp.dma_start(g.gate[:], g.gate_dram.rearrange("(c p) e -> p c e", p=P)).then_inc(gate_in, 16)
                sp.wait_ge(gate_in, 16)

            @block.gpsimd
            def _(pool):
                nc.gpsimd.memset(g.ident[:], 0.0).then_inc(cleared, 1)
                nc.gpsimd.memset(ones[:], 1.0).then_inc(cleared, 1)
                nc.gpsimd.iota(count_p[:], pattern=[[1, P]], base=0, channel_multiplier=0,
                               allow_small_or_imprecise_dtypes=True).then_inc(constants, 1)
                nc.gpsimd.iota(count_t[:], pattern=[[1, SORT_TILES]], base=0, channel_multiplier=0,
                               allow_small_or_imprecise_dtypes=True).then_inc(constants, 1)
                nc.gpsimd.iota(token_up[:], pattern=[[P, TOK_TILES]], base=1, channel_multiplier=1,
                               allow_small_or_imprecise_dtypes=True).then_inc(constants, 1)
                nc.gpsimd.iota(plan_no[:], pattern=[[1, SORT_TILES], [0, HASHES]], base=0, channel_multiplier=0,
                               allow_small_or_imprecise_dtypes=True).then_inc(constants, 1)
                pool.wait_ge(cleared, 2)
                nc.gpsimd.affine_select(out=g.ident[:], in_=g.ident[:], compare_op=ALU.not_equal, fill=1.0,
                                        base=0, pattern=[[-1, P]], channel_multiplier=1).then_inc(constants, 1)
                nc.gpsimd.affine_select(out=below[:], in_=ones[:], compare_op=ALU.is_gt, fill=0.0,
                                        base=0, pattern=[[1, P]], channel_multiplier=-1).then_inc(constants, 1)

            @block.vector
            def _(dve):
                v = nc.vector
                link = sequence(dve, v_chain)
                dve.wait_ge(ids_in, 16)
                link(v.tensor_scalar(ids_f[:], ids_i[:], float(VOCAB - 1), 0.0, ALU.min, ALU.max))
                v.tensor_copy(ids_f[:], ids_f[:]).then_inc(ids_float, 1)
                dve.wait_ge(ids_turned, 1)
                v.tensor_copy(ids[:], ps[:, 0, 0:TOK_TILES]).then_inc(v_chain, 1)
                dve.wait_ge(v_chain, 2)
                link = sequence(dve, v_chain2)
                link(v.memset(at_least[:, 0, :], 1.0))
                link(v.memset(at_least[:, HASHES, :], 0.0))
                for e in range(1, HASHES):
                    link(v.tensor_scalar(at_least[:, e, :], ids[:], float(e * HASH_SPAN), None, ALU.is_ge))
                v.tensor_tensor(w.member[:], at_least[:, 0:HASHES, :], at_least[:, 1:HASHES + 1, :],
                                ALU.subtract).then_inc(members, 1)
                dve.wait_ge(ranked, 1)
                shape = ps[:, 1, 0:HASHES * TOK_TILES].rearrange("p (g t) -> p g t", g=HASHES)
                shape2 = ps[:, 2, 0:HASHES * TOK_TILES].rearrange("p (g t) -> p g t", g=HASHES)
                slots_of_groups(nc, link, w, HASHES, TOK_TILES, [(slice(0, HASHES), shape2)], [(slice(0, HASHES), shape)])
                link(v.tensor_tensor(picked[:], w.slot[:], w.member[:], ALU.mult))
                link(v.tensor_reduce(slot_of[:], picked[:].rearrange("p g t -> p t g"), AX.X, ALU.add))
                link(v.tensor_copy(g.slot_of_token[:], slot_of[:]))
                split_slot(nc, link, tile_of[:], place_of[:], tok_i[:], slot_of[:])
                dve.wait_ge(constants, 6)
                link(v.tensor_tensor(at_place[:], count_p[:].unsqueeze(1).to_broadcast([P, TOK_TILES, P]),
                                     place_of[:].unsqueeze(2).to_broadcast([P, TOK_TILES, P]), ALU.is_equal))
                link(v.tensor_tensor(at_tile[:], count_t[:].unsqueeze(1).to_broadcast([P, TOK_TILES, SORT_TILES]),
                                     tile_of[:].unsqueeze(2).to_broadcast([P, TOK_TILES, SORT_TILES]), ALU.is_equal))
                v.tensor_tensor(at_tile[:], at_tile[:], token_up[:].unsqueeze(2).to_broadcast([P, TOK_TILES, SORT_TILES]),
                                ALU.mult).then_inc(placed, 1)
                dve.wait_ge(tabled, 1)
                link(v.tensor_copy(table[:], ps[:, 3, 0:SORT_TILES]))
                link(v.tensor_scalar(g.slot_full[:], table[:], 0.5, None, ALU.is_gt))
                link(v.tensor_scalar(g.token_of_slot[:], table[:], -1.0, 0.0, ALU.add, ALU.max))
                link(v.tensor_tensor(plan[:], w.tiles_end[0:1, :].unsqueeze(1).to_broadcast([1, SORT_TILES, HASHES]),
                                     plan_no[:], ALU.is_le))
                link(v.tensor_reduce(plan_f[:], plan[:], AX.X, ALU.add))
                link(v.tensor_scalar(g.hash_of_tile[:], plan_f[:], float(HASHES - 1), None, ALU.min))

            @block.scalar
            def _(act):
                for n in range(HASHES * DC):
                    act.wait_ge(ct_turned, n + 1)
                    e, c = n // DC, n % DC
                    nc.scalar.copy(g.ctx_t[:, e, c, :], ps_ct[:, n % 4, :]).then_inc(ct_copied, 1)

            @block.tensor
            def _(pe):
                pe.wait_ge(constants, 6)
                pe.wait_ge(ids_float, 1)
                pe.transpose(ps[:, 0, 0:TOK_TILES], ids_f[:], g.ident[0:TOK_TILES, 0:TOK_TILES]).then_inc(ids_turned, 1)
                pe.wait_ge(ctx_in, 16)

                def turn(n):
                    e, c = n // DC, n % DC
                    if n >= 4:
                        pe.wait_ge(ct_copied, n - 3)
                    for r in range(DC):
                        last = pe.transpose(ps_ct[:, n % 4, r * P:(r + 1) * P],
                                            ctx_rows[:, e * DC + r, c * P:(c + 1) * P], g.ident[:])
                    last.then_inc(ct_turned, 1)

                for n in range(2):
                    turn(n)
                pe.wait_ge(members, 1)
                flat = w.member[:].rearrange("p g t -> p (g t)")
                pe.matmul(ps[:, 1, 0:HASHES * TOK_TILES], below[:], flat, start=True, stop=True)
                pe.matmul(ps[:, 2, 0:HASHES * TOK_TILES], ones[:], flat, start=True, stop=True).then_inc(ranked, 1)
                for n in range(2, HASHES * DC):
                    turn(n)
                pe.wait_ge(placed, 1)
                for t in range(TOK_TILES):
                    last = pe.matmul(ps[:, 3, 0:SORT_TILES], at_place[:, t, :], at_tile[:, t, :],
                                     start=(t == 0), stop=(t == TOK_TILES - 1))
                last.then_inc(tabled, 1)


class Step:

    def __init__(self, tile, buf, lap, unroll):
        self.tile, self.buf, self.lap, self.unroll = tile, buf, lap, unroll

    def at(self, k):
        n = self.buf + k
        return Step(self.tile + k, n % self.unroll, self.lap + n // self.unroll, self.unroll)

    def within(self, count):
        return not isinstance(self.tile, int) or 0 <= self.tile < count

    def after(self, n):
        return not isinstance(self.tile, int) or self.tile >= n


def run_steps(eng, count, unroll, head, tail, body):
    looped = (count - head - tail) // unroll
    for t in range(head):
        body(Step(t, t % unroll, t // unroll, unroll))
    with eng.Fori(0, looped) as i:
        for u in range(unroll):
            body(Step(i * unroll + (head + u), u, i + head // unroll, unroll))
    for t in range(head + looped * unroll, count):
        body(Step(t, t % unroll, t // unroll, unroll))


def hold(eng, g, sem, value):
    if not isinstance(value, int):
        value = eng.to_reg(value)
        eng.wait_ge(g.constant, 1)
    eng.wait_ge(sem, value)


def stage_hash_ffn(nc, g):
    with ExitStack() as ctx:
        def sb(name, shape, dt=F32):
            return ctx.enter_context(nc.sbuf_tensor(f"hash_ffn_{name}", shape, dt))

        def sem(name):
            return ctx.enter_context(nc.semaphore(f"hash_ffn_{name}"))

        def bank(name, n=1):
            return ctx.enter_context(nc.psum_tensor(f"hash_ffn_{name}", [P, n, 512], F32))

        N, U = SORT_TILES, 4
        index = sb("index", [P, U], I32)
        rows = sb("rows", [P, U, D])
        x_t = sb("x_t", [P, 2, DC, P])
        silu = sb("silu", [P, 2, D])
        h = sb("h", [P, 2, D])
        h_t = sb("h_t", [P, DC, P])
        total = sb("total", [P, 2, D])
        stats = sb("stats", [P, 6])
        mean_var = sb("mean_var", [P, 2, 2])
        var_eps = sb("var_eps", [P, 2])
        rstd = sb("rstd", [P, 2])
        x2 = sb("x2", [P, U, D])
        x2_t = sb("x2_t", [P, DC, P])
        logits = sb("logits", [P, EXPERTS])
        largest = sb("largest", [P, 8])
        largest_at = sb("largest_at", [P, 8], U32)

        ps_x, ps_h, ps_x2, ps_u, ps_y, ps_l = bank("ps_x"), bank("ps_h"), bank("ps_x2"), bank("ps_u", 2), bank("ps_y", 2), bank("ps_l")
        rows_in = [sem(f"rows_in{u}") for u in range(U)]
        stored = [sem(f"stored{u}") for u in range(U)]
        index_set, x_turned, xt_copied = sem("index_set"), sem("x_turned"), sem("xt_copied")
        u_done, silu_done, h_done, h_turned, ht_copied = sem("u_done"), sem("silu_done"), sem("h_done"), sem("h_turned"), sem("ht_copied")
        y_done, added, stats_done, averaged = sem("y_done"), sem("added"), sem("stats_done"), sem("averaged")
        eps_added, rstd_done, x2_done = sem("eps_added"), sem("rstd_done"), sem("x2_done")
        x2_turned, x2t_copied, logits_done = sem("x2_turned"), sem("x2t_copied"), sem("logits_done")
        logits_copied, top_found, top_indexed, top_kept = sem("logits_copied"), sem("top_found"), sem("top_indexed"), sem("top_kept")

        def steps(eng, body):
            run_steps(eng, N, U, U, 3, body)

        with nc.Block() as block:
            @block.sync
            def _(sp):
                def store(s):
                    hold(sp, g, x2_done, s.tile + 1)
                    for dram in (g.x2_rows, g.sum_rows):
                        sp.dma_start(dram[bass.ds(s.tile * P, P), :], x2[:, s.buf, :]).then_inc(stored[s.buf], 16)

                steps(sp, store)
                for u in range(U):
                    sp.wait_ge(stored[u], 32 * len(range(u, N, U)))

            @block.gpsimd
            def _(pool):
                def rstd_of(s):
                    b = s.buf % 2
                    hold(pool, g, averaged, s.tile + 1)
                    nc.gpsimd.tensor_scalar(var_eps[:, b:b + 1], mean_var[:, b, 1:2], EPS, None, ALU.add).then_inc(eps_added, 1)
                    hold(pool, g, eps_added, s.tile + 1)
                    if s.after(2):
                        hold(pool, g, x2_done, s.tile - 1)
                    nc.gpsimd.tensor_tensor(rstd[:, b:b + 1], var_eps[:, b:b + 1], g.minus_half[:], ALU.pow).then_inc(rstd_done, 1)

                def gather(s):
                    if s.after(U):
                        hold(pool, g, added, s.tile - (U - 1))
                    nc.gpsimd.tensor_copy(index[:, s.buf:s.buf + 1], g.token_of_slot[:, bass.ds(s.tile, 1)]).then_inc(index_set, 1)
                    hold(pool, g, index_set, s.tile + 1)
                    nc.gpsimd.indirect_dma_start(
                        out=rows[:, s.buf, :], out_offset=None, in_=g.x1_rows,
                        in_offset=bass.IndirectOffsetOnAxis(ap=index[:, s.buf:s.buf + 1], axis=0),
                    ).then_inc(rows_in[s.buf], 16)

                pool.wait_ge(g.constant, 1)
                for t in range(3):
                    gather(Step(t, t % U, t // U, U))

                def body(s):
                    if s.at(3).within(N):
                        gather(s.at(3))
                    rstd_of(s)

                steps(pool, body)

            @block.scalar
            def _(act):
                def xt(s):
                    if s.after(2):
                        hold(act, g, u_done, s.tile - 1)
                    hold(act, g, x_turned, s.tile + 1)
                    nc.scalar.copy(x_t[:, s.buf % 2].rearrange("p c t -> p (c t)"), ps_x[:, 0, :]).then_inc(xt_copied, 1)

                def silu_of(s):
                    if s.after(2):
                        hold(act, g, h_done, s.tile - 1)
                    hold(act, g, u_done, s.tile + 1)
                    nc.scalar.activation(silu[:, s.buf % 2, :], ps_u[:, s.buf % 2, :], ACT.Silu).then_inc(silu_done, 1)

                def ht(s):
                    if s.after(1):
                        hold(act, g, y_done, s.tile)
                    hold(act, g, h_turned, s.tile + 1)
                    nc.scalar.copy(h_t[:].rearrange("p c t -> p (c t)"), ps_h[:, 0, :]).then_inc(ht_copied, 1)

                def x2t(s):
                    if s.after(1):
                        hold(act, g, logits_done, s.tile)
                    hold(act, g, x2_turned, s.tile + 1)
                    nc.scalar.copy(x2_t[:].rearrange("p c t -> p (c t)"), ps_x2[:, 0, :]).then_inc(x2t_copied, 1)

                first = Step(0, 0, 0, U)
                xt(first)
                silu_of(first)
                xt(first.at(1))

                def body(s):
                    ht(s)
                    if s.at(1).within(N):
                        silu_of(s.at(1))
                    if s.at(2).within(N):
                        xt(s.at(2))
                    if s.after(1):
                        x2t(s.at(-1))

                steps(act, body)
                x2t(Step(N - 1, (N - 1) % U, (N - 1) // U, U))

            @block.vector
            def _(dve):
                v = nc.vector

                def gate(s):
                    if s.after(2):
                        hold(dve, g, h_turned, s.tile - 1)
                    hold(dve, g, silu_done, s.tile + 1)
                    v.tensor_tensor(h[:, s.buf % 2, :], ps_u[:, s.buf % 2, :], silu[:, s.buf % 2, :], ALU.mult).then_inc(h_done, 1)

                def norm_in(s):
                    b = s.buf % 2
                    hold(dve, g, y_done, s.tile + 1)
                    v.tensor_tensor(total[:, b, :], ps_y[:, b, :], rows[:, s.buf, :], ALU.add).then_inc(added, 1)
                    hold(dve, g, added, s.tile + 1)
                    v.bn_stats(stats[:], total[:, b, :]).then_inc(stats_done, 1)
                    hold(dve, g, stats_done, s.tile + 1)
                    v.bn_aggr(mean_var[:, b, :], stats[:]).then_inc(averaged, 1)

                def norm_out(s):
                    b = s.buf % 2
                    if s.after(U):
                        hold(dve, g, stored[s.buf], s.lap * 32)
                        hold(dve, g, x2_turned, s.tile - (U - 1))
                    hold(dve, g, rstd_done, s.tile + 1)
                    v.tensor_scalar(x2[:, s.buf, :], total[:, b, :], mean_var[:, b, 0:1], rstd[:, b:b + 1],
                                    ALU.subtract, ALU.mult).then_inc(x2_done, 1)

                def top(s):
                    hold(dve, g, logits_done, s.tile + 1)
                    if s.after(1):
                        hold(dve, g, top_kept, s.tile)
                    v.tensor_copy(logits[:], ps_l[:, 0, 0:EXPERTS]).then_inc(logits_copied, 1)
                    hold(dve, g, logits_copied, s.tile + 1)
                    v.max(largest[:], logits[:]).then_inc(top_found, 1)
                    hold(dve, g, top_found, s.tile + 1)
                    v.max_index(largest_at[:], largest[:], logits[:]).then_inc(top_indexed, 1)
                    v.tensor_copy(g.top_logits[:, bass.ds(s.tile, 1), :].rearrange("p a k -> p (a k)"), largest[:])
                    hold(dve, g, top_indexed, s.tile + 1)
                    v.tensor_copy(g.top_experts[:, bass.ds(s.tile, 1), :].rearrange("p a k -> p (a k)"), largest_at[:]).then_inc(top_kept, 1)

                first = Step(0, 0, 0, U)
                gate(first)

                def body(s):
                    if s.at(1).within(N):
                        gate(s.at(1))
                    norm_in(s)
                    if s.after(1):
                        top(s.at(-1))
                    norm_out(s)

                steps(dve, body)
                top(Step(N - 1, (N - 1) % U, (N - 1) // U, U))

            @block.tensor
            def _(pe):
                def turn(source, target, done):
                    for c in range(DC):
                        last = pe.transpose(target[:, 0, c * P:(c + 1) * P], source[:, c * P:(c + 1) * P], g.ident[:])
                    last.then_inc(done, 1)

                def turn_x(s):
                    hold(pe, g, rows_in[s.buf], (s.lap + 1) * 16)
                    if s.after(1):
                        hold(pe, g, xt_copied, s.tile)
                    turn(rows[:, s.buf, :], ps_x, x_turned)

                def times_context(s, source, bank_of, done):
                    expert = pe.value_load(g.hash_of_tile[0:1, bass.ds(s.tile, 1)], min_val=0, max_val=HASHES - 1)
                    for c in range(DC):
                        last = pe.matmul(bank_of[:, s.buf % 2, :], source[:, c, :],
                                         g.ctx_t[:, bass.ds(expert, 1), c, :].rearrange("p a n -> p (a n)"),
                                         start=(c == 0), stop=(c == DC - 1))
                    last.then_inc(done, 1)

                def mm_u(s):
                    if s.after(2):
                        hold(pe, g, h_done, s.tile - 1)
                    hold(pe, g, xt_copied, s.tile + 1)
                    times_context(s, x_t[:, s.buf % 2], ps_u, u_done)

                def turn_h(s):
                    hold(pe, g, h_done, s.tile + 1)
                    if s.after(1):
                        hold(pe, g, ht_copied, s.tile)
                    turn(h[:, s.buf % 2, :], ps_h, h_turned)

                def mm_y(s):
                    if s.after(2):
                        hold(pe, g, added, s.tile - 1)
                    hold(pe, g, ht_copied, s.tile + 1)
                    times_context(s, h_t[:], ps_y, y_done)

                def route(s):
                    hold(pe, g, x2_done, s.tile + 1)
                    if s.after(1):
                        hold(pe, g, x2t_copied, s.tile)
                    turn(x2[:, s.buf, :], ps_x2, x2_turned)
                    if s.after(1):
                        hold(pe, g, logits_copied, s.tile)
                    hold(pe, g, x2t_copied, s.tile + 1)
                    for c in range(DC):
                        last = pe.matmul(ps_l[:, 0, 0:EXPERTS], x2_t[:, c, :], g.gate[:, c, :], start=(c == 0), stop=(c == DC - 1))
                    last.then_inc(logits_done, 1)

                first = Step(0, 0, 0, U)
                turn_x(first)
                mm_u(first)
                turn_x(first.at(1))

                def body(s):
                    turn_h(s)
                    if s.at(1).within(N):
                        mm_u(s.at(1))
                    mm_y(s)
                    if s.at(2).within(N):
                        turn_x(s.at(2))
                    if s.after(1):
                        route(s.at(-1))

                steps(pe, body)
                route(Step(N - 1, (N - 1) % U, (N - 1) // U, U))


def stage_attention(nc, g):
    HD, HEADS, EMB = 16, 16, 256
    EC, QT = EMB // P, T // P
    HG = P // HD
    QUADS = HEADS // 4
    COPIES, ZERO_ROW, MAX_ROW = 4, 64, 65
    K_MAX, K_EXP = 65, 67
    VW = 32
    MASKED = -1e30
    SCALE = HD ** -0.5

    with ExitStack() as ctx:
        def sb(name, shape, dt=F32):
            return ctx.enter_context(nc.sbuf_tensor(f"attn_{name}", shape, dt))

        def sem(name):
            return ctx.enter_context(nc.semaphore(f"attn_{name}"))

        def bank(name, n=1):
            return ctx.enter_context(nc.psum_tensor(f"attn_{name}", [P, n, 512], F32))

        N, U = B * QUADS, QUADS
        w_rows = sb("w_rows", [P, 3, 2, EMB])
        w_t = sb("w_t", [P, EC, 3, 2 * P])
        x_in = sb("x_in", [P, QT, EMB])
        x_t = sb("x_t", [P, EC, T])
        hi = sb("hi", [P, 2, T], F32R)
        lo = sb("lo", [P, 2, T], F32R)
        qs = sb("qs", [P, 2, HG, T], F32R)
        ks = sb("ks", [P, 2, HG, T], F32R)
        v_one = sb("v_one", [P, 2, QT, HG, VW])
        maxima = sb("maxima", [P, 2, QT, 4])
        neg_max = sb("neg_max", [P, QT, 2, 4], F32R)
        neg_max_t = sb("neg_max_t", [2 * 4, T], F32R)
        exps = sb("exps", [P, 2, 4, T])
        o_t = sb("o_t", [P, T])
        sums_inv = sb("sums_inv", [P, QT, 4])
        o_norm = sb("o_norm", [P, QT, 4, HD])
        res = sb("res", [P, QT, D])
        stats = sb("stats", [P, QT, 6])
        mean_var = sb("mean_var", [P, QT, 2])
        var_eps = sb("var_eps", [P, QT])
        rstd = sb("rstd", [P, QT])
        x1 = sb("x1", [P, QT, D])
        one_f = sb("one_f", [P, 512])
        ident_b = sb("ident_b", [P, P], BF16)
        later_key = sb("later_key", [P, P], BF16)
        earlier_query = sb("earlier_query", [P, P], BF16)
        mask_f = sb("mask_f", [P, 2, P])

        ps_s, ps_t, ps_o, ps_m = bank("ps_s", 2), bank("ps_t", 4), bank("ps_o"), bank("ps_m")

        w_in, x_arrived, res_in = sem("w_in"), sem("x_arrived"), sem("res_in")
        split_out, cleared, masks_made, constants, rows_set = sem("split_out"), sem("cleared"), sem("masks_made"), sem("constants"), sem("rows_set")
        w_turned, w_copied, xt_turned, xt_copied = sem("w_turned"), sem("w_copied"), sem("xt_turned"), sem("xt_copied")
        projected, hi_done, lo_done, v_projected, v_copied = sem("projected"), sem("hi_done"), sem("lo_done"), sem("v_projected"), sem("v_copied")
        q_stacked, k_stacked = [sem(f"q_stacked{i}") for i in range(2)], [sem(f"k_stacked{i}") for i in range(2)]
        s_done, max_done, max_hi, max_lo = sem("s_done"), sem("max_done"), sem("max_hi"), sem("max_lo")
        max_turned, max_copied, max_stacked = sem("max_turned"), sem("max_copied"), sem("max_stacked")
        t_done, exp_done, pv_done, o_copied = sem("t_done"), sem("exp_done"), sem("pv_done"), sem("o_copied")
        o_turned, inv_done, o_normed, res_added = sem("o_turned"), sem("inv_done"), sem("o_normed"), sem("res_added")
        stats_done, averaged, eps_added, rstd_done, x1_done, stored = (
            sem("stats_done"), sem("averaged"), sem("eps_added"), sem("rstd_done"), sem("x1_done"), sem("stored"))

        def steps(eng, body):
            run_steps(eng, N, U, U, U, body)

        def group(s):
            return s.lap * 2 + s.buf // 2

        def leads_group(s):
            return s.buf % 2 == 0 and s.at(2).within(N)

        def turns_x(s):
            return s.buf == 1 and s.at(QUADS - 1).within(N)

        PER_S, PER_T = 4 * QT, 2 * QT
        Q, K, V = 0, 1, 2
        X = (0, 1)
        HEADS_TURNED, MAX_TURNED = 4, 7
        LAST_V = 1
        LEAD = [3, 3, 3, 3, 2, 2, 0, 0]

        with nc.Block() as block:
            @block.sync
            def _(sp):
                for n, w_dram in enumerate((g.wq, g.wk, g.wv)):
                    for half in range(2):
                        for h in range(HG):
                            sp.dma_start(w_rows[h * HD:(h + 1) * HD, n, half, :],
                                         w_dram[half * HG + h, 0:HD, 0:EMB]).then_inc(w_in, 16)

                def load_x(b):
                    if not (isinstance(b, int) and b == 0):
                        hold(sp, g, xt_turned, b * EC)
                    sp.dma_start(x_in[:], g.x_dram[bass.ds(b, 1), :, 0:EMB].rearrange("a (c p) e -> p (a c) e", p=P)).then_inc(x_arrived, 16)

                def load_res(b):
                    if not (isinstance(b, int) and b == 0):
                        hold(sp, g, x1_done, b * QT)
                    sp.dma_start(res[:], g.x_dram[bass.ds(b, 1), :, :].rearrange("a (c p) e -> p (a c) e", p=P)).then_inc(res_in, 16)

                def stack(n, half):
                    if not (isinstance(n, int) and n < 2):
                        hold(sp, g, t_done, (n - 1) * 2 * PER_T)
                    else:
                        sp.wait_ge(rows_set, 2)
                    hold(sp, g, hi_done, n * 2 + 2)
                    hold(sp, g, lo_done, n * 2 + 2)
                    for p, part in enumerate((hi, lo)):
                        sp.dma_start(g.split_rows[half, p].rearrange("w r t -> r w t"), part[:].bitcast(F32)).then_inc(split_out, 16)
                    hold(sp, g, split_out, n * 32 + 32)
                    for which, stacked, done in ((0, qs, q_stacked), (1, ks, k_stacked)):
                        for r in range(COPIES):
                            p = (r // 2, r % 2)[which]
                            sp.dma_start(stacked[r * HD:(r + 1) * HD, half, :, :].bitcast(F32),
                                         g.split_rows[half, p, which].rearrange("(h d) t -> d h t", d=HD)).then_inc(done[half], 16)

                def stack_max(s):
                    half = s.buf // 2
                    h = (s.buf % 2) * 4
                    if s.after(1):
                        hold(sp, g, max_stacked, s.tile * 32)
                    hold(sp, g, max_copied, s.tile + 1)
                    for part in range(2):
                        sp.dma_start(qs[MAX_ROW + part:MAX_ROW + part + 1, half, h:h + 4, :].bitcast(F32),
                                     neg_max_t[part * 4:part * 4 + 4, :].bitcast(F32)).then_inc(max_stacked, 16)

                def store(b):
                    hold(sp, g, x1_done, b * QT + QT)
                    sp.dma_start(g.x1_rows[bass.ds(b * T, T), :].rearrange("(c p) d -> p c d", p=P), x1[:]).then_inc(stored, 16)

                load_x(0)
                load_res(0)
                stack(0, 0)
                first = Step(0, 0, 0, U)
                stack_max(first)

                def body(s):
                    if s.buf == 0 and s.at(U).within(N):
                        load_x(s.lap + 1)
                    if leads_group(s):
                        stack(group(s) + 1, 1 - s.buf // 2)
                    if s.buf == 1 and s.after(U):
                        store(s.lap - 1)
                        load_res(s.lap)
                    if s.at(1).within(N):
                        stack_max(s.at(1))

                steps(sp, body)
                store(B - 1)
                sp.wait_ge(stored, 16 * B)

            @block.gpsimd
            def _(pool):
                m = nc.gpsimd
                m.memset(mask_f[:], 0.0).then_inc(cleared, 1)
                m.memset(one_f[:], 1.0).then_inc(cleared, 1)
                m.memset(v_one[:], 0.0).then_inc(cleared, 1)
                pool.wait_ge(cleared, 3)
                m.affine_select(out=mask_f[:, 0, :], in_=mask_f[:, 0, :], compare_op=ALU.is_ge, fill=MASKED, base=0,
                                pattern=[[-1, P]], channel_multiplier=1).then_inc(masks_made, 1)
                m.affine_select(out=mask_f[:, 1, :], in_=mask_f[:, 1, :], compare_op=ALU.is_ge, fill=MASKED, base=0,
                                pattern=[[1, P]], channel_multiplier=-1).then_inc(masks_made, 1)
                m.memset(v_one[:].rearrange("p a c h w -> p (a c h) w")[:, :, HD:HD + 1], 1.0).then_inc(cleared, 1)
                pool.wait_ge(masks_made, 2)
                m.tensor_copy(later_key[:], mask_f[:, 0, :]).then_inc(constants, 1)
                m.tensor_copy(earlier_query[:], mask_f[:, 1, :]).then_inc(constants, 1)
                m.tensor_copy(ident_b[:], g.ident[:]).then_inc(constants, 1)
                pool.wait_ge(cleared, 4)
                pool.sem_inc(constants, 1)

                def add_attention(s):
                    q = s.buf
                    hold(pool, g, o_normed, s.tile + 1)
                    if q == 0:
                        hold(pool, g, res_in, (s.lap + 1) * 16)
                    part = res[:, :, q * 4 * HD:(q + 1) * 4 * HD]
                    m.tensor_tensor(part, part, o_norm[:].rearrange("p c h d -> p c (h d)"), ALU.add).then_inc(res_added, 1)

                def rstd_of(b):
                    hold(pool, g, averaged, b * QT + QT)
                    if not (isinstance(b, int) and b == 0):
                        hold(pool, g, x1_done, b * QT)
                    m.tensor_scalar(var_eps[:], mean_var[:, :, 1], EPS, None, ALU.add).then_inc(eps_added, 1)
                    hold(pool, g, eps_added, b + 1)
                    m.tensor_tensor(rstd[:], var_eps[:], g.minus_half[:].to_broadcast([P, QT]), ALU.pow).then_inc(rstd_done, 1)

                def scale_rows(b):
                    if not (isinstance(b, int) and b == 0):
                        hold(pool, g, stored, b * 16)
                    hold(pool, g, rstd_done, b + 1)
                    for c in range(QT):
                        m.tensor_scalar(x1[:, c, :], res[:, c, :], mean_var[:, c, 0:1], rstd[:, c:c + 1],
                                        ALU.subtract, ALU.mult).then_inc(x1_done, 1)

                def body(s):
                    if s.after(1):
                        add_attention(s.at(-1))
                        if s.buf == 0:
                            rstd_of(s.lap - 1)
                            scale_rows(s.lap - 1)

                steps(pool, body)
                add_attention(Step(N - 1, U - 1, B - 1, U))
                rstd_of(B - 1)
                scale_rows(B - 1)

            @block.scalar
            def _(act):
                a = nc.scalar
                for n in range(3 * EC):
                    act.wait_ge(w_turned, n + 1)
                    a.copy(w_t[:, n % EC, n // EC, :], ps_m[:, 0, 0:2 * P]).then_inc(w_copied, 1)

                def project(n, half, which):
                    if which == V:
                        if not (isinstance(n, int) and n < 2):
                            hold(act, g, pv_done, (n - 1) * 2 * QT)
                        hold(act, g, v_projected, n + 1)
                        a.copy(v_one[:, half, :, :, 0:HD], ps_m[:, 0, :].rearrange("p (c h d) -> p c h d", c=QT, d=HD)).then_inc(v_copied, 1)
                        return
                    if not (isinstance(n, int) and n == 0):
                        hold(act, g, split_out, n * 32)
                    hold(act, g, projected, n * 2 + which + 1)
                    a.activation(hi[:, which, :], ps_m[:, 0, :], ACT.Copy, scale=SCALE if which == Q else 1.0).then_inc(hi_done, 1)

                def turn_x(b, c):
                    if not (isinstance(b, int) and b == 0):
                        hold(act, g, v_projected, b * 2)
                    hold(act, g, xt_turned, b * EC + c + 1)
                    a.copy(x_t[:, c, :], ps_m[:, 0, :]).then_inc(xt_copied, 1)

                def copy_max(s):
                    if s.after(1):
                        hold(act, g, max_stacked, s.tile * 32)
                    hold(act, g, max_turned, s.tile + 1)
                    a.copy(neg_max_t[:], ps_m[0:8, 0, :]).then_inc(max_copied, 1)

                def copy_heads(s):
                    if s.after(1):
                        hold(act, g, o_turned, s.tile)
                    hold(act, g, pv_done, s.tile * QT + QT)
                    a.copy(o_t[:], ps_o[:, 0, :]).then_inc(o_copied, 1)

                def exponentials(s, j):
                    i, pair = j // 2, j % 2
                    w = T - i * P
                    if not (isinstance(s.tile, int) and s.tile == 0 and i < 2):
                        hold(act, g, pv_done, s.tile * QT + i - 1)
                    hold(act, g, t_done, s.tile * PER_T + j + 1)
                    a.activation(exps[:, i % 2, 2 * pair:2 * pair + 2, 0:w], ps_t[:, 2 * pair:2 * pair + 2, 0:w],
                                 ACT.Exp).then_inc(exp_done, 1)

                for c in range(EC):
                    turn_x(0, c)
                for which in (Q, K, V):
                    project(0, 0, which)
                copy_max(Step(0, 0, 0, U))

                def body(s):
                    for j in range(PER_T):
                        if leads_group(s) and j in (Q, K, V):
                            project(group(s) + 1, 1 - s.buf // 2, j)
                        if turns_x(s) and j in X:
                            turn_x(s.lap + 1, X.index(j))
                        if j == LAST_V + 1 and s.after(1):
                            copy_heads(s.at(-1))
                        if j == MAX_TURNED and s.at(1).within(N):
                            copy_max(s.at(1))
                        exponentials(s, j)

                steps(act, body)
                copy_heads(Step(N - 1, U - 1, B - 1, U))

            @block.vector
            def _(dve):
                v = nc.vector
                dve.wait_ge(cleared, 4)
                v.tensor_scalar(qs[64:96].rearrange("p a h t -> p (a h t)"),
                                one_f[64:96, 0:1].to_broadcast([32, 2 * HG * T]), 0.0, None, ALU.mult).then_inc(rows_set, 1)
                v.tensor_scalar(ks[64:96].rearrange("p a h t -> p (a h t)"),
                                one_f[64:96, 0:1].to_broadcast([32, 2 * HG * T]), 1.0, None, ALU.mult).then_inc(rows_set, 1)

                def split(n, which):
                    hold(dve, g, hi_done, n * 2 + which + 1)
                    v.scalar_tensor_tensor(out=lo[:, which, :], in0=ps_m[:, 0, :], scalar=SCALE if which == Q else 1.0,
                                           in1=hi[:, which, :].bitcast(F32), op0=ALU.mult, op1=ALU.subtract).then_inc(lo_done, 1)

                def find_max(s, unit):
                    h, i = unit // QT, unit % QT
                    hold(dve, g, s_done, s.tile * PER_S + unit + 1)
                    v.tensor_reduce(maxima[:, s.buf % 2, i, h:h + 1], ps_s[:, unit % 2, 0:(i + 1) * P], AX.X,
                                    ALU.max).then_inc(max_done, 1)

                def split_max(s):
                    b = s.buf % 2
                    if s.after(1):
                        hold(dve, g, max_turned, s.tile)
                    hold(dve, g, max_done, (s.tile + 1) * PER_S)
                    v.tensor_scalar(neg_max[:, :, 0, :], maxima[:, b], -1.0, None, ALU.mult).then_inc(max_hi, 1)
                    hold(dve, g, max_hi, s.tile + 1)
                    v.scalar_tensor_tensor(out=neg_max[:, :, 1, :], in0=maxima[:, b], scalar=-1.0,
                                           in1=neg_max[:, :, 0, :].bitcast(F32), op0=ALU.mult, op1=ALU.subtract).then_inc(max_lo, 1)

                def norm_heads(s):
                    turned = ps_m[:, 0, :].rearrange("p (c h w) -> p c h w", c=QT, w=VW)
                    if s.after(1):
                        hold(dve, g, res_added, s.tile)
                    hold(dve, g, o_turned, s.tile + 1)
                    v.reciprocal(sums_inv[:], turned[:, :, :, HD]).then_inc(inv_done, 1)
                    hold(dve, g, inv_done, s.tile + 1)
                    v.tensor_tensor(o_norm[:].rearrange("p c h d -> p (c h) d"),
                                    turned[:, :, :, 0:HD].rearrange("p c h d -> p (c h) d"),
                                    sums_inv[:].rearrange("p c h -> p (c h)").unsqueeze(2).to_broadcast([P, QT * 4, HD]),
                                    ALU.mult).then_inc(o_normed, 1)

                def norm_rows(b):
                    hold(dve, g, res_added, b * QUADS + QUADS)
                    for c in range(QT):
                        v.bn_stats(stats[:, c, :], res[:, c, :]).then_inc(stats_done, 1)
                    for c in range(QT):
                        hold(dve, g, stats_done, b * QT + c + 1)
                        v.bn_aggr(mean_var[:, c, :], stats[:, c, :]).then_inc(averaged, 1)

                for which in (Q, K):
                    split(0, which)
                for unit in range(PER_S):
                    find_max(Step(0, 0, 0, U), unit)
                split_max(Step(0, 0, 0, U))

                def body(s):
                    done = 0
                    for j in range(PER_T):
                        if leads_group(s) and j in (Q, K):
                            split(group(s) + 1, j)
                        if j == HEADS_TURNED + 1 and s.after(1):
                            norm_heads(s.at(-1))
                        if s.at(1).within(N):
                            for _ in range(LEAD[j]):
                                find_max(s.at(1), done)
                                done += 1
                    if s.at(1).within(N):
                        split_max(s.at(1))
                    if s.after(1) and s.buf == 0:
                        norm_rows(s.lap - 1)

                steps(dve, body)
                norm_heads(Step(N - 1, U - 1, B - 1, U))
                norm_rows(B - 1)

            @block.tensor
            def _(pe):
                pe.wait_ge(w_in, 16 * 3 * 2 * HG)
                for n in range(3 * EC):
                    which, c = n // EC, n % EC
                    if n >= 1:
                        pe.wait_ge(w_copied, n)
                    for half in range(2):
                        last = pe.transpose(ps_m[:, 0, half * P:(half + 1) * P], w_rows[:, which, half, c * P:(c + 1) * P], g.ident[:])
                    last.then_inc(w_turned, 1)
                pe.wait_ge(w_copied, 3 * EC)
                pe.wait_ge(constants, 4)

                def turn_x(b, c):
                    if c:
                        hold(pe, g, xt_copied, b * EC + c)
                    else:
                        hold(pe, g, x_arrived, b * 16 + 16)
                    for t in range(QT):
                        last = pe.transpose(ps_m[:, 0, t * P:(t + 1) * P], x_in[:, t, c * P:(c + 1) * P], g.ident[:])
                    last.then_inc(xt_turned, 1)

                def project(n, half, which):
                    if which == Q:
                        if half == 0:
                            hold(pe, g, xt_copied, n * EC // 2 + EC)
                    else:
                        hold(pe, g, hi_done, n * 2 + which)
                        hold(pe, g, lo_done, n * 2 + which)
                    if which != V:
                        for c in range(EC):
                            last = pe.matmul(ps_m[:, 0, :], w_t[:, c, which, half * P:(half + 1) * P], x_t[:, c, :],
                                             start=(c == 0), stop=(c == EC - 1))
                        last.then_inc(projected, 1)
                    else:
                        for t in range(QT):
                            for c in range(EC):
                                last = pe.matmul(ps_m[:, 0, t * P:(t + 1) * P], x_t[:, c, t * P:(t + 1) * P],
                                                 w_t[:, c, 2, half * P:(half + 1) * P], start=(c == 0), stop=(c == EC - 1))
                        last.then_inc(v_projected, 1)

                def first_pass(s, unit):
                    h, i = unit // QT, unit % QT
                    half, head, w = s.buf // 2, (s.buf % 2) * 4 + h, (i + 1) * P
                    out = ps_s[:, unit % 2, 0:w]
                    if unit == 0 and s.buf % 2 == 0:
                        hold(pe, g, q_stacked[half], (s.lap + 1) * COPIES * 16)
                        hold(pe, g, k_stacked[half], (s.lap + 1) * COPIES * 16)
                    if s.after(1) or unit >= 2:
                        hold(pe, g, max_done, s.tile * PER_S + unit - 1)
                    pe.matmul(out, qs[0:K_MAX, half, head, i * P:(i + 1) * P], ks[0:K_MAX, half, head, 0:w], start=True, stop=False)
                    pe.matmul(out[:, i * P:w], ident_b[:], later_key[:], start=False, stop=True).then_inc(s_done, 1)

                def turn_max(s):
                    hold(pe, g, max_lo, s.tile + 1)
                    for i in range(QT):
                        last = pe.transpose(ps_m[0:8, 0, i * P:(i + 1) * P],
                                            neg_max[:, i].rearrange("p a h -> p (a h)").bitcast(F32), g.ident[:])
                    last.then_inc(max_turned, 1)

                def second_pass(s, i, pair):
                    half, w = s.buf // 2, T - i * P
                    unit = 2 * i + pair
                    if unit == 0:
                        hold(pe, g, max_stacked, (s.tile + 1) * 32)
                    if s.after(1) or unit >= 2:
                        hold(pe, g, exp_done, s.tile * PER_T + unit - 1)
                    for k in range(2):
                        head = (s.buf % 2) * 4 + 2 * pair + k
                        out = ps_t[:, 2 * pair + k, 0:w]
                        pe.matmul(out, ks[0:K_EXP, half, head, i * P:(i + 1) * P], qs[0:K_EXP, half, head, i * P:T], start=True, stop=False)
                        last = pe.matmul(out[:, 0:P], ident_b[:], earlier_query[:], start=False, stop=True)
                    last.then_inc(t_done, 1)

                def times_v(s, i):
                    half = s.buf // 2
                    if i == 0:
                        if s.buf % 2 == 0:
                            hold(pe, g, v_copied, group(s) + 1)
                        if s.after(1):
                            hold(pe, g, o_copied, s.tile)
                    hold(pe, g, exp_done, s.tile * PER_T + 2 * i + 2)
                    for h in range(4):
                        last = pe.matmul(ps_o[VW * h:VW * (h + 1), 0, i * P:T], v_one[:, half, i, (s.buf % 2) * 4 + h, :],
                                         exps[:, i % 2, h, 0:T - i * P], start=(i == 0), stop=(i == QT - 1), tile_position=(0, VW * h))
                    last.then_inc(pv_done, 1)

                def turn_heads(s):
                    hold(pe, g, o_copied, s.tile + 1)
                    n = s.at(1)
                    if leads_group(n):
                        hold(pe, g, v_copied, group(n) + 2)
                    elif turns_x(n):
                        hold(pe, g, xt_copied, n.lap * EC + 2 * EC)
                    elif n.within(N):
                        hold(pe, g, max_copied, n.tile + 1)
                    for i in range(QT):
                        last = pe.transpose(ps_m[:, 0, i * P:(i + 1) * P], o_t[:, i * P:(i + 1) * P], g.ident[:])
                    last.then_inc(o_turned, 1)

                for c in range(EC):
                    turn_x(0, c)
                for which in (Q, K, V):
                    project(0, 0, which)
                first = Step(0, 0, 0, U)
                for unit in range(PER_S):
                    first_pass(first, unit)
                pe.wait_ge(v_copied, 1)
                turn_max(first)

                def body(s):
                    done = 0
                    for j in range(PER_T):
                        if j in (Q, X[0]) and (leads_group(s) or turns_x(s)):
                            hold(pe, g, max_copied, s.tile + 1)
                        if leads_group(s) and j in (Q, K, V):
                            project(group(s) + 1, 1 - s.buf // 2, j)
                        if turns_x(s) and j in X:
                            turn_x(s.lap + 1, X.index(j))
                        if j == HEADS_TURNED and s.after(1):
                            turn_heads(s.at(-1))
                        if j == MAX_TURNED and s.at(1).within(N):
                            if s.after(1):
                                hold(pe, g, o_normed, s.tile)
                            elif leads_group(s):
                                hold(pe, g, v_copied, group(s) + 2)
                            turn_max(s.at(1))
                        if s.at(1).within(N):
                            for _ in range(LEAD[j]):
                                first_pass(s.at(1), done)
                                done += 1
                        second_pass(s, j // 2, j % 2)
                        if j == LAST_V and s.after(1):
                            times_v(s.at(-1), QT - 1)
                        if j % 2 and j >= 3:
                            times_v(s, j // 2 - 1)

                steps(pe, body)
                final = Step(N - 1, U - 1, B - 1, U)
                times_v(final, QT - 1)
                pe.wait_ge(o_normed, N - 1)
                turn_heads(final)


def stage_dispatch(nc, g):
    J, K, E = SORT_TILES, TOP_K, EXPERTS
    with ExitStack() as ctx:
        def sb(name, shape, dt=F32):
            return ctx.enter_context(nc.sbuf_tensor(f"dispatch_{name}", shape, dt))

        def sem(name):
            return ctx.enter_context(nc.semaphore(f"dispatch_{name}"))

        top = sb("top", [P, J, K])
        shifted = sb("shifted", [P, J, K])
        powers = sb("powers", [P, J, K])
        weight = sb("weight", [P, J, K])
        weight_sum = sb("weight_sum", [P, J])
        expert_no = sb("expert_no", [P, J, K])
        chosen = sb("chosen", [P, J, K, E])
        w = sort_buffers(sb, "moe", E, J)
        picked = sb("picked", [P, J, K, E])
        pair_slot = sb("pair_slot", [P, J, K])
        tile_of = sb("tile_of", [P, J, K])
        place_of = sb("place_of", [P, J, K])
        tmp_i = sb("tmp_i", [P, J * K], I32)
        hidden = sb("hidden", [P, J])
        at_place = sb("at_place", [P, 2, K, P])
        at_tile = sb("at_tile", [P, 2, K, PAIR_TILES])
        at_tile_row = sb("at_tile_row", [P, 2, K, 2, PAIR_TILES])
        count_e = sb("count_e", [P, E])
        count_p = sb("count_p", [P, P])
        count_t = sb("count_t", [P, PAIR_TILES])
        slot_up = sb("slot_up", [P, J])
        spare_row = sb("spare_row", [P, 1])
        ones = sb("ones", [P, P])
        below = sb("below", [P, P])
        row_up = sb("row_up", [P, PAIR_TILES])
        empty = sb("empty", [P, PAIR_TILES])
        row_of = sb("row_of", [P, PAIR_TILES])
        ends = sb("ends", [1, PLAN, E])
        tile_no = sb("tile_no", [1, PLAN, E])
        expert_of = sb("expert_of", [1, PLAN])
        ones_t = sb("ones_t", [1, PLAN])
        changed = sb("changed", [1, PLAN])
        changes = sb("changes", [1, PLAN])
        changes_i = sb("changes_i", [1, PLAN], I32)
        half = E // 2
        ps_rank = ctx.enter_context(nc.psum_tensor("ps_rank", [P, 2, 512], F32))
        ps_sum = ctx.enter_context(nc.psum_tensor("ps_sum", [P, 2, 512], F32))
        ps_table = ctx.enter_context(nc.psum_tensor("ps_table", [P, 512], F32))

        cleared, constants, v_chain = sem("cleared"), sem("constants"), sem("v_chain")
        shift_ready, exp_ready, members, ranked = sem("shift_ready"), sem("exp_ready"), sem("members"), sem("ranked")
        tiles_at, rows_at, weights_at, tabled = sem("tiles_at"), sem("rows_at"), sem("weights_at"), sem("tabled")
        table_used = sem("table_used")

        with nc.Block() as block:
            @block.gpsimd
            def _(pool):
                iota = nc.gpsimd.iota
                nc.gpsimd.memset(ones[:], 1.0).then_inc(cleared, 1)
                for out, pattern, base, step in (
                    (count_e[:], [[1, E]], 0, 0), (count_p[:], [[1, P]], 0, 0), (count_t[:], [[1, PAIR_TILES]], 0, 0),
                    (slot_up[:], [[P, J]], 1, 1),
                    (spare_row[:], [[0, 1]], SLOTS + 1, 1),
                    (tile_no[:], [[1, PLAN], [0, E]], 0, 0),
                ):
                    iota(out, pattern=pattern, base=base, channel_multiplier=step,
                         allow_small_or_imprecise_dtypes=True).then_inc(constants, 1)
                pool.wait_ge(cleared, 1)
                nc.gpsimd.affine_select(out=below[:], in_=ones[:], compare_op=ALU.is_gt, fill=0.0,
                                        base=0, pattern=[[1, P]], channel_multiplier=-1).then_inc(constants, 1)

            @block.scalar
            def _(act):
                act.wait_ge(shift_ready, 1)
                nc.scalar.activation(powers[:], shifted[:], ACT.Exp).then_inc(exp_ready, 1)

            @block.vector
            def _(dve):
                v = nc.vector
                link = sequence(dve, v_chain)
                link(v.tensor_copy(top[:], g.top_logits[:, :, 0:K]))
                v.tensor_tensor(shifted[:], top[:], top[:, :, 0:1].to_broadcast([P, J, K]), ALU.subtract).then_inc(shift_ready, 1)
                link(v.tensor_copy(expert_no[:], g.top_experts[:, :, 0:K]))
                dve.wait_ge(constants, 7)
                link(v.tensor_tensor(chosen[:].rearrange("p j k e -> p (j k) e"),
                                     count_e[:].unsqueeze(1).to_broadcast([P, J * K, E]),
                                     expert_no[:].rearrange("p j k -> p (j k)").unsqueeze(2).to_broadcast([P, J * K, E]),
                                     ALU.is_equal))
                link(v.tensor_tensor(chosen[:].rearrange("p j k e -> p j (k e)"), chosen[:].rearrange("p j k e -> p j (k e)"),
                                     g.slot_full[:].unsqueeze(2).to_broadcast([P, J, K * E]), ALU.mult))
                v.tensor_reduce(w.member[:], chosen[:].rearrange("p j k e -> p e j k"), AX.X, ALU.add).then_inc(members, 1)
                dve.wait_ge(exp_ready, 1)
                link(v.tensor_reduce(weight_sum[:], powers[:], AX.X, ALU.add))
                link(v.reciprocal(weight_sum[:], weight_sum[:]))
                link(v.tensor_tensor(weight[:], powers[:], weight_sum[:].unsqueeze(2).to_broadcast([P, J, K]), ALU.mult))
                dve.wait_ge(ranked, 1)
                halves = lambda ps: [(slice(i * half, (i + 1) * half),
                                      ps[:, i, 0:half * J].rearrange("p (g t) -> p g t", g=half)) for i in range(2)]
                slots_of_groups(nc, link, w, E, J, halves(ps_sum), halves(ps_rank))
                link(v.tensor_tensor(picked[:], chosen[:],
                                     w.slot[:].rearrange("p e j -> p j e").unsqueeze(2).to_broadcast([P, J, K, E]), ALU.mult))
                link(v.tensor_reduce(pair_slot[:], picked[:], AX.X, ALU.add))
                flat = "p j k -> p (j k)"
                split_slot(nc, link, tile_of[:].rearrange(flat), place_of[:].rearrange(flat), tmp_i[:], pair_slot[:].rearrange(flat))
                link(v.tensor_scalar(hidden[:], g.slot_full[:], -1.0, 1000.0, ALU.add, ALU.mult))
                link(v.tensor_tensor(tile_of[:], tile_of[:], hidden[:].unsqueeze(2).to_broadcast([P, J, K]), ALU.add))

                link(v.tensor_tensor(ends[:], w.tiles_end[0:1, :].unsqueeze(1).to_broadcast([1, PLAN, E]), tile_no[:], ALU.is_le))
                link(v.tensor_reduce(expert_of[:], ends[:], AX.X, ALU.add))
                link(v.tensor_scalar(expert_of[:], expert_of[:], float(E - 1), None, ALU.min))
                link(v.memset(changed[:, 0:1], 1.0))
                link(v.memset(ones_t[:], 1.0))
                link(v.tensor_tensor(changed[:, 1:], expert_of[:, 1:], expert_of[:, 0:PLAN - 1], ALU.not_equal))
                link(v.tensor_tensor_scan(changes[:], ones_t[:], changed[:], -1.0, ALU.mult, ALU.add))
                link(v.tensor_copy(changes_i[:], changes[:]))
                link(v.tensor_scalar(g.plan[:, 2, :], changes_i[:], WEIGHT_SLOTS - 1, None, ALU.bitwise_and))
                link(v.tensor_copy(g.plan[:, 0, :], expert_of[:]))
                link(v.tensor_copy(g.plan[:, 1, :], changed[:]))

                def place_pairs(s):
                    if s.after(2):
                        hold(dve, g, table_used, s.tile - 1)
                    j = bass.ds(s.tile, 1)
                    of = lambda x: x[:, j, :].rearrange("p a k -> p (a k)")
                    v.tensor_tensor(at_place[:, s.buf], count_p[:].unsqueeze(1).to_broadcast([P, K, P]),
                                    of(place_of).unsqueeze(2).to_broadcast([P, K, P]), ALU.is_equal)
                    v.tensor_tensor(at_tile[:, s.buf], count_t[:].unsqueeze(1).to_broadcast([P, K, PAIR_TILES]),
                                    of(tile_of).unsqueeze(2).to_broadcast([P, K, PAIR_TILES]), ALU.is_equal).then_inc(tiles_at, 1)
                    hold(dve, g, tiles_at, s.tile + 1)
                    v.tensor_scalar(at_tile_row[:, s.buf, :, 0, :], at_tile[:, s.buf], slot_up[:, j], None, ALU.mult).then_inc(rows_at, 1)
                    v.tensor_tensor(at_tile_row[:, s.buf, :, 1, :], at_tile[:, s.buf],
                                    of(weight).unsqueeze(2).to_broadcast([P, K, PAIR_TILES]), ALU.mult).then_inc(weights_at, 1)

                run_steps(dve, J, 2, 2, 1, place_pairs)
                dve.wait_ge(tabled, 1)
                link(v.tensor_copy(row_up[:], ps_table[:, 0:PAIR_TILES]))
                link(v.tensor_copy(g.pair_weight[:], ps_table[:, PAIR_TILES:2 * PAIR_TILES]))
                link(v.tensor_scalar(empty[:], row_up[:], 0.5, None, ALU.is_lt))
                link(v.tensor_scalar(g.pair_row[:], row_up[:], -1.0, 0.0, ALU.add, ALU.max))
                link(v.tensor_scalar(empty[:], empty[:], spare_row[:, 0:1], None, ALU.mult))
                link(v.tensor_tensor(row_of[:], row_up[:], empty[:], ALU.add))
                link(v.tensor_scalar(g.pair_sum_row[:], row_of[:], -1.0, None, ALU.add))

            @block.tensor
            def _(pe):
                pe.wait_ge(constants, 7)
                pe.wait_ge(members, 1)
                for i in range(2):
                    member = w.member[:, i * half:(i + 1) * half, :].rearrange("p g t -> p (g t)")
                    pe.matmul(ps_rank[:, i, 0:half * J], below[:], member, start=True, stop=True)
                    last = pe.matmul(ps_sum[:, i, 0:half * J], ones[:], member, start=True, stop=True)
                last.then_inc(ranked, 1)

                def add_to_table(s):
                    hold(pe, g, rows_at, s.tile + 1)
                    hold(pe, g, weights_at, s.tile + 1)
                    for k in range(K):
                        first = isinstance(s.tile, int) and s.tile == 0 and k == 0
                        final = isinstance(s.tile, int) and s.tile == J - 1 and k == K - 1
                        last = pe.matmul(ps_table[:, 0:2 * PAIR_TILES], at_place[:, s.buf, k, :],
                                         at_tile_row[:, s.buf, k].rearrange("p a t -> p (a t)"), start=first, stop=final)
                    last.then_inc(table_used, 1)
                    if final:
                        pe.wait_ge(table_used, J)
                        pe.sem_inc(tabled, 1)

                run_steps(pe, J, 2, 2, 1, add_to_table)


def stage_experts(nc, g):
    with ExitStack() as ctx:
        def sb(name, shape, dt=F32):
            return ctx.enter_context(nc.sbuf_tensor(f"experts_{name}", shape, dt))

        def sem(name):
            return ctx.enter_context(nc.semaphore(f"experts_{name}"))

        def bank(name, n=1):
            return ctx.enter_context(nc.psum_tensor(f"experts_{name}", [P, n, 512], F32))

        N, U = PAIR_TILES, 4
        up_w = sb("up_w", [P, WEIGHT_SLOTS, DC * 2 * INTER])
        down_w = sb("down_w", [IW, WEIGHT_SLOTS, IC * D])
        index = sb("index", [P, U], I32)
        sum_index = sb("sum_index", [P, U], I32)
        rows = sb("rows", [P, U, D])
        x_t = sb("x_t", [P, 2, DC, P])
        silu = sb("silu", [P, 2, INTER])
        h = sb("h", [P, 2, INTER])
        h_t = sb("h_t", [IW, IC, P])
        y = sb("y", [P, U, D])
        ps_x, ps_h, ps_gu, ps_y = bank("ps_x", 2), bank("ps_h", 2), bank("ps_gu", 2), bank("ps_y", 2)

        rows_in = [sem(f"rows_in{u}") for u in range(U)]
        weights_in = [sem(f"weights_in{u}") for u in range(U)]
        added = sem("added")
        index_set, sum_index_set = sem("index_set"), sem("sum_index_set")
        x_turned, xt_copied, gu_done, silu_done = sem("x_turned"), sem("xt_copied"), sem("gu_done"), sem("silu_done")
        h_done, h_turned, ht_copied, y_done, y_scaled = sem("h_done"), sem("h_turned"), sem("ht_copied"), sem("y_done"), sem("y_scaled")

        def steps(eng, body):
            run_steps(eng, N, U, U, 3, body)

        with nc.Block() as block:
            @block.sync
            def _(sp):
                def load(s):
                    if s.after(U):
                        hold(sp, g, y_done, s.tile - (U - 1))
                    t = bass.ds(s.tile, 1)
                    expert = sp.value_load(g.plan[0:1, 0, t], min_val=0, max_val=EXPERTS - 1)
                    is_new = sp.value_load(g.plan[0:1, 1, t], min_val=0, max_val=1)
                    slot = sp.value_load(g.plan[0:1, 2, t], min_val=0, max_val=WEIGHT_SLOTS - 1)
                    e, b = bass.ds(expert, 1), bass.ds(slot, 1)
                    sp.dma_start(up_w[:, b, :].rearrange("p a (c f) -> p (a c) f", c=DC),
                                 g.up_dram[e, :, :].rearrange("a (c p) f -> p (a c) f", p=P),
                                 cond=is_new).then_inc(weights_in[s.buf], 16)
                    sp.dma_start(down_w[:, b, :].rearrange("p a (c n) -> p (a c) n", c=IC),
                                 g.down_dram[e, :, :].rearrange("a (c p) n -> p (a c) n", p=IW),
                                 cond=is_new).then_inc(weights_in[s.buf], 16)

                steps(sp, load)

            @block.gpsimd
            def _(pool):
                def gather(s):
                    if s.after(U):
                        hold(pool, g, x_turned, s.tile - (U - 1))
                    nc.gpsimd.tensor_copy(index[:, s.buf:s.buf + 1], g.pair_row[:, bass.ds(s.tile, 1)]).then_inc(index_set, 1)
                    hold(pool, g, index_set, s.tile + 1)
                    nc.gpsimd.indirect_dma_start(
                        out=rows[:, s.buf, :], out_offset=None, in_=g.x2_rows,
                        in_offset=bass.IndirectOffsetOnAxis(ap=index[:, s.buf:s.buf + 1], axis=0),
                    ).then_inc(rows_in[s.buf], 16)

                def add(s):
                    nc.gpsimd.tensor_copy(sum_index[:, s.buf:s.buf + 1], g.pair_sum_row[:, bass.ds(s.tile, 1)]).then_inc(sum_index_set, 1)
                    hold(pool, g, sum_index_set, s.tile + 1)
                    hold(pool, g, y_scaled, s.tile + 1)
                    if s.after(1):
                        hold(pool, g, added, s.tile * 16)
                    nc.gpsimd.indirect_dma_start(
                        out=g.sum_rows, out_offset=bass.IndirectOffsetOnAxis(ap=sum_index[:, s.buf:s.buf + 1], axis=0),
                        in_=y[:, s.buf, :], in_offset=None, compute_op=ALU.add,
                    ).then_inc(added, 16)

                for t in range(3):
                    gather(Step(t, t % U, t // U, U))

                def body(s):
                    if s.at(3).within(N):
                        gather(s.at(3))
                    add(s)

                steps(pool, body)
                pool.wait_ge(added, 16 * N)

            @block.scalar
            def _(act):
                def xt(s):
                    b = s.buf % 2
                    if s.after(2):
                        hold(act, g, gu_done, s.tile - 1)
                    hold(act, g, x_turned, s.tile + 1)
                    nc.scalar.copy(x_t[:, b].rearrange("p c t -> p (c t)"), ps_x[:, b, :]).then_inc(xt_copied, 1)

                def silu_of(s):
                    b = s.buf % 2
                    if s.after(2):
                        hold(act, g, h_done, s.tile - 1)
                    hold(act, g, gu_done, s.tile + 1)
                    nc.scalar.activation(silu[:, b, :], ps_gu[:, b, 0:INTER], ACT.Silu).then_inc(silu_done, 1)

                def ht(s):
                    if s.after(1):
                        hold(act, g, y_done, s.tile)
                    hold(act, g, h_turned, s.tile + 1)
                    nc.scalar.copy(h_t[:].rearrange("p c t -> p (c t)"), ps_h[0:IW, s.buf % 2, 0:IC * P]).then_inc(ht_copied, 1)

                first = Step(0, 0, 0, U)
                xt(first)
                silu_of(first)
                xt(first.at(1))

                def body(s):
                    ht(s)
                    if s.at(1).within(N):
                        silu_of(s.at(1))
                    if s.at(2).within(N):
                        xt(s.at(2))

                steps(act, body)

            @block.vector
            def _(dve):
                v = nc.vector

                def gate(s):
                    b = s.buf % 2
                    if s.after(2):
                        hold(dve, g, h_turned, s.tile - 1)
                    hold(dve, g, silu_done, s.tile + 1)
                    v.tensor_tensor(h[:, b, :], ps_gu[:, b, INTER:2 * INTER], silu[:, b, :], ALU.mult).then_inc(h_done, 1)

                def scale(s):
                    if s.after(U):
                        hold(dve, g, added, 16 * (s.tile - (U - 1)))
                    hold(dve, g, y_done, s.tile + 1)
                    v.tensor_scalar(y[:, s.buf, :], ps_y[:, s.buf % 2, :], g.pair_weight[:, bass.ds(s.tile, 1)], None,
                                    ALU.mult).then_inc(y_scaled, 1)

                gate(Step(0, 0, 0, U))

                def body(s):
                    if s.at(1).within(N):
                        gate(s.at(1))
                    scale(s)

                steps(dve, body)

            @block.tensor
            def _(pe):
                def turn_x(s):
                    b = s.buf % 2
                    hold(pe, g, rows_in[s.buf], (s.lap + 1) * 16)
                    if s.after(2):
                        hold(pe, g, xt_copied, s.tile - 1)
                    for c in range(DC):
                        last = pe.transpose(ps_x[:, b, c * P:(c + 1) * P], rows[:, s.buf, c * P:(c + 1) * P], g.ident[:])
                    last.then_inc(x_turned, 1)

                def slot_of(s):
                    return bass.ds(pe.value_load(g.plan[0:1, 2, bass.ds(s.tile, 1)], min_val=0, max_val=WEIGHT_SLOTS - 1), 1)

                def mm_up(s):
                    b = s.buf % 2
                    slot = slot_of(s)
                    if s.after(2):
                        hold(pe, g, h_done, s.tile - 1)
                    hold(pe, g, weights_in[s.buf], (s.lap + 1) * 32)
                    hold(pe, g, xt_copied, s.tile + 1)
                    for c in range(DC):
                        last = pe.matmul(ps_gu[:, b, 0:2 * INTER], x_t[:, b, c, :],
                                         up_w[:, slot, c * 2 * INTER:(c + 1) * 2 * INTER].rearrange("p a n -> p (a n)"),
                                         start=(c == 0), stop=(c == DC - 1))
                    last.then_inc(gu_done, 1)

                def turn_h(s):
                    b = s.buf % 2
                    hold(pe, g, h_done, s.tile + 1)
                    if s.after(2):
                        hold(pe, g, ht_copied, s.tile - 1)
                    for c in range(IC):
                        last = pe.transpose(ps_h[0:IW, b, c * P:(c + 1) * P], h[:, b, c * IW:(c + 1) * IW], g.ident[:])
                    last.then_inc(h_turned, 1)

                def mm_down(s):
                    b = s.buf % 2
                    slot = slot_of(s)
                    if s.after(2):
                        hold(pe, g, y_scaled, s.tile - 1)
                    hold(pe, g, ht_copied, s.tile + 1)
                    for c in range(IC):
                        last = pe.matmul(ps_y[:, b, :], h_t[:, c, :],
                                         down_w[:, slot, c * D:(c + 1) * D].rearrange("p a n -> p (a n)"),
                                         start=(c == 0), stop=(c == IC - 1))
                    last.then_inc(y_done, 1)

                first = Step(0, 0, 0, U)
                turn_x(first)
                mm_up(first)
                turn_x(first.at(1))

                def body(s):
                    turn_h(s)
                    if s.at(1).within(N):
                        mm_up(s.at(1))
                    mm_down(s)
                    if s.at(2).within(N):
                        turn_x(s.at(2))

                steps(pe, body)


def stage_finish(nc, g):
    with ExitStack() as ctx:
        def sb(name, shape, dt=F32):
            return ctx.enter_context(nc.sbuf_tensor(f"finish_{name}", shape, dt))

        def sem(name):
            return ctx.enter_context(nc.semaphore(f"finish_{name}"))

        N, U = TOK_TILES, 4
        index = sb("index", [P, N], I32)
        rows = sb("rows", [P, U, D])
        stats = sb("stats", [P, U, 6])
        mean_var = sb("mean_var", [P, U, 2])
        var_eps = sb("var_eps", [P, U])
        rstd = sb("rstd", [P, U])
        normed = sb("normed", [P, U, D])
        rows_in = [sem(f"rows_in{u}") for u in range(U)]
        stored = [sem(f"stored{u}") for u in range(U)]
        index_set, stats_done, averaged, eps_added, rstd_done, out_done = (
            sem("index_set"), sem("stats_done"), sem("averaged"), sem("eps_added"), sem("rstd_done"), sem("out_done"))

        def steps(eng, body):
            run_steps(eng, N, U, U, 4, body)

        with nc.Block() as block:
            @block.sync
            def _(sp):
                def store(s):
                    hold(sp, g, out_done, s.tile + 1)
                    sp.dma_start(g.out_rows[bass.ds(s.tile * P, P), :], normed[:, s.buf, :]).then_inc(stored[s.buf], 16)

                steps(sp, store)
                for u in range(U):
                    sp.wait_ge(stored[u], 16 * len(range(u, N, U)))

            @block.gpsimd
            def _(pool):
                def gather(s):
                    if s.after(U):
                        hold(pool, g, out_done, s.tile - (U - 1))
                    nc.gpsimd.tensor_copy(index[:, s.buf:s.buf + 1], g.slot_of_token[:, bass.ds(s.tile, 1)]).then_inc(index_set, 1)
                    hold(pool, g, index_set, s.tile + 1)
                    nc.gpsimd.indirect_dma_start(
                        out=rows[:, s.buf, :], out_offset=None, in_=g.sum_rows,
                        in_offset=bass.IndirectOffsetOnAxis(ap=index[:, s.buf:s.buf + 1], axis=0),
                    ).then_inc(rows_in[s.buf], 16)

                def rstd_of(s):
                    b = s.buf
                    hold(pool, g, averaged, s.tile + 1)
                    if s.after(U):
                        hold(pool, g, out_done, s.tile - (U - 1))
                    nc.gpsimd.tensor_scalar(var_eps[:, b:b + 1], mean_var[:, b, 1:2], EPS, None, ALU.add).then_inc(eps_added, 1)
                    hold(pool, g, eps_added, s.tile + 1)
                    nc.gpsimd.tensor_tensor(rstd[:, b:b + 1], var_eps[:, b:b + 1], g.minus_half[:], ALU.pow).then_inc(rstd_done, 1)

                for t in range(3):
                    gather(Step(t, t % U, t // U, U))

                def body(s):
                    if s.at(3).within(N):
                        gather(s.at(3))
                    rstd_of(s)

                steps(pool, body)

            @block.vector
            def _(dve):
                v = nc.vector

                def norm_in(s):
                    b = s.buf
                    hold(dve, g, rows_in[b], (s.lap + 1) * 16)
                    v.bn_stats(stats[:, b, :], rows[:, b, :]).then_inc(stats_done, 1)
                    hold(dve, g, stats_done, s.tile + 1)
                    v.bn_aggr(mean_var[:, b, :], stats[:, b, :]).then_inc(averaged, 1)

                def norm_out(s):
                    b = s.buf
                    if s.after(U):
                        hold(dve, g, stored[b], s.lap * 16)
                    hold(dve, g, rstd_done, s.tile + 1)
                    v.tensor_scalar(normed[:, b, :], rows[:, b, :], mean_var[:, b, 0:1], rstd[:, b:b + 1],
                                    ALU.subtract, ALU.mult).then_inc(out_done, 1)

                norm_in(Step(0, 0, 0, U))

                def body(s):
                    if s.at(1).within(N):
                        norm_in(s.at(1))
                    norm_out(s)

                steps(dve, body)


def decoder_layer(nc, x, tokens, context, wq, wk, wv, gate, up, down, out):
    g = Tensors()
    g.x_dram, g.tokens, g.context, g.wq, g.wk, g.wv = x, tokens, context, wq, wk, wv
    g.gate_dram, g.up_dram, g.down_dram = gate, up, down
    g.out_rows = out.rearrange("b t d -> (b t) d")
    g.x1_rows = nc.dram_tensor("x1_rows", (N_TOK, D), F32).ap()
    g.x2_rows = nc.dram_tensor("x2_rows", (SLOTS, D), F32).ap()
    g.split_rows = nc.dram_tensor("split_rows", (2, 2, 2, P, T), F32).ap()
    g.sum_rows = nc.dram_tensor("sum_rows", (SLOTS + P, D), F32).ap()

    sb = nc.alloc_sbuf_tensor
    g.ident = sb("ident", [P, P], F32)
    g.minus_half = sb("minus_half", [P, 1], F32)
    g.gate = sb("gate_w", [P, DC, EXPERTS], F32)
    g.slot_of_token = sb("slot_of_token", [P, TOK_TILES], I32)
    g.token_of_slot = sb("token_of_slot", [P, SORT_TILES], I32)
    g.slot_full = sb("slot_full", [P, SORT_TILES], F32)
    g.hash_of_tile = sb("hash_of_tile", [1, SORT_TILES], I32)
    g.top_logits = sb("top_logits", [P, SORT_TILES, 8], F32)
    g.top_experts = sb("top_experts", [P, SORT_TILES, 8], U32)
    g.plan = sb("plan", [1, 3, PLAN], I32)
    g.pair_weight = sb("pair_weight", [P, PAIR_TILES], F32)
    g.pair_row = sb("pair_row", [P, PAIR_TILES], I32)
    g.pair_sum_row = sb("pair_sum_row", [P, PAIR_TILES], I32)
    g.constant = nc.alloc_semaphore("constant")

    with nc.sbuf_tensor("ctx_t", [P, HASHES, DC, D], F32) as g.ctx_t:
        with nc.sbuf_tensor("spare_zeros", [P, D], F32) as zeros, nc.semaphore("zeroed") as zeroed, \
             nc.semaphore("spare_stored") as spare_stored, nc.Block() as block:
            @block.gpsimd
            def _(pool):
                nc.gpsimd.memset(g.minus_half[:], -0.5).then_inc(g.constant, 1)
                nc.gpsimd.memset(zeros[:], 0.0).then_inc(zeroed, 1)

            @block.sync
            def _(sp):
                sp.wait_ge(zeroed, 1)
                sp.dma_start(g.sum_rows[SLOTS:SLOTS + P, :], zeros[:]).then_inc(spare_stored, 16)
                sp.wait_ge(spare_stored, 16)

        stage_sort(nc, g)
        stage_attention(nc, g)
        stage_hash_ffn(nc, g)
    stage_dispatch(nc, g)
    stage_experts(nc, g)
    stage_finish(nc, g)


_INS = ["x", "itok_BxS_13_99985", "ctx_2048", "L0_attn_Wq", "L0_attn_Wk", "L0_attn_Wv",
        "L0_ffn_gate", "L0_ffn_gate_up_proj", "L0_ffn_down_proj"]


def kernel(**inputs):
    import numpy as _np
    import concourse.bacc as _bacc
    from concourse import mybir as _mybir
    from concourse.bass_utils import run_bass_kernel_spmd as _run

    nc = _bacc.Bacc("TRN2", target_bir_lowering=False, num_devices=1)
    arrays, args = {}, []
    for name in _INS:
        a = _np.ascontiguousarray(inputs[name])
        arrays[f"in_{name}_dram"] = a
        args.append(nc.dram_tensor(f"in_{name}_dram", a.shape, _mybir.dt.from_np(a.dtype), kind="ExternalInput").ap())
    args.append(nc.dram_tensor("out_0_dram", (B, T, D), _mybir.dt.float32, kind="ExternalOutput").ap())
    decoder_layer(nc, *args)
    r = _run(nc, [arrays], core_ids=[0])
    return r.results[0]["out_0_dram"]
```

```python
from contextlib import ExitStack

import concourse.bass as bass
from concourse import mybir

P = 128
ALU = mybir.AluOpType
ACT = mybir.ActivationFunctionType
AX = mybir.AxisListType
F32 = mybir.dt.float32
F32R = mybir.dt.float32r
BF16 = mybir.dt.bfloat16
I32 = mybir.dt.int32
U32 = mybir.dt.uint32

B, T, D = 4, 512, 512
N_TOK = B * T
TOK_TILES = N_TOK // P
DC = D // P
EPS = 1e-5
HD, EMB = 16, 256

VOCAB, HASHES = 25000, 4
HASH_SPAN = VOCAB // HASHES
SORT_TILES = TOK_TILES + HASHES - 1
SLOTS = SORT_TILES * P

EXPERTS, TOP_K, INTER = 32, 4, 192
IC = 2
IW = INTER // IC
PAIR_TILES = N_TOK * TOP_K // P + EXPERTS - 1
PLAN = PAIR_TILES + 1
WEIGHT_SLOTS = 4


class Tensors:
    pass


def sequence(eng, sem):
    done = [0]

    def link(instruction):
        done[0] += 1
        instruction.then_inc(sem, 1)
        eng.wait_ge(sem, done[0])

    return link


def slots_of_groups(nc, link, w, groups, tiles, ones_sum, ranks):
    v = nc.vector
    flat = "p g t -> p (g t)"
    link(v.memset(w.keep[:], 1.0))
    link(v.memset(w.keep[:, :, 0:1], 0.0))
    for part, ps in ones_sum:
        link(v.tensor_copy(w.sums[:, part], ps))
    link(v.tensor_tensor_scan(w.upto[:].rearrange(flat), w.keep[:].rearrange(flat),
                              w.sums[:].rearrange(flat), 0.0, ALU.mult, ALU.add))
    link(v.tensor_scalar(w.n_tiles_i[:], w.upto[:, :, tiles - 1], P / 2 - 0.5, 1.0 / P, ALU.add, ALU.mult))
    link(v.tensor_copy(w.n_tiles[:], w.n_tiles_i[:]))
    link(v.memset(w.ones_g[:], 1.0))
    link(v.tensor_tensor_scan(w.tiles_end[:], w.ones_g[:], w.n_tiles[:], 0.0, ALU.mult, ALU.add))
    link(v.tensor_tensor(w.first[:], w.tiles_end[:], w.n_tiles[:], ALU.subtract))
    link(v.tensor_scalar(w.first[:], w.first[:], float(P), None, ALU.mult))
    link(v.tensor_tensor(w.slot[:], w.upto[:], w.sums[:], ALU.subtract))
    for part, ps in ranks:
        link(v.tensor_tensor(w.slot[:, part], ps, w.slot[:, part], ALU.add))
    link(v.tensor_tensor(w.slot[:], w.slot[:], w.first[:].unsqueeze(2).to_broadcast([P, groups, tiles]), ALU.add))


def sort_buffers(sb, name, groups, tiles):
    w = Tensors()
    w.keep, w.sums, w.upto, w.slot = (
        sb(f"{name}_{n}", [P, groups, tiles], F32) for n in ("keep", "sums", "upto", "slot"))
    w.n_tiles, w.ones_g, w.tiles_end, w.first = (
        sb(f"{name}_{n}", [P, groups], F32) for n in ("n_tiles", "ones_g", "tiles_end", "first"))
    w.n_tiles_i = sb(f"{name}_n_tiles_i", [P, groups], I32)
    return w


def split_slot(nc, link, tile_of, place_of, tmp_i, slots):
    v = nc.vector
    link(v.tensor_scalar(tmp_i, slots, -(P / 2 - 0.5), 1.0 / P, ALU.add, ALU.mult))
    link(v.tensor_copy(tile_of, tmp_i))
    link(v.scalar_tensor_tensor(out=place_of, in0=tile_of, scalar=-float(P), in1=slots,
                                op0=ALU.mult, op1=ALU.add))


def stage_sort(nc, g):
    count_p, ones, below = g.count_p, g.ones, g.below
    with ExitStack() as ctx:
        def sb(name, shape, dt=F32):
            return ctx.enter_context(nc.sbuf_tensor(f"sort_{name}", shape, dt))

        def sem(name):
            return ctx.enter_context(nc.semaphore(f"sort_{name}"))

        ids_i = sb("ids_i", [TOK_TILES, P], I32)
        ids_f = sb("ids_f", [TOK_TILES, P])
        ids = sb("ids", [P, TOK_TILES])
        at_least = sb("at_least", [P, HASHES + 1, TOK_TILES])
        member = sb("member", [P, HASHES, TOK_TILES])
        w = sort_buffers(sb, "hash", HASHES, TOK_TILES)
        picked = sb("picked", [P, HASHES, TOK_TILES])
        tok_i = sb("tok_i", [P, TOK_TILES], I32)
        tile_of = sb("tile_of", [P, TOK_TILES])
        place_of = sb("place_of", [P, TOK_TILES])
        slot_of = sb("slot_of", [P, TOK_TILES])
        at_place = sb("at_place", [P, TOK_TILES, P])
        at_tile = sb("at_tile", [P, TOK_TILES, SORT_TILES])
        token_up = sb("token_up", [P, TOK_TILES])
        w_rows = sb("w_rows", [P, 3, 2, EMB])
        spare_up = sb("spare_up", [P, SORT_TILES])
        empty = sb("empty", [P, SORT_TILES])
        row_up = sb("row_up", [P, SORT_TILES])
        ctx_rows = sb("ctx_rows", [P, HASHES * DC, D])
        plan = sb("plan", [1, SORT_TILES, HASHES])
        plan_f = sb("plan_f", [1, SORT_TILES])
        plan_no = sb("plan_no", [1, SORT_TILES, HASHES])
        ps = ctx.enter_context(nc.psum_tensor("sort_ps", [P, 4, 512], F32))
        ps_ct = ctx.enter_context(nc.psum_tensor("ct_ps", [P, 4, 512], F32))

        ids_in, ctx_in, gate_in = sem("ids_in"), sem("ctx_in"), sem("gate_in")
        w_in, x_arrived, w_turned, w_copied = sem("w_in"), sem("x_arrived"), sem("w_turned"), sem("w_copied")
        cleared, constants = sem("cleared"), sem("constants")
        ids_float, ids_turned = sem("ids_float"), sem("ids_turned")
        members, ranked, v_chain, v_chain2 = sem("members"), sem("ranked"), sem("v_chain"), sem("v_chain2")
        placed, tabled = sem("placed"), sem("tabled")
        ct_turned, ct_copied = sem("ct_turned"), sem("ct_copied")

        with nc.Block() as block:
            @block.sync
            def _(sp):
                sp.dma_start(ids_i[:], g.tokens.rearrange("b (j p) -> (b j) p", p=P)).then_inc(ids_in, 16)
                sp.dma_start(ctx_rows[:], g.context.rearrange("e (c p) d -> p (e c) d", p=P)).then_inc(ctx_in, 16)
                with nc.allow_non_contiguous_dma(reason="the gate's rows are 32 elements"):
                    sp.dma_start(g.gate[:], g.gate_dram.rearrange("(c p) e -> p c e", p=P)).then_inc(gate_in, 16)
                for n, w_dram in enumerate((g.wq, g.wk, g.wv)):
                    for half in range(2):
                        for h in range(P // HD):
                            sp.dma_start(w_rows[h * HD:(h + 1) * HD, n, half, :],
                                         w_dram[half * (P // HD) + h, 0:HD, 0:EMB]).then_inc(w_in, 16)
                sp.dma_start(g.x_in[:], g.x_dram[0, :, 0:EMB].rearrange("(c p) e -> p c e", p=P)).then_inc(x_arrived, 16)
                sp.wait_ge(gate_in, 16)
                sp.wait_ge(x_arrived, 16)

            @block.gpsimd
            def _(pool):
                nc.gpsimd.memset(g.ident[:], 0.0).then_inc(cleared, 1)
                nc.gpsimd.memset(ones[:], 1.0).then_inc(cleared, 1)
                nc.gpsimd.iota(count_p[:], pattern=[[1, P]], base=0, channel_multiplier=0,
                               allow_small_or_imprecise_dtypes=True).then_inc(constants, 1)
                nc.gpsimd.iota(g.count_t[:], pattern=[[1, PLAN]], base=0, channel_multiplier=0,
                               allow_small_or_imprecise_dtypes=True).then_inc(constants, 1)
                nc.gpsimd.iota(token_up[:], pattern=[[P, TOK_TILES]], base=1, channel_multiplier=1,
                               allow_small_or_imprecise_dtypes=True).then_inc(constants, 1)
                nc.gpsimd.iota(spare_up[:], pattern=[[P, SORT_TILES]], base=N_TOK + 1, channel_multiplier=1,
                               allow_small_or_imprecise_dtypes=True).then_inc(constants, 1)
                nc.gpsimd.iota(plan_no[:], pattern=[[1, SORT_TILES], [0, HASHES]], base=0, channel_multiplier=0,
                               allow_small_or_imprecise_dtypes=True).then_inc(constants, 1)
                pool.wait_ge(cleared, 2)
                nc.gpsimd.affine_select(out=g.ident[:], in_=g.ident[:], compare_op=ALU.not_equal, fill=1.0,
                                        base=0, pattern=[[-1, P]], channel_multiplier=1).then_inc(constants, 1)
                nc.gpsimd.affine_select(out=below[:], in_=ones[:], compare_op=ALU.is_gt, fill=0.0,
                                        base=0, pattern=[[1, P]], channel_multiplier=-1).then_inc(constants, 1)
                nc.gpsimd.iota(g.pair_offset[:], pattern=[[N_TOK, TOP_K]], base=0, channel_multiplier=0,
                               allow_small_or_imprecise_dtypes=True)
                nc.gpsimd.iota(g.spare_pair_up[:], pattern=[[P, PAIR_TILES]], base=TOP_K * N_TOK + 1, channel_multiplier=1,
                               allow_small_or_imprecise_dtypes=True)

            @block.vector
            def _(dve):
                v = nc.vector
                link = sequence(dve, v_chain)
                dve.wait_ge(ids_in, 16)
                link(v.tensor_scalar(ids_f[:], ids_i[:], float(VOCAB - 1), 0.0, ALU.min, ALU.max))
                v.tensor_copy(ids_f[:], ids_f[:]).then_inc(ids_float, 1)
                dve.wait_ge(ids_turned, 1)
                v.tensor_copy(ids[:], ps[:, 0, 0:TOK_TILES]).then_inc(v_chain, 1)
                dve.wait_ge(v_chain, 2)
                link = sequence(dve, v_chain2)
                link(v.memset(at_least[:, 0, :], 1.0))
                link(v.memset(at_least[:, HASHES, :], 0.0))
                for e in range(1, HASHES):
                    link(v.tensor_scalar(at_least[:, e, :], ids[:], float(e * HASH_SPAN), None, ALU.is_ge))
                v.tensor_tensor(member[:], at_least[:, 0:HASHES, :], at_least[:, 1:HASHES + 1, :],
                                ALU.subtract).then_inc(members, 1)
                dve.wait_ge(ranked, 1)
                shape = ps[:, 1, 0:HASHES * TOK_TILES].rearrange("p (g t) -> p g t", g=HASHES)
                shape2 = ps[:, 2, 0:HASHES * TOK_TILES].rearrange("p (g t) -> p g t", g=HASHES)
                slots_of_groups(nc, link, w, HASHES, TOK_TILES, [(slice(0, HASHES), shape2)], [(slice(0, HASHES), shape)])
                link(v.tensor_tensor(picked[:], w.slot[:], member[:], ALU.mult))
                link(v.tensor_reduce(slot_of[:], picked[:].rearrange("p g t -> p t g"), AX.X, ALU.add))
                split_slot(nc, link, tile_of[:], place_of[:], tok_i[:], slot_of[:])
                dve.wait_ge(constants, 7)
                link(v.tensor_tensor(at_place[:], count_p[:].unsqueeze(1).to_broadcast([P, TOK_TILES, P]),
                                     place_of[:].unsqueeze(2).to_broadcast([P, TOK_TILES, P]), ALU.is_equal))
                link(v.tensor_tensor(at_tile[:], g.count_t[:, 0:SORT_TILES].unsqueeze(1).to_broadcast([P, TOK_TILES, SORT_TILES]),
                                     tile_of[:].unsqueeze(2).to_broadcast([P, TOK_TILES, SORT_TILES]), ALU.is_equal))
                v.tensor_tensor(at_tile[:], at_tile[:], token_up[:].unsqueeze(2).to_broadcast([P, TOK_TILES, SORT_TILES]),
                                ALU.mult).then_inc(placed, 1)
                dve.wait_ge(tabled, 1)
                link(v.tensor_copy(g.slot_token_up[:], ps[:, 3, 0:SORT_TILES]))
                link(v.tensor_scalar(g.slot_full[:], g.slot_token_up[:], 0.5, None, ALU.is_gt))
                link(v.tensor_scalar(g.token_of_slot[:], g.slot_token_up[:], -1.0, 0.0, ALU.add, ALU.max))
                link(v.tensor_scalar(empty[:], g.slot_token_up[:], 0.5, None, ALU.is_lt))
                link(v.tensor_tensor(row_up[:], empty[:], spare_up[:], ALU.mult))
                link(v.tensor_tensor(row_up[:], row_up[:], g.slot_token_up[:], ALU.add))
                link(v.tensor_scalar(g.x2_row_of_slot[:], row_up[:], -1.0, None, ALU.add))
                link(v.tensor_tensor(plan[:], w.tiles_end[0:1, :].unsqueeze(1).to_broadcast([1, SORT_TILES, HASHES]),
                                     plan_no[:], ALU.is_le))
                link(v.tensor_reduce(plan_f[:], plan[:], AX.X, ALU.add))
                link(v.tensor_scalar(g.hash_of_tile[:], plan_f[:], float(HASHES - 1), None, ALU.min))

            @block.scalar
            def _(act):
                for n in range(HASHES * DC):
                    act.wait_ge(ct_turned, n + 1)
                    e, c = n // DC, n % DC
                    nc.scalar.copy(g.ctx_t[:, e, c, :], ps_ct[:, n % 4, :]).then_inc(ct_copied, 1)
                for n in range(3 * EMB // P):
                    act.wait_ge(w_turned, n + 1)
                    nc.scalar.copy(g.w_t[:, n % (EMB // P), n // (EMB // P), :], ps_ct[:, n % 4, 0:EMB]).then_inc(w_copied, 1)

            @block.tensor
            def _(pe):
                pe.wait_ge(constants, 7)
                pe.wait_ge(ids_float, 1)
                pe.transpose(ps[:, 0, 0:TOK_TILES], ids_f[:], g.ident[0:TOK_TILES, 0:TOK_TILES]).then_inc(ids_turned, 1)
                pe.wait_ge(ctx_in, 16)

                def turn(n):
                    e, c = n // DC, n % DC
                    if n >= 4:
                        pe.wait_ge(ct_copied, n - 3)
                    for r in range(DC):
                        last = pe.transpose(ps_ct[:, n % 4, r * P:(r + 1) * P],
                                            ctx_rows[:, e * DC + r, c * P:(c + 1) * P], g.ident[:])
                    last.then_inc(ct_turned, 1)

                for n in range(2):
                    turn(n)
                pe.wait_ge(members, 1)
                flat = member[:].rearrange("p g t -> p (g t)")
                pe.matmul(ps[:, 1, 0:HASHES * TOK_TILES], below[:], flat, start=True, stop=True)
                pe.matmul(ps[:, 2, 0:HASHES * TOK_TILES], ones[:], flat, start=True, stop=True).then_inc(ranked, 1)
                for n in range(2, HASHES * DC):
                    turn(n)
                pe.wait_ge(placed, 1)
                for t in range(TOK_TILES):
                    last = pe.matmul(ps[:, 3, 0:SORT_TILES], at_place[:, t, :], at_tile[:, t, :],
                                     start=(t == 0), stop=(t == TOK_TILES - 1))
                last.then_inc(tabled, 1)
                pe.wait_ge(w_in, 16 * 3 * EMB // HD)
                pe.wait_ge(ct_copied, HASHES * DC)
                for n in range(3 * EMB // P):
                    which, c = n // (EMB // P), n % (EMB // P)
                    if n >= 4:
                        pe.wait_ge(w_copied, n - 3)
                    for half in range(2):
                        last = pe.transpose(ps_ct[:, n % 4, half * P:(half + 1) * P],
                                            w_rows[:, which, half, c * P:(c + 1) * P], g.ident[:])
                    last.then_inc(w_turned, 1)


class Step:

    def __init__(self, tile, buf, lap, unroll):
        self.tile, self.buf, self.lap, self.unroll = tile, buf, lap, unroll

    def at(self, k):
        n = self.buf + k
        return Step(self.tile + k, n % self.unroll, self.lap + n // self.unroll, self.unroll)

    def within(self, count):
        return not isinstance(self.tile, int) or 0 <= self.tile < count

    def after(self, n):
        return not isinstance(self.tile, int) or self.tile >= n


def run_steps(eng, count, unroll, head, tail, body):
    looped = (count - head - tail) // unroll
    for t in range(head):
        body(Step(t, t % unroll, t // unroll, unroll))
    with eng.Fori(0, looped) as i:
        for u in range(unroll):
            body(Step(i * unroll + (head + u), u, i + head // unroll, unroll))
    for t in range(head + looped * unroll, count):
        body(Step(t, t % unroll, t // unroll, unroll))


def hold(eng, g, sem, value):
    if not isinstance(value, int):
        value = eng.to_reg(value)
        eng.wait_ge(g.constant, 1)
    eng.wait_ge(sem, value)


def stage_hash_ffn(nc, g):
    with ExitStack() as ctx:
        def sb(name, shape, dt=F32):
            return ctx.enter_context(nc.sbuf_tensor(f"hash_ffn_{name}", shape, dt))

        def sem(name):
            return ctx.enter_context(nc.semaphore(f"hash_ffn_{name}"))

        def bank(name, n=1):
            return ctx.enter_context(nc.psum_tensor(f"hash_ffn_{name}", [P, n, 512], F32))

        N, U = SORT_TILES, 4
        index = sb("index", [P, U], I32)
        out_index = sb("out_index", [P, U], I32)
        rows = sb("rows", [P, U, D])
        x_t = sb("x_t", [P, 2, DC, P])
        silu = sb("silu", [P, 2, D])
        h = sb("h", [P, 2, D])
        h_t = sb("h_t", [P, DC, P])
        total = sb("total", [P, 2, D])
        stats = sb("stats", [P, 6])
        mean_var = sb("mean_var", [P, 2, 2])
        var_eps = sb("var_eps", [P, 2])
        rstd = sb("rstd", [P, 2])
        x2 = sb("x2", [P, U, D])
        x2_t = sb("x2_t", [P, DC, P])
        logits = sb("logits", [P, EXPERTS])
        largest = sb("largest", [P, 8])
        largest_at = sb("largest_at", [P, 8], U32)
        absent = sb("absent", [P, SORT_TILES])
        expert_no = sb("expert_no", [P, TOP_K])
        chosen = sb("chosen", [P, TOP_K, EXPERTS])
        member = sb("member", [P, EXPERTS])

        ps_x, ps_h, ps_x2, ps_u, ps_y, ps_l = bank("ps_x"), bank("ps_h"), bank("ps_x2"), bank("ps_u", 2), bank("ps_y", 2), bank("ps_l")
        rows_in = [sem(f"rows_in{u}") for u in range(U)]
        stored = [sem(f"stored{u}") for u in range(U)]
        index_set, out_index_set, x_turned, xt_copied = sem("index_set"), sem("out_index_set"), sem("x_turned"), sem("xt_copied")
        u_done, silu_done, h_done, h_turned, ht_copied = sem("u_done"), sem("silu_done"), sem("h_done"), sem("h_turned"), sem("ht_copied")
        y_done, added, stats_done, averaged = sem("y_done"), sem("added"), sem("stats_done"), sem("averaged")
        eps_added, rstd_done, x2_done = sem("eps_added"), sem("rstd_done"), sem("x2_done")
        x2_turned, x2t_copied, logits_done = sem("x2_turned"), sem("x2t_copied"), sem("logits_done")
        logits_copied, top_found, top_indexed, top_kept = sem("logits_copied"), sem("top_found"), sem("top_indexed"), sem("top_kept")
        absent_set, numbered, compared, counted = sem("absent_set"), sem("numbered"), sem("compared"), sem("counted")

        def steps(eng, body):
            run_steps(eng, N, U, U, 3, body)

        with nc.Block() as block:
            @block.gpsimd
            def _(pool):
                def rstd_of(s):
                    b = s.buf % 2
                    hold(pool, g, averaged, s.tile + 1)
                    nc.gpsimd.tensor_scalar(var_eps[:, b:b + 1], mean_var[:, b, 1:2], EPS, None, ALU.add).then_inc(eps_added, 1)
                    hold(pool, g, eps_added, s.tile + 1)
                    if s.after(2):
                        hold(pool, g, x2_done, s.tile - 1)
                    nc.gpsimd.tensor_tensor(rstd[:, b:b + 1], var_eps[:, b:b + 1], g.minus_half[:], ALU.pow).then_inc(rstd_done, 1)

                def gather(s):
                    if s.after(U):
                        hold(pool, g, added, s.tile - (U - 1))
                    nc.gpsimd.tensor_copy(index[:, s.buf:s.buf + 1], g.token_of_slot[:, bass.ds(s.tile, 1)]).then_inc(index_set, 1)
                    hold(pool, g, index_set, s.tile + 1)
                    nc.gpsimd.indirect_dma_start(
                        out=rows[:, s.buf, :], out_offset=None, in_=g.x1_rows,
                        in_offset=bass.IndirectOffsetOnAxis(ap=index[:, s.buf:s.buf + 1], axis=0),
                    ).then_inc(rows_in[s.buf], 16)

                def store(s):
                    if s.after(U):
                        hold(pool, g, stored[s.buf], s.lap * 16)
                    nc.gpsimd.tensor_copy(out_index[:, s.buf:s.buf + 1], g.x2_row_of_slot[:, bass.ds(s.tile, 1)]).then_inc(out_index_set, 1)
                    hold(pool, g, out_index_set, s.tile + 1)
                    hold(pool, g, x2_done, s.tile + 1)
                    nc.gpsimd.indirect_dma_start(
                        out=g.x2_rows, out_offset=bass.IndirectOffsetOnAxis(ap=out_index[:, s.buf:s.buf + 1], axis=0),
                        in_=x2[:, s.buf, :], in_offset=None,
                    ).then_inc(stored[s.buf], 16)

                pool.wait_ge(g.constant, 1)
                for t in range(3):
                    gather(Step(t, t % U, t // U, U))

                def body(s):
                    if s.at(3).within(N):
                        gather(s.at(3))
                    rstd_of(s)
                    if s.after(1):
                        store(s.at(-1))

                steps(pool, body)
                store(Step(N - 1, (N - 1) % U, (N - 1) // U, U))
                for u in range(U):
                    pool.wait_ge(stored[u], 16 * len(range(u, N, U)))

            @block.scalar
            def _(act):
                def xt(s):
                    if s.after(2):
                        hold(act, g, u_done, s.tile - 1)
                    hold(act, g, x_turned, s.tile + 1)
                    nc.scalar.copy(x_t[:, s.buf % 2].rearrange("p c t -> p (c t)"), ps_x[:, 0, :]).then_inc(xt_copied, 1)

                def silu_of(s):
                    if s.after(2):
                        hold(act, g, h_done, s.tile - 1)
                    hold(act, g, u_done, s.tile + 1)
                    nc.scalar.activation(silu[:, s.buf % 2, :], ps_u[:, s.buf % 2, :], ACT.Silu).then_inc(silu_done, 1)

                def ht(s):
                    if s.after(1):
                        hold(act, g, y_done, s.tile)
                    hold(act, g, h_turned, s.tile + 1)
                    nc.scalar.copy(h_t[:].rearrange("p c t -> p (c t)"), ps_h[:, 0, :]).then_inc(ht_copied, 1)

                def x2t(s):
                    if s.after(1):
                        hold(act, g, logits_done, s.tile)
                    hold(act, g, x2_turned, s.tile + 1)
                    nc.scalar.copy(x2_t[:].rearrange("p c t -> p (c t)"), ps_x2[:, 0, :]).then_inc(x2t_copied, 1)

                first = Step(0, 0, 0, U)
                xt(first)
                silu_of(first)
                xt(first.at(1))

                def body(s):
                    ht(s)
                    if s.at(1).within(N):
                        silu_of(s.at(1))
                    if s.after(1):
                        x2t(s.at(-1))
                    if s.at(2).within(N):
                        xt(s.at(2))

                steps(act, body)
                x2t(Step(N - 1, (N - 1) % U, (N - 1) // U, U))

            @block.vector
            def _(dve):
                v = nc.vector

                def gate(s):
                    if s.after(2):
                        hold(dve, g, h_turned, s.tile - 1)
                    hold(dve, g, silu_done, s.tile + 1)
                    v.tensor_tensor(h[:, s.buf % 2, :], ps_u[:, s.buf % 2, :], silu[:, s.buf % 2, :], ALU.mult).then_inc(h_done, 1)

                def norm_in(s):
                    b = s.buf % 2
                    hold(dve, g, y_done, s.tile + 1)
                    v.tensor_tensor(total[:, b, :], ps_y[:, b, :], rows[:, s.buf, :], ALU.add).then_inc(added, 1)
                    hold(dve, g, added, s.tile + 1)
                    v.bn_stats(stats[:], total[:, b, :]).then_inc(stats_done, 1)
                    hold(dve, g, stats_done, s.tile + 1)
                    v.bn_aggr(mean_var[:, b, :], stats[:]).then_inc(averaged, 1)

                def norm_out(s):
                    b = s.buf % 2
                    if s.after(U):
                        hold(dve, g, stored[s.buf], s.lap * 16)
                        hold(dve, g, x2_turned, s.tile - (U - 1))
                    hold(dve, g, rstd_done, s.tile + 1)
                    v.tensor_scalar(x2[:, s.buf, :], total[:, b, :], mean_var[:, b, 0:1], rstd[:, b:b + 1],
                                    ALU.subtract, ALU.mult).then_inc(x2_done, 1)

                def top(s):
                    hold(dve, g, logits_done, s.tile + 1)
                    if s.after(1):
                        hold(dve, g, top_kept, s.tile)
                    v.tensor_copy(logits[:], ps_l[:, 0, 0:EXPERTS]).then_inc(logits_copied, 1)
                    hold(dve, g, logits_copied, s.tile + 1)
                    v.max(largest[:], logits[:]).then_inc(top_found, 1)
                    hold(dve, g, top_found, s.tile + 1)
                    v.max_index(largest_at[:], largest[:], logits[:]).then_inc(top_indexed, 1)
                    v.tensor_copy(g.top_logits[:, bass.ds(s.tile, 1), :].rearrange("p a k -> p (a k)"), largest[:])
                    hold(dve, g, top_indexed, s.tile + 1)
                    v.tensor_scalar(expert_no[:], largest_at[:, 0:TOP_K], absent[:, bass.ds(s.tile, 1)], None, ALU.add).then_inc(numbered, 1)
                    hold(dve, g, numbered, s.tile + 1)
                    v.tensor_tensor(chosen[:], g.count_p[:, 0:EXPERTS].unsqueeze(1).to_broadcast([P, TOP_K, EXPERTS]),
                                    expert_no[:].unsqueeze(2).to_broadcast([P, TOP_K, EXPERTS]), ALU.is_equal).then_inc(compared, 1)
                    hold(dve, g, compared, s.tile + 1)
                    v.tensor_reduce(member[:], chosen[:].rearrange("p k e -> p e k"), AX.X, ALU.add).then_inc(counted, 1)
                    v.tensor_copy(g.chosen[:, bass.ds(s.tile, 1)].rearrange("p a k e -> p (a k e)"), chosen[:].rearrange("p k e -> p (k e)"))
                    hold(dve, g, counted, s.tile + 1)
                    v.tensor_copy(g.member[:, :, bass.ds(s.tile, 1)].rearrange("p e a -> p (e a)"), member[:]).then_inc(top_kept, 1)

                v.tensor_scalar(absent[:], g.slot_full[:], -1.0, -1000.0, ALU.add, ALU.mult).then_inc(absent_set, 1)
                dve.wait_ge(absent_set, 1)
                first = Step(0, 0, 0, U)
                gate(first)

                def body(s):
                    if s.at(1).within(N):
                        gate(s.at(1))
                    norm_in(s)
                    if s.after(1):
                        top(s.at(-1))
                    norm_out(s)

                steps(dve, body)
                top(Step(N - 1, (N - 1) % U, (N - 1) // U, U))

            @block.tensor
            def _(pe):
                def turn(source, target, done):
                    for c in range(DC):
                        last = pe.transpose(target[:, 0, c * P:(c + 1) * P], source[:, c * P:(c + 1) * P], g.ident[:])
                    last.then_inc(done, 1)

                def turn_x(s):
                    hold(pe, g, rows_in[s.buf], (s.lap + 1) * 16)
                    if s.after(1):
                        hold(pe, g, xt_copied, s.tile)
                    turn(rows[:, s.buf, :], ps_x, x_turned)

                def times_context(s, source, bank_of, done):
                    expert = pe.value_load(g.hash_of_tile[0:1, bass.ds(s.tile, 1)], min_val=0, max_val=HASHES - 1)
                    for c in range(DC):
                        last = pe.matmul(bank_of[:, s.buf % 2, :], source[:, c, :],
                                         g.ctx_t[:, bass.ds(expert, 1), c, :].rearrange("p a n -> p (a n)"),
                                         start=(c == 0), stop=(c == DC - 1))
                    last.then_inc(done, 1)

                def mm_u(s):
                    if s.after(2):
                        hold(pe, g, h_done, s.tile - 1)
                    hold(pe, g, xt_copied, s.tile + 1)
                    times_context(s, x_t[:, s.buf % 2], ps_u, u_done)

                def turn_h(s):
                    hold(pe, g, h_done, s.tile + 1)
                    if s.after(1):
                        hold(pe, g, ht_copied, s.tile)
                    turn(h[:, s.buf % 2, :], ps_h, h_turned)

                def mm_y(s):
                    if s.after(2):
                        hold(pe, g, added, s.tile - 1)
                    hold(pe, g, ht_copied, s.tile + 1)
                    times_context(s, h_t[:], ps_y, y_done)

                def turn_x2(s):
                    hold(pe, g, x2_done, s.tile + 1)
                    if s.after(1):
                        hold(pe, g, x2t_copied, s.tile)
                    turn(x2[:, s.buf, :], ps_x2, x2_turned)

                def route(s):
                    if s.after(1):
                        hold(pe, g, logits_copied, s.tile)
                    hold(pe, g, x2t_copied, s.tile + 1)
                    for c in range(DC):
                        last = pe.matmul(ps_l[:, 0, 0:EXPERTS], x2_t[:, c, :], g.gate[:, c, :], start=(c == 0), stop=(c == DC - 1))
                    last.then_inc(logits_done, 1)

                first = Step(0, 0, 0, U)
                turn_x(first)
                mm_u(first)
                turn_x(first.at(1))

                def body(s):
                    turn_h(s)
                    if s.at(1).within(N):
                        mm_u(s.at(1))
                    if s.after(1):
                        turn_x2(s.at(-1))
                    if s.at(2).within(N):
                        turn_x(s.at(2))
                    mm_y(s)
                    if s.after(1):
                        route(s.at(-1))

                steps(pe, body)
                turn_x2(Step(N - 1, (N - 1) % U, (N - 1) // U, U))
                route(Step(N - 1, (N - 1) % U, (N - 1) // U, U))


def stage_attention(nc, g):
    HEADS = EMB // HD
    EC, QT = EMB // P, T // P
    HG = P // HD
    QUADS = HEADS // 4
    COPIES = 4
    STACKED = COPIES * HD
    VW = 32
    MASKED = -1e30
    SCALE = HD ** -0.5

    with ExitStack() as ctx:
        def sb(name, shape, dt=F32):
            return ctx.enter_context(nc.sbuf_tensor(f"attn_{name}", shape, dt))

        def sem(name):
            return ctx.enter_context(nc.semaphore(f"attn_{name}"))

        def bank(name, n=1):
            return ctx.enter_context(nc.psum_tensor(f"attn_{name}", [P, n, 512], F32))

        N, U = B * QUADS, QUADS
        w_t, x_in = g.w_t, g.x_in
        x_t = sb("x_t", [P, EC, T])
        hi = sb("hi", [P, 2, T], F32R)
        lo = sb("lo", [P, 2, T], F32R)
        qs = sb("qs", [P, 2, HG, T], F32R)
        ks = sb("ks", [P, 2, HG, T], F32R)
        v_one = sb("v_one", [P, 2, QT, HG, VW])
        maxima = sb("maxima", [P, 2, QT, 4])
        neg_max = sb("neg_max", [P, QT, 2, 4], F32R)
        neg_max_t = sb("neg_max_t", [P, T], F32R)
        of_head = sb("of_head", [P, 4, P], F32R)
        head_rows = sb("head_rows", [P, 4])
        exps = sb("exps", [P, 2, 4, T])
        o_t = sb("o_t", [P, T])
        sums_inv = sb("sums_inv", [P, QT, 4])
        o_norm = sb("o_norm", [P, QT, 4, HD])
        res = sb("res", [P, QT, D])
        stats = sb("stats", [P, QT, 6])
        mean_var = sb("mean_var", [P, QT, 2])
        var_eps = sb("var_eps", [P, QT])
        rstd = sb("rstd", [P, QT])
        x1 = sb("x1", [P, QT, D])
        one_f = sb("one_f", [P, 512])
        ident_b = sb("ident_b", [P, P], BF16)
        later_key = sb("later_key", [P, P], BF16)
        earlier_query = sb("earlier_query", [P, P], BF16)
        mask_f = sb("mask_f", [P, 2, P])

        ps_s, ps_t, ps_o, ps_m = bank("ps_s", 2), bank("ps_t", 4), bank("ps_o"), bank("ps_m")

        x_arrived, res_in = sem("x_arrived"), sem("res_in")
        split_out, cleared, masks_made, constants, rows_set = sem("split_out"), sem("cleared"), sem("masks_made"), sem("constants"), sem("rows_set")
        xt_turned, xt_copied = sem("xt_turned"), sem("xt_copied")
        projected, hi_done, lo_done, v_projected, v_copied = sem("projected"), sem("hi_done"), sem("lo_done"), sem("v_projected"), sem("v_copied")
        q_stacked, k_stacked = [sem(f"q_stacked{i}") for i in range(2)], [sem(f"k_stacked{i}") for i in range(2)]
        s_done, max_done, max_hi, max_lo = sem("s_done"), sem("max_done"), sem("max_hi"), sem("max_lo")
        max_turned, max_copied = sem("max_turned"), sem("max_copied")
        t_done, exp_done, pv_done, o_copied = sem("t_done"), sem("exp_done"), sem("pv_done"), sem("o_copied")
        o_turned, inv_done, o_normed, res_added = sem("o_turned"), sem("inv_done"), sem("o_normed"), sem("res_added")
        stats_done, averaged, eps_added, rstd_done, x1_done, stored = (
            sem("stats_done"), sem("averaged"), sem("eps_added"), sem("rstd_done"), sem("x1_done"), sem("stored"))

        def steps(eng, body):
            run_steps(eng, N, U, U, U, body)

        def group(s):
            return s.lap * 2 + s.buf // 2

        def leads_group(s):
            return s.buf % 2 == 0 and s.at(2).within(N)

        def turns_x(s):
            return s.buf == 1 and s.at(QUADS - 1).within(N)

        PER_S, PER_T = 4 * QT, 2 * QT
        Q, K, V = 0, 1, 2
        X = (0, 1)
        HEADS_TURNED, MAX_TURNED = 4, 7
        LAST_V = 1
        LEAD = [3, 3, 2, 2, 2, 2, 2, 0]

        with nc.Block() as block:
            @block.sync
            def _(sp):
                def load_x(b):
                    hold(sp, g, xt_turned, b * EC)
                    sp.dma_start(x_in[:], g.x_dram[bass.ds(b, 1), :, 0:EMB].rearrange("a (c p) e -> p (a c) e", p=P)).then_inc(x_arrived, 16)

                def load_res(b):
                    if not (isinstance(b, int) and b == 0):
                        hold(sp, g, x1_done, b * QT)
                    sp.dma_start(res[:], g.x_dram[bass.ds(b, 1), :, :].rearrange("a (c p) e -> p (a c) e", p=P)).then_inc(res_in, 16)

                def stack(n, half):
                    if not (isinstance(n, int) and n < 2):
                        hold(sp, g, t_done, (n - 1) * 2 * PER_T)
                    else:
                        sp.wait_ge(rows_set, 2)
                    hold(sp, g, hi_done, n * 2 + 2)
                    hold(sp, g, lo_done, n * 2 + 2)
                    for p, part in enumerate((hi, lo)):
                        sp.dma_start(g.split_rows[half, p].rearrange("w r t -> r w t"), part[:].bitcast(F32)).then_inc(split_out, 16)
                    hold(sp, g, split_out, n * 32 + 32)
                    for which, stacked, done in ((0, qs, q_stacked), (1, ks, k_stacked)):
                        for r in range(COPIES):
                            p = (r // 2, r % 2)[which]
                            sp.dma_start(stacked[r * HD:(r + 1) * HD, half, :, :].bitcast(F32),
                                         g.split_rows[half, p, which].rearrange("(h d) t -> d h t", d=HD)).then_inc(done[half], 16)

                def store(b):
                    hold(sp, g, x1_done, b * QT + QT)
                    sp.dma_start(g.x1_rows[bass.ds(b * T, T), :].rearrange("(c p) d -> p c d", p=P), x1[:]).then_inc(stored, 16)

                load_res(0)
                stack(0, 0)

                def body(s):
                    if s.buf == 0 and s.at(U).within(N):
                        load_x(s.lap + 1)
                    if leads_group(s):
                        stack(group(s) + 1, 1 - s.buf // 2)
                    if s.buf == 1 and s.after(U):
                        store(s.lap - 1)
                        load_res(s.lap)

                steps(sp, body)
                store(B - 1)
                sp.wait_ge(stored, 16 * B)

            @block.gpsimd
            def _(pool):
                m = nc.gpsimd
                m.memset(mask_f[:], 0.0).then_inc(cleared, 1)
                m.memset(one_f[:], 1.0).then_inc(cleared, 1)
                m.memset(v_one[:], 0.0).then_inc(cleared, 1)
                pool.wait_ge(cleared, 3)
                m.affine_select(out=mask_f[:, 0, :], in_=mask_f[:, 0, :], compare_op=ALU.is_ge, fill=MASKED, base=0,
                                pattern=[[-1, P]], channel_multiplier=1).then_inc(masks_made, 1)
                m.affine_select(out=mask_f[:, 1, :], in_=mask_f[:, 1, :], compare_op=ALU.is_ge, fill=MASKED, base=0,
                                pattern=[[1, P]], channel_multiplier=-1).then_inc(masks_made, 1)
                m.memset(v_one[:].rearrange("p a c h w -> p (a c h) w")[:, :, HD:HD + 1], 1.0).then_inc(cleared, 1)
                pool.wait_ge(masks_made, 2)
                m.tensor_copy(later_key[:], mask_f[:, 0, :]).then_inc(constants, 1)
                m.tensor_copy(earlier_query[:], mask_f[:, 1, :]).then_inc(constants, 1)
                m.tensor_copy(ident_b[:], g.ident[:]).then_inc(constants, 1)
                pool.wait_ge(cleared, 4)
                pool.sem_inc(constants, 1)

                def add_attention(s):
                    q = s.buf
                    hold(pool, g, o_normed, s.tile + 1)
                    if q == 0:
                        hold(pool, g, res_in, (s.lap + 1) * 16)
                    part = res[:, :, q * 4 * HD:(q + 1) * 4 * HD]
                    m.tensor_tensor(part, part, o_norm[:].rearrange("p c h d -> p c (h d)"), ALU.add).then_inc(res_added, 1)

                def rstd_of(b):
                    hold(pool, g, averaged, b * QT + QT)
                    if not (isinstance(b, int) and b == 0):
                        hold(pool, g, x1_done, b * QT)
                    m.tensor_scalar(var_eps[:], mean_var[:, :, 1], EPS, None, ALU.add).then_inc(eps_added, 1)
                    hold(pool, g, eps_added, b + 1)
                    m.tensor_tensor(rstd[:], var_eps[:], g.minus_half[:].to_broadcast([P, QT]), ALU.pow).then_inc(rstd_done, 1)

                def scale_rows(b):
                    if not (isinstance(b, int) and b == 0):
                        hold(pool, g, stored, b * 16)
                    hold(pool, g, rstd_done, b + 1)
                    for c in range(QT):
                        m.tensor_scalar(x1[:, c, :], res[:, c, :], mean_var[:, c, 0:1], rstd[:, c:c + 1],
                                        ALU.subtract, ALU.mult).then_inc(x1_done, 1)

                def body(s):
                    if s.after(1):
                        add_attention(s.at(-1))
                        if s.buf == 0:
                            rstd_of(s.lap - 1)
                            scale_rows(s.lap - 1)

                steps(pool, body)
                add_attention(Step(N - 1, U - 1, B - 1, U))
                rstd_of(B - 1)
                scale_rows(B - 1)

            @block.scalar
            def _(act):
                a = nc.scalar

                def project(n, half, which):
                    if which == V:
                        if not (isinstance(n, int) and n < 2):
                            hold(act, g, pv_done, (n - 1) * 2 * QT)
                        hold(act, g, v_projected, n + 1)
                        a.copy(v_one[:, half, :, :, 0:HD], ps_m[:, 0, :].rearrange("p (c h d) -> p c h d", c=QT, d=HD)).then_inc(v_copied, 1)
                        return
                    if not (isinstance(n, int) and n == 0):
                        hold(act, g, split_out, n * 32)
                    hold(act, g, projected, n * 2 + which + 1)
                    a.activation(hi[:, which, :], ps_m[:, 0, :], ACT.Copy, scale=SCALE if which == Q else 1.0).then_inc(hi_done, 1)

                def turn_x(b, c):
                    if not (isinstance(b, int) and b == 0):
                        hold(act, g, v_projected, b * 2)
                    hold(act, g, xt_turned, b * EC + c + 1)
                    a.copy(x_t[:, c, :], ps_m[:, 0, :]).then_inc(xt_copied, 1)

                def copy_max(s):
                    if s.after(1):
                        hold(act, g, t_done, s.tile * PER_T)
                    else:
                        act.wait_ge(rows_set, 3)
                    hold(act, g, max_turned, s.tile + 1)
                    a.copy(neg_max_t[0:8, :], ps_m[0:8, 0, :]).then_inc(max_copied, 1)

                def copy_heads(s):
                    if s.after(1):
                        hold(act, g, o_turned, s.tile)
                    hold(act, g, pv_done, s.tile * QT + QT)
                    a.copy(o_t[:], ps_o[:, 0, :]).then_inc(o_copied, 1)

                def exponentials(s, j):
                    i, pair = j // 2, j % 2
                    w = T - i * P
                    if not (isinstance(s.tile, int) and s.tile == 0 and i < 2):
                        hold(act, g, pv_done, s.tile * QT + i - 1)
                    hold(act, g, t_done, s.tile * PER_T + j + 1)
                    a.activation(exps[:, i % 2, 2 * pair:2 * pair + 2, 0:w], ps_t[:, 2 * pair:2 * pair + 2, 0:w],
                                 ACT.Exp).then_inc(exp_done, 1)

                for c in range(EC):
                    turn_x(0, c)
                for which in (Q, K, V):
                    project(0, 0, which)
                copy_max(Step(0, 0, 0, U))

                def body(s):
                    for j in range(PER_T):
                        if leads_group(s) and j in (Q, K, V):
                            project(group(s) + 1, 1 - s.buf // 2, j)
                        if turns_x(s) and j in X:
                            turn_x(s.lap + 1, X.index(j))
                        if j == LAST_V + 1 and s.after(1):
                            copy_heads(s.at(-1))
                        exponentials(s, j)
                        if j == MAX_TURNED and s.at(1).within(N):
                            copy_max(s.at(1))

                steps(act, body)
                copy_heads(Step(N - 1, U - 1, B - 1, U))

            @block.vector
            def _(dve):
                v = nc.vector
                dve.wait_ge(cleared, 4)
                for rows in (qs, ks):
                    v.tensor_scalar(rows[STACKED:P].rearrange("p a h t -> p (a h t)"),
                                    one_f[STACKED:P, 0:1].to_broadcast([P - STACKED, 2 * HG * T]), 0.0, None,
                                    ALU.mult).then_inc(rows_set, 1)
                v.tensor_scalar(neg_max_t[:], one_f[:, 0:T], 0.0, None, ALU.mult).then_inc(rows_set, 1)
                v.tensor_tensor(head_rows[:], g.ident[:, 0:4], g.ident[:, 4:8], ALU.add).then_inc(rows_set, 1)
                dve.wait_ge(rows_set, 4)
                v.tensor_copy(of_head[:], head_rows[:].unsqueeze(2).to_broadcast([P, 4, P])).then_inc(rows_set, 1)

                def split(n, which):
                    hold(dve, g, hi_done, n * 2 + which + 1)
                    v.scalar_tensor_tensor(out=lo[:, which, :], in0=ps_m[:, 0, :], scalar=SCALE if which == Q else 1.0,
                                           in1=hi[:, which, :].bitcast(F32), op0=ALU.mult, op1=ALU.subtract).then_inc(lo_done, 1)

                def find_max(s, unit):
                    h, i = unit // QT, unit % QT
                    hold(dve, g, s_done, s.tile * PER_S + unit + 1)
                    v.tensor_reduce(maxima[:, s.buf % 2, i, h:h + 1], ps_s[:, unit % 2, 0:(i + 1) * P], AX.X,
                                    ALU.max).then_inc(max_done, 1)

                def split_max(s):
                    b = s.buf % 2
                    if s.after(1):
                        hold(dve, g, max_turned, s.tile)
                    hold(dve, g, max_done, (s.tile + 1) * PER_S)
                    v.tensor_scalar(neg_max[:, :, 0, :], maxima[:, b], -1.0, None, ALU.mult).then_inc(max_hi, 1)
                    hold(dve, g, max_hi, s.tile + 1)
                    v.scalar_tensor_tensor(out=neg_max[:, :, 1, :], in0=maxima[:, b], scalar=-1.0,
                                           in1=neg_max[:, :, 0, :].bitcast(F32), op0=ALU.mult, op1=ALU.subtract).then_inc(max_lo, 1)

                def norm_heads(s):
                    turned = ps_m[:, 0, :].rearrange("p (c h w) -> p c h w", c=QT, w=VW)
                    if s.after(1):
                        hold(dve, g, res_added, s.tile)
                    hold(dve, g, o_turned, s.tile + 1)
                    v.reciprocal(sums_inv[:], turned[:, :, :, HD]).then_inc(inv_done, 1)
                    hold(dve, g, inv_done, s.tile + 1)
                    v.tensor_tensor(o_norm[:].rearrange("p c h d -> p (c h) d"),
                                    turned[:, :, :, 0:HD].rearrange("p c h d -> p (c h) d"),
                                    sums_inv[:].rearrange("p c h -> p (c h)").unsqueeze(2).to_broadcast([P, QT * 4, HD]),
                                    ALU.mult).then_inc(o_normed, 1)

                def norm_rows(b):
                    hold(dve, g, res_added, b * QUADS + QUADS)
                    for c in range(QT):
                        v.bn_stats(stats[:, c, :], res[:, c, :]).then_inc(stats_done, 1)
                    for c in range(QT):
                        hold(dve, g, stats_done, b * QT + c + 1)
                        v.bn_aggr(mean_var[:, c, :], stats[:, c, :]).then_inc(averaged, 1)

                for which in (Q, K):
                    split(0, which)
                for unit in range(PER_S):
                    find_max(Step(0, 0, 0, U), unit)
                split_max(Step(0, 0, 0, U))

                def body(s):
                    for j in range(PER_T):
                        if j == HEADS_TURNED + 1 and s.after(1):
                            norm_heads(s.at(-1))
                        for n in range(max(LEAD[j], 1)):
                            if n < LEAD[j] and s.at(1).within(N):
                                find_max(s.at(1), sum(LEAD[:j]) + n)
                            if n == 0 and leads_group(s) and j in (Q, K):
                                split(group(s) + 1, j)
                    if s.at(1).within(N):
                        split_max(s.at(1))
                    if s.after(1) and s.buf == 0:
                        norm_rows(s.lap - 1)

                steps(dve, body)
                norm_heads(Step(N - 1, U - 1, B - 1, U))
                norm_rows(B - 1)

            @block.tensor
            def _(pe):
                pe.wait_ge(constants, 4)

                def turn_x(b, c):
                    if c:
                        hold(pe, g, xt_copied, b * EC + c)
                    elif not (isinstance(b, int) and b == 0):
                        hold(pe, g, x_arrived, b * 16)
                    for t in range(QT):
                        last = pe.transpose(ps_m[:, 0, t * P:(t + 1) * P], x_in[:, t, c * P:(c + 1) * P], g.ident[:])
                    last.then_inc(xt_turned, 1)

                def project(n, half, which):
                    if which == Q:
                        if half == 0:
                            hold(pe, g, xt_copied, n * EC // 2 + EC)
                    else:
                        hold(pe, g, hi_done, n * 2 + which)
                        hold(pe, g, lo_done, n * 2 + which)
                    if which != V:
                        for c in range(EC):
                            last = pe.matmul(ps_m[:, 0, :], w_t[:, c, which, half * P:(half + 1) * P], x_t[:, c, :],
                                             start=(c == 0), stop=(c == EC - 1))
                        last.then_inc(projected, 1)
                    else:
                        for t in range(QT):
                            for c in range(EC):
                                last = pe.matmul(ps_m[:, 0, t * P:(t + 1) * P], x_t[:, c, t * P:(t + 1) * P],
                                                 w_t[:, c, 2, half * P:(half + 1) * P], start=(c == 0), stop=(c == EC - 1))
                        last.then_inc(v_projected, 1)

                def first_pass(s, unit):
                    h, i = unit // QT, unit % QT
                    half, head, w = s.buf // 2, (s.buf % 2) * 4 + h, (i + 1) * P
                    out = ps_s[:, unit % 2, 0:w]
                    if unit == 0 and s.buf % 2 == 0:
                        hold(pe, g, q_stacked[half], (s.lap + 1) * COPIES * 16)
                        hold(pe, g, k_stacked[half], (s.lap + 1) * COPIES * 16)
                    if s.after(1) or unit >= 2:
                        hold(pe, g, max_done, s.tile * PER_S + unit - 1)
                    pe.matmul(out, qs[:, half, head, i * P:(i + 1) * P], ks[:, half, head, 0:w], start=True, stop=False)
                    pe.matmul(out[:, i * P:w], ident_b[:], later_key[:], start=False, stop=True).then_inc(s_done, 1)

                def turn_max(s):
                    hold(pe, g, max_lo, s.tile + 1)
                    for i in range(QT):
                        last = pe.transpose(ps_m[0:8, 0, i * P:(i + 1) * P],
                                            neg_max[:, i].rearrange("p a h -> p (a h)").bitcast(F32), g.ident[:])
                    last.then_inc(max_turned, 1)

                def second_pass(s, i, pair, k):
                    half, w = s.buf // 2, T - i * P
                    unit = 2 * i + pair
                    if k == 0 and (s.after(1) or unit >= 2):
                        hold(pe, g, exp_done, s.tile * PER_T + unit - 1)
                    head = (s.buf % 2) * 4 + 2 * pair + k
                    out = ps_t[:, 2 * pair + k, 0:w]
                    pe.matmul(out, ks[:, half, head, i * P:(i + 1) * P], qs[:, half, head, i * P:T], start=True, stop=False)
                    pe.matmul(out[:, 0:P], ident_b[:], earlier_query[:], start=False, stop=False)
                    if unit == 0 and k == 0:
                        hold(pe, g, max_copied, s.tile + 1)
                        if not s.after(1):
                            pe.wait_ge(rows_set, 5)
                    last = pe.matmul(out, of_head[:, 2 * pair + k, :], neg_max_t[:, i * P:T], start=False, stop=True)
                    if k == 1:
                        last.then_inc(t_done, 1)

                def times_v(s, i):
                    half = s.buf // 2
                    if i == 0:
                        if s.buf % 2 == 0:
                            hold(pe, g, v_copied, group(s) + 1)
                        if s.after(1):
                            hold(pe, g, o_copied, s.tile)
                    hold(pe, g, exp_done, s.tile * PER_T + 2 * i + 2)
                    for h in range(4):
                        last = pe.matmul(ps_o[VW * h:VW * (h + 1), 0, i * P:T], v_one[:, half, i, (s.buf % 2) * 4 + h, :],
                                         exps[:, i % 2, h, 0:T - i * P], start=(i == 0), stop=(i == QT - 1), tile_position=(0, VW * h))
                    last.then_inc(pv_done, 1)

                def turn_heads(s):
                    hold(pe, g, o_copied, s.tile + 1)
                    n = s.at(1)
                    if leads_group(n):
                        hold(pe, g, v_copied, group(n) + 2)
                    elif turns_x(n):
                        hold(pe, g, xt_copied, n.lap * EC + 2 * EC)
                    elif n.within(N):
                        hold(pe, g, max_copied, n.tile + 1)
                    for i in range(QT):
                        last = pe.transpose(ps_m[:, 0, i * P:(i + 1) * P], o_t[:, i * P:(i + 1) * P], g.ident[:])
                    last.then_inc(o_turned, 1)

                for c in range(EC):
                    turn_x(0, c)
                for which in (Q, K, V):
                    project(0, 0, which)
                first = Step(0, 0, 0, U)
                for unit in range(PER_S):
                    first_pass(first, unit)
                pe.wait_ge(v_copied, 1)
                turn_max(first)

                def lead(s, j, n):
                    if n < LEAD[j] and s.at(1).within(N):
                        first_pass(s.at(1), sum(LEAD[:j]) + n)

                def body(s):
                    for j in range(PER_T):
                        if j in (Q, X[0]) and (leads_group(s) or turns_x(s)):
                            hold(pe, g, max_copied, s.tile + 1)
                        if leads_group(s) and j in (Q, K, V):
                            project(group(s) + 1, 1 - s.buf // 2, j)
                        if turns_x(s) and j in X:
                            turn_x(s.lap + 1, X.index(j))
                        if j == HEADS_TURNED and s.after(1):
                            turn_heads(s.at(-1))
                        lead(s, j, 0)
                        second_pass(s, j // 2, j % 2, 0)
                        lead(s, j, 1)
                        second_pass(s, j // 2, j % 2, 1)
                        lead(s, j, 2)
                        if j == MAX_TURNED and s.at(1).within(N):
                            if s.after(1):
                                hold(pe, g, o_normed, s.tile)
                            elif leads_group(s):
                                hold(pe, g, v_copied, group(s) + 2)
                            turn_max(s.at(1))
                        if j == LAST_V and s.after(1):
                            times_v(s.at(-1), QT - 1)
                        if j % 2 and j >= 3:
                            times_v(s, j // 2 - 1)

                steps(pe, body)
                final = Step(N - 1, U - 1, B - 1, U)
                times_v(final, QT - 1)
                pe.wait_ge(o_normed, N - 1)
                turn_heads(final)


def load_expert(sp, g, s):
    t = bass.ds(s.tile, 1)
    expert = sp.value_load(g.plan[0:1, 0, t], min_val=0, max_val=EXPERTS - 1)
    is_new = sp.value_load(g.plan[0:1, 1, t], min_val=0, max_val=1)
    slot = sp.value_load(g.plan[0:1, 2, t], min_val=0, max_val=WEIGHT_SLOTS - 1)
    e, b = bass.ds(expert, 1), bass.ds(slot, 1)
    sp.dma_start(g.up_w[:, b, :].rearrange("p a (c f) -> p (a c) f", c=DC),
                 g.up_dram[e, :, :].rearrange("a (c p) f -> p (a c) f", p=P),
                 cond=is_new).then_inc(g.weights_in[s.buf], 16)
    sp.dma_start(g.down_w[:, b, :].rearrange("p a (c n) -> p (a c) n", c=IC),
                 g.down_dram[e, :, :].rearrange("a (c p) n -> p (a c) n", p=IW),
                 cond=is_new).then_inc(g.weights_in[s.buf], 16)


def stage_dispatch(nc, g):
    J, K, E = SORT_TILES, TOP_K, EXPERTS
    U = 4
    with ExitStack() as ctx:
        def sb(name, shape, dt=F32):
            return ctx.enter_context(nc.sbuf_tensor(f"dispatch_{name}", shape, dt))

        def sem(name):
            return ctx.enter_context(nc.semaphore(f"dispatch_{name}"))

        top = g.top_logits[:, :, 0:K]
        shifted = sb("shifted", [P, J, K])
        powers = sb("powers", [P, J, K])
        weight = sb("weight", [P, J, K])
        weight_sum = sb("weight_sum", [P, J])
        w = sort_buffers(sb, "moe", E, J)
        picked = sb("picked", [P, J, K, E])
        pair_slot = sb("pair_slot", [P, J, K])
        tile_of = sb("tile_of", [P, J, K])
        place_of = sb("place_of", [P, J, K])
        tmp_i = sb("tmp_i", [P, J * K], I32)
        hidden = sb("hidden", [P, J])
        at_place = sb("at_place", [P, U, K, P])
        at_tile = sb("at_tile", [P, U, K, PAIR_TILES])
        at_tile_row = sb("at_tile_row", [P, U, K, 2, PAIR_TILES])
        pair_up = sb("pair_up", [P, J, K])
        row_up = sb("row_up", [P, PAIR_TILES])
        empty = sb("empty", [P, PAIR_TILES])
        row_of = sb("row_of", [P, PAIR_TILES])
        pair_i = sb("pair_i", [P, PAIR_TILES], I32)
        end_of = sb("end_of", [E, 1])
        ended = sb("ended", [E, PLAN])
        expert_of = sb("expert_of", [1, PLAN])
        ones_t = sb("ones_t", [1, PLAN])
        changed = sb("changed", [1, PLAN])
        changes = sb("changes", [1, PLAN])
        changes_i = sb("changes_i", [1, PLAN], I32)
        half = E // 2
        ps_rank = ctx.enter_context(nc.psum_tensor("ps_rank", [P, 2, 512], F32))
        ps_sum = ctx.enter_context(nc.psum_tensor("ps_sum", [P, 2, 512], F32))
        ps_table = ctx.enter_context(nc.psum_tensor("ps_table", [P, 512], F32))
        ps_ends = ctx.enter_context(nc.psum_tensor("ps_ends", [P, 512], F32))
        ps_plan = ctx.enter_context(nc.psum_tensor("ps_plan", [P, 512], F32))

        v_chain = sem("v_chain")
        shift_ready, exp_ready, summed, ranked = sem("shift_ready"), sem("exp_ready"), sem("summed"), sem("ranked")
        ends_known, ends_turned, ends_compared, ends_counted = sem("ends_known"), sem("ends_turned"), sem("ends_compared"), sem("ends_counted")
        plan_made, tiles_at, places_at = sem("plan_made"), sem("tiles_at"), sem("places_at")
        numbers_at, weights_at = sem("numbers_at"), sem("weights_at")
        table_used, tabled = sem("table_used"), sem("tabled")

        with nc.Block() as block:
            @block.sync
            def _(sp):
                sp.wait_ge(plan_made, 1)
                for t in range(WEIGHT_SLOTS):
                    load_expert(sp, g, Step(t, t, 0, WEIGHT_SLOTS))

            @block.gpsimd
            def _(pool):
                def number_tiles(s):
                    if s.after(U):
                        hold(pool, g, table_used, s.tile - (U - 1))
                    hold(pool, g, tiles_at, s.tile + 1)
                    number = pair_up[:, bass.ds(s.tile, 1), :].rearrange("p a k -> p (a k)")
                    nc.gpsimd.tensor_tensor(at_tile_row[:, s.buf, :, 0, :], at_tile[:, s.buf],
                                            number.unsqueeze(2).to_broadcast([P, K, PAIR_TILES]), ALU.mult).then_inc(numbers_at, 1)

                run_steps(pool, J, U, U, 1, number_tiles)

            @block.scalar
            def _(act):
                act.wait_ge(shift_ready, 1)
                nc.scalar.activation(powers[:], shifted[:], ACT.Exp).then_inc(exp_ready, 1)

                def weigh_tiles(s):
                    if s.after(U):
                        hold(act, g, table_used, s.tile - (U - 1))
                    hold(act, g, tiles_at, s.tile + 1)
                    for k in range(K):
                        last = nc.scalar.activation(at_tile_row[:, s.buf, k, 1, :], at_tile[:, s.buf, k, :], ACT.Copy,
                                                    scale=weight[:, bass.ds(s.tile, 1), k:k + 1].rearrange("p a k -> p (a k)"))
                    last.then_inc(weights_at, 1)

                run_steps(act, J, U, U, 1, weigh_tiles)

            @block.vector
            def _(dve):
                v = nc.vector
                link = sequence(dve, v_chain)
                v.tensor_tensor(shifted[:], top, top[:, :, 0:1].to_broadcast([P, J, K]), ALU.subtract).then_inc(shift_ready, 1)
                link(v.tensor_tensor(pair_up[:], g.pair_offset[:].unsqueeze(1).to_broadcast([P, J, K]),
                                     g.slot_token_up[:].unsqueeze(2).to_broadcast([P, J, K]), ALU.add))
                dve.wait_ge(exp_ready, 1)
                link(v.tensor_reduce(weight_sum[:], powers[:], AX.X, ALU.add))
                link(v.reciprocal(weight_sum[:], weight_sum[:]))
                link(v.tensor_tensor(weight[:], powers[:], weight_sum[:].unsqueeze(2).to_broadcast([P, J, K]), ALU.mult))
                dve.wait_ge(summed, 1)
                dve.wait_ge(ranked, 1)
                halves = lambda ps: [(slice(i * half, (i + 1) * half),
                                      ps[:, i, 0:half * J].rearrange("p (g t) -> p g t", g=half)) for i in range(2)]
                slots_of_groups(nc, link, w, E, J, halves(ps_sum), halves(ps_rank))
                dve.sem_inc(ends_known, 1)
                link(v.tensor_tensor(picked[:], g.chosen[:],
                                     w.slot[:].rearrange("p e j -> p j e").unsqueeze(2).to_broadcast([P, J, K, E]), ALU.mult))
                dve.wait_ge(ends_turned, 1)
                link(v.tensor_copy(end_of[:], ps_ends[0:E, 0:1]))
                v.tensor_scalar(ended[:], g.count_t[0:E, :], end_of[:, 0:1], None, ALU.is_ge).then_inc(ends_compared, 1)
                link(v.tensor_reduce(pair_slot[:], picked[:], AX.X, ALU.add))
                flat = "p j k -> p (j k)"
                split_slot(nc, link, tile_of[:].rearrange(flat), place_of[:].rearrange(flat), tmp_i[:], pair_slot[:].rearrange(flat))
                link(v.tensor_scalar(hidden[:], g.slot_full[:], -1.0, 1000.0, ALU.add, ALU.mult))
                link(v.tensor_tensor(tile_of[:], tile_of[:], hidden[:].unsqueeze(2).to_broadcast([P, J, K]), ALU.add))

                dve.wait_ge(ends_counted, 1)
                link(v.tensor_scalar(expert_of[:], ps_plan[0:1, 0:PLAN], float(E - 1), None, ALU.min))
                link(v.memset(changed[:, 0:1], 1.0))
                link(v.memset(ones_t[:], 1.0))
                link(v.tensor_tensor(changed[:, 1:], expert_of[:, 1:], expert_of[:, 0:PLAN - 1], ALU.not_equal))
                link(v.tensor_tensor_scan(changes[:], ones_t[:], changed[:], -1.0, ALU.mult, ALU.add))
                link(v.tensor_copy(changes_i[:], changes[:]))
                link(v.tensor_scalar(g.plan[:, 2, :], changes_i[:], WEIGHT_SLOTS - 1, None, ALU.bitwise_and))
                link(v.tensor_copy(g.plan[:, 0, :], expert_of[:]))
                link(v.tensor_copy(g.plan[:, 1, :], changed[:]))
                dve.sem_inc(plan_made, 1)

                def place_pairs(s):
                    if s.after(U):
                        hold(dve, g, table_used, s.tile - (U - 1))
                        hold(dve, g, numbers_at, s.tile - (U - 1))
                        hold(dve, g, weights_at, s.tile - (U - 1))
                    of = lambda x: x[:, bass.ds(s.tile, 1), :].rearrange("p a k -> p (a k)")
                    v.tensor_tensor(at_tile[:, s.buf], g.count_t[:, 0:PAIR_TILES].unsqueeze(1).to_broadcast([P, K, PAIR_TILES]),
                                    of(tile_of).unsqueeze(2).to_broadcast([P, K, PAIR_TILES]), ALU.is_equal).then_inc(tiles_at, 1)
                    v.tensor_tensor(at_place[:, s.buf], g.count_p[:].unsqueeze(1).to_broadcast([P, K, P]),
                                    of(place_of).unsqueeze(2).to_broadcast([P, K, P]), ALU.is_equal).then_inc(places_at, 1)

                run_steps(dve, J, U, U, 1, place_pairs)
                dve.wait_ge(tabled, 1)
                link(v.tensor_copy(row_up[:], ps_table[:, 0:PAIR_TILES]))
                link(v.tensor_copy(g.pair_weight[:], ps_table[:, PAIR_TILES:2 * PAIR_TILES]))
                link(v.tensor_scalar(empty[:], row_up[:], 0.5, None, ALU.is_lt))
                link(v.tensor_scalar(pair_i[:], row_up[:], -1.0, 0.0, ALU.add, ALU.max))
                link(v.tensor_scalar(g.pair_token[:], pair_i[:], N_TOK - 1, None, ALU.bitwise_and))
                link(v.tensor_tensor(empty[:], empty[:], g.spare_pair_up[:], ALU.mult))
                link(v.tensor_tensor(row_of[:], row_up[:], empty[:], ALU.add))
                link(v.tensor_scalar(g.pair_row[:], row_of[:], -1.0, None, ALU.add))

            @block.tensor
            def _(pe):
                for ps, rows, done in ((ps_sum, g.ones, summed), (ps_rank, g.below, ranked)):
                    for i in range(2):
                        member = g.member[:, i * half:(i + 1) * half, :].rearrange("p g t -> p (g t)")
                        last = pe.matmul(ps[:, i, 0:half * J], rows[:], member, start=True, stop=True)
                    last.then_inc(done, 1)
                pe.wait_ge(ends_known, 1)
                pe.transpose(ps_ends[0:E, 0:P], w.tiles_end[:], g.ident[:]).then_inc(ends_turned, 1)
                pe.wait_ge(ends_compared, 1)
                pe.matmul(ps_plan[:, 0:PLAN], g.ones[0:E, :], ended[:], start=True, stop=True).then_inc(ends_counted, 1)

                def add_to_table(s):
                    hold(pe, g, places_at, s.tile + 1)
                    hold(pe, g, numbers_at, s.tile + 1)
                    hold(pe, g, weights_at, s.tile + 1)
                    for k in range(K):
                        first = isinstance(s.tile, int) and s.tile == 0 and k == 0
                        final = isinstance(s.tile, int) and s.tile == J - 1 and k == K - 1
                        last = pe.matmul(ps_table[:, 0:2 * PAIR_TILES], at_place[:, s.buf, k, :],
                                         at_tile_row[:, s.buf, k].rearrange("p a t -> p (a t)"), start=first, stop=final)
                    last.then_inc(table_used, 1)
                    if final:
                        pe.wait_ge(table_used, J)
                        pe.sem_inc(tabled, 1)

                run_steps(pe, J, U, U, 1, add_to_table)


def stage_experts(nc, g):
    with ExitStack() as ctx:
        def sb(name, shape, dt=F32):
            return ctx.enter_context(nc.sbuf_tensor(f"experts_{name}", shape, dt))

        def sem(name):
            return ctx.enter_context(nc.semaphore(f"experts_{name}"))

        def bank(name, n=1):
            return ctx.enter_context(nc.psum_tensor(f"experts_{name}", [P, n, 512], F32))

        N, U = PAIR_TILES, 4
        index = sb("index", [P, U], I32)
        out_index = sb("out_index", [P, U], I32)
        rows = sb("rows", [P, U, D])
        x_t = sb("x_t", [P, 2, DC, P])
        silu = sb("silu", [P, 2, INTER])
        h = sb("h", [P, 2, INTER])
        h_t = sb("h_t", [IW, IC, P])
        y = sb("y", [P, U, D])
        ps_x, ps_h, ps_gu, ps_y = bank("ps_x", 2), bank("ps_h", 2), bank("ps_gu", 2), bank("ps_y", 2)

        rows_in = [sem(f"rows_in{u}") for u in range(U)]
        stored = [sem(f"stored{u}") for u in range(U)]
        index_set, out_index_set = sem("index_set"), sem("out_index_set")
        x_turned, xt_copied, gu_done, silu_done = sem("x_turned"), sem("xt_copied"), sem("gu_done"), sem("silu_done")
        h_done, h_turned, ht_copied, y_done, y_scaled = sem("h_done"), sem("h_turned"), sem("ht_copied"), sem("y_done"), sem("y_scaled")

        def steps(eng, body):
            run_steps(eng, N, U, U, U, body)

        with nc.Block() as block:
            @block.sync
            def _(sp):
                def load(s):
                    if s.after(U):
                        hold(sp, g, y_done, s.tile - (U - 1))
                        load_expert(sp, g, s)

                steps(sp, load)

            @block.gpsimd
            def _(pool):
                def gather(s):
                    if s.after(U):
                        hold(pool, g, x_turned, s.tile - (U - 1))
                    nc.gpsimd.tensor_copy(index[:, s.buf:s.buf + 1], g.pair_token[:, bass.ds(s.tile, 1)]).then_inc(index_set, 1)
                    hold(pool, g, index_set, s.tile + 1)
                    nc.gpsimd.indirect_dma_start(
                        out=rows[:, s.buf, :], out_offset=None, in_=g.x2_rows[0:N_TOK, :],
                        in_offset=bass.IndirectOffsetOnAxis(ap=index[:, s.buf:s.buf + 1], axis=0),
                    ).then_inc(rows_in[s.buf], 16)

                def store(s):
                    if s.after(U):
                        hold(pool, g, stored[s.buf], s.lap * 16)
                    nc.gpsimd.tensor_copy(out_index[:, s.buf:s.buf + 1], g.pair_row[:, bass.ds(s.tile, 1)]).then_inc(out_index_set, 1)
                    hold(pool, g, out_index_set, s.tile + 1)
                    hold(pool, g, y_scaled, s.tile + 1)
                    nc.gpsimd.indirect_dma_start(
                        out=g.y_rows, out_offset=bass.IndirectOffsetOnAxis(ap=out_index[:, s.buf:s.buf + 1], axis=0),
                        in_=y[:, s.buf, :], in_offset=None,
                    ).then_inc(stored[s.buf], 16)

                for t in range(U):
                    gather(Step(t, t % U, t // U, U))

                def body(s):
                    if s.at(U).within(N):
                        gather(s.at(U))
                    store(s)

                steps(pool, body)
                for u in range(U):
                    pool.wait_ge(stored[u], 16 * len(range(u, N, U)))

            @block.scalar
            def _(act):
                def xt(s):
                    b = s.buf % 2
                    if s.after(2):
                        hold(act, g, gu_done, s.tile - 1)
                    hold(act, g, x_turned, s.tile + 1)
                    nc.scalar.copy(x_t[:, b].rearrange("p c t -> p (c t)"), ps_x[:, b, :]).then_inc(xt_copied, 1)

                def silu_of(s):
                    b = s.buf % 2
                    if s.after(2):
                        hold(act, g, h_done, s.tile - 1)
                    hold(act, g, gu_done, s.tile + 1)
                    nc.scalar.activation(silu[:, b, :], ps_gu[:, b, 0:INTER], ACT.Silu).then_inc(silu_done, 1)

                def ht(s):
                    if s.after(1):
                        hold(act, g, y_done, s.tile)
                    hold(act, g, h_turned, s.tile + 1)
                    nc.scalar.copy(h_t[:].rearrange("p c t -> p (c t)"), ps_h[0:IW, s.buf % 2, 0:IC * P]).then_inc(ht_copied, 1)

                first = Step(0, 0, 0, U)
                xt(first)
                silu_of(first)
                xt(first.at(1))

                def body(s):
                    ht(s)
                    if s.at(1).within(N):
                        silu_of(s.at(1))
                    if s.at(2).within(N):
                        xt(s.at(2))

                steps(act, body)

            @block.vector
            def _(dve):
                v = nc.vector

                def gate(s):
                    b = s.buf % 2
                    if s.after(2):
                        hold(dve, g, h_turned, s.tile - 1)
                    hold(dve, g, silu_done, s.tile + 1)
                    v.tensor_tensor(h[:, b, :], ps_gu[:, b, INTER:2 * INTER], silu[:, b, :], ALU.mult).then_inc(h_done, 1)

                def scale(s):
                    if s.after(U):
                        hold(dve, g, stored[s.buf], s.lap * 16)
                    hold(dve, g, y_done, s.tile + 1)
                    v.tensor_scalar(y[:, s.buf, :], ps_y[:, s.buf % 2, :], g.pair_weight[:, bass.ds(s.tile, 1)], None,
                                    ALU.mult).then_inc(y_scaled, 1)

                gate(Step(0, 0, 0, U))

                def body(s):
                    if s.at(1).within(N):
                        gate(s.at(1))
                    scale(s)

                steps(dve, body)

            @block.tensor
            def _(pe):
                def turn_x(s):
                    b = s.buf % 2
                    hold(pe, g, rows_in[s.buf], (s.lap + 1) * 16)
                    if s.after(2):
                        hold(pe, g, xt_copied, s.tile - 1)
                    for c in range(DC):
                        last = pe.transpose(ps_x[:, b, c * P:(c + 1) * P], rows[:, s.buf, c * P:(c + 1) * P], g.ident[:])
                    last.then_inc(x_turned, 1)

                def slot_of(s):
                    return bass.ds(pe.value_load(g.plan[0:1, 2, bass.ds(s.tile, 1)], min_val=0, max_val=WEIGHT_SLOTS - 1), 1)

                def mm_up(s):
                    b = s.buf % 2
                    slot = slot_of(s)
                    if s.after(2):
                        hold(pe, g, h_done, s.tile - 1)
                    hold(pe, g, g.weights_in[s.buf], (s.lap + 1) * 32)
                    hold(pe, g, xt_copied, s.tile + 1)
                    for c in range(DC):
                        last = pe.matmul(ps_gu[:, b, 0:2 * INTER], x_t[:, b, c, :],
                                         g.up_w[:, slot, c * 2 * INTER:(c + 1) * 2 * INTER].rearrange("p a n -> p (a n)"),
                                         start=(c == 0), stop=(c == DC - 1))
                    last.then_inc(gu_done, 1)

                def turn_h(s):
                    b = s.buf % 2
                    hold(pe, g, h_done, s.tile + 1)
                    if s.after(2):
                        hold(pe, g, ht_copied, s.tile - 1)
                    for c in range(IC):
                        last = pe.transpose(ps_h[0:IW, b, c * P:(c + 1) * P], h[:, b, c * IW:(c + 1) * IW], g.ident[:])
                    last.then_inc(h_turned, 1)

                def mm_down(s):
                    b = s.buf % 2
                    slot = slot_of(s)
                    if s.after(2):
                        hold(pe, g, y_scaled, s.tile - 1)
                    hold(pe, g, ht_copied, s.tile + 1)
                    for c in range(IC):
                        last = pe.matmul(ps_y[:, b, :], h_t[:, c, :],
                                         g.down_w[:, slot, c * D:(c + 1) * D].rearrange("p a n -> p (a n)"),
                                         start=(c == 0), stop=(c == IC - 1))
                    last.then_inc(y_done, 1)

                first = Step(0, 0, 0, U)
                turn_x(first)
                mm_up(first)
                turn_x(first.at(1))

                def body(s):
                    turn_h(s)
                    if s.at(1).within(N):
                        mm_up(s.at(1))
                    if s.at(2).within(N):
                        turn_x(s.at(2))
                    mm_down(s)

                steps(pe, body)


def stage_finish(nc, g):
    with ExitStack() as ctx:
        def sb(name, shape, dt=F32):
            return ctx.enter_context(nc.sbuf_tensor(f"finish_{name}", shape, dt))

        def sem(name):
            return ctx.enter_context(nc.semaphore(f"finish_{name}"))

        N, U = TOK_TILES, 4
        x2 = sb("x2", [P, U, D])
        ys = sb("ys", [P, U, TOP_K, D])
        parts = sb("parts", [P, U, 2, D])
        total = sb("total", [P, U, D])
        stats = sb("stats", [P, U, 6])
        mean_var = sb("mean_var", [P, U, 2])
        var_eps = sb("var_eps", [P, U])
        rstd = sb("rstd", [P, U])
        normed = sb("normed", [P, U, D])
        rows_in = [sem(f"rows_in{u}") for u in range(U)]
        stored = [sem(f"stored{u}") for u in range(U)]
        x2_added, halved, added = sem("x2_added"), sem("halved"), sem("added")
        shift = sb("shift", [P, U])
        stats_done, averaged, eps_added, rstd_done, shift_done, out_done = (
            sem("stats_done"), sem("averaged"), sem("eps_added"), sem("rstd_done"), sem("shift_done"), sem("out_done"))

        def steps(eng, body):
            run_steps(eng, N, U, U, 4, body)

        with nc.Block() as block:
            @block.sync
            def _(sp):
                y_by_token = g.y_rows[0:TOP_K * N_TOK, :].rearrange("(k t) d -> t k d", t=N_TOK)

                def load(s):
                    if s.after(U):
                        hold(sp, g, halved, s.tile - (U - 1))
                    rows = bass.ds(s.tile * P, P)
                    sp.dma_start(x2[:, s.buf, :], g.x2_rows[rows, :]).then_inc(rows_in[s.buf], 16)
                    sp.dma_start(ys[:, s.buf], y_by_token[rows, :, :]).then_inc(rows_in[s.buf], 16)

                steps(sp, load)

            @block.scalar
            def _(act):
                def norm_out(s):
                    b = s.buf
                    if s.after(U):
                        hold(act, g, stored[b], s.lap * 16)
                    hold(act, g, shift_done, s.tile + 1)
                    nc.scalar.activation(normed[:, b, :], total[:, b, :], ACT.Identity, bias=shift[:, b:b + 1],
                                         scale=rstd[:, b:b + 1]).then_inc(out_done, 1)
                    hold(act, g, out_done, s.tile + 1)
                    act.dma_start(g.out_rows[bass.ds(s.tile * P, P), :], normed[:, s.buf, :]).then_inc(stored[s.buf], 16)

                steps(act, norm_out)
                for u in range(U):
                    act.wait_ge(stored[u], 16 * len(range(u, N, U)))

            @block.gpsimd
            def _(pool):
                def add(s):
                    b, last = s.buf, TOP_K - 1
                    hold(pool, g, rows_in[b], (s.lap + 1) * 32)
                    nc.gpsimd.tensor_tensor(ys[:, b, last, :], ys[:, b, last, :], x2[:, b, :], ALU.add).then_inc(x2_added, 1)

                def rstd_of(s):
                    b = s.buf
                    hold(pool, g, averaged, s.tile + 1)
                    if s.after(U):
                        hold(pool, g, out_done, s.tile - (U - 1))
                    nc.gpsimd.tensor_scalar(var_eps[:, b:b + 1], mean_var[:, b, 1:2], EPS, None, ALU.add).then_inc(eps_added, 1)
                    hold(pool, g, eps_added, s.tile + 1)
                    nc.gpsimd.tensor_tensor(rstd[:, b:b + 1], var_eps[:, b:b + 1], g.minus_half[:], ALU.pow).then_inc(rstd_done, 1)
                    hold(pool, g, rstd_done, s.tile + 1)
                    nc.gpsimd.tensor_scalar(shift[:, b:b + 1], mean_var[:, b, 0:1], rstd[:, b:b + 1], -1.0,
                                            ALU.mult, ALU.mult).then_inc(shift_done, 1)

                add(Step(0, 0, 0, U))

                def body(s):
                    if s.at(1).within(N):
                        add(s.at(1))
                    rstd_of(s)

                steps(pool, body)

            @block.vector
            def _(dve):
                v = nc.vector

                def norm_in(s):
                    b = s.buf
                    half = TOP_K // 2
                    hold(dve, g, x2_added, s.tile + 1)
                    v.tensor_tensor(parts[:, b], ys[:, b, 0:half, :], ys[:, b, half:TOP_K, :], ALU.add).then_inc(halved, 1)
                    hold(dve, g, halved, s.tile + 1)
                    if s.after(U):
                        hold(dve, g, out_done, s.tile - (U - 1))
                    v.tensor_tensor(total[:, b, :], parts[:, b, 0, :], parts[:, b, 1, :], ALU.add).then_inc(added, 1)
                    hold(dve, g, added, s.tile + 1)
                    v.bn_stats(stats[:, b, :], total[:, b, :]).then_inc(stats_done, 1)
                    hold(dve, g, stats_done, s.tile + 1)
                    v.bn_aggr(mean_var[:, b, :], stats[:, b, :]).then_inc(averaged, 1)

                steps(dve, norm_in)


def decoder_layer(nc, x, tokens, context, wq, wk, wv, gate, up, down, out):
    g = Tensors()
    g.x_dram, g.tokens, g.context, g.wq, g.wk, g.wv = x, tokens, context, wq, wk, wv
    g.gate_dram, g.up_dram, g.down_dram = gate, up, down
    g.out_rows = out.rearrange("b t d -> (b t) d")
    g.x1_rows = nc.dram_tensor("x1_rows", (N_TOK, D), F32).ap()
    g.x2_rows = nc.dram_tensor("x2_rows", (N_TOK + SLOTS, D), F32).ap()
    g.y_rows = nc.dram_tensor("y_rows", (TOP_K * N_TOK + PAIR_TILES * P, D), F32).ap()
    g.split_rows = nc.dram_tensor("split_rows", (2, 2, 2, P, T), F32).ap()

    sb = nc.alloc_sbuf_tensor
    g.ident = sb("ident", [P, P], F32)
    g.ones = sb("ones", [P, P], F32)
    g.below = sb("below", [P, P], F32)
    g.count_p = sb("count_p", [P, P], F32)
    g.count_t = sb("count_t", [P, PLAN], F32)
    g.pair_offset = sb("pair_offset", [P, TOP_K], F32)
    g.spare_pair_up = sb("spare_pair_up", [P, PAIR_TILES], F32)
    g.minus_half = sb("minus_half", [P, 1], F32)
    g.gate = sb("gate_w", [P, DC, EXPERTS], F32)
    g.slot_token_up = sb("slot_token_up", [P, SORT_TILES], F32)
    g.x2_row_of_slot = sb("x2_row_of_slot", [P, SORT_TILES], I32)
    g.token_of_slot = sb("token_of_slot", [P, SORT_TILES], I32)
    g.slot_full = sb("slot_full", [P, SORT_TILES], F32)
    g.hash_of_tile = sb("hash_of_tile", [1, SORT_TILES], I32)
    g.top_logits = sb("top_logits", [P, SORT_TILES, 8], F32)
    g.chosen = sb("chosen", [P, SORT_TILES, TOP_K, EXPERTS], F32)
    g.member = sb("member", [P, EXPERTS, SORT_TILES], F32)
    g.plan = sb("plan", [1, 3, PLAN], I32)
    g.pair_weight = sb("pair_weight", [P, PAIR_TILES], F32)
    g.pair_row = sb("pair_row", [P, PAIR_TILES], I32)
    g.pair_token = sb("pair_token", [P, PAIR_TILES], I32)
    g.constant = nc.alloc_semaphore("constant")
    g.weights_in = [nc.alloc_semaphore(f"weights_in{u}") for u in range(WEIGHT_SLOTS)]

    with nc.sbuf_tensor("ctx_t", [P, HASHES, DC, D], F32) as g.ctx_t:
        with nc.Block() as block:
            @block.gpsimd
            def _(pool):
                nc.gpsimd.memset(g.minus_half[:], -0.5).then_inc(g.constant, 1)

        with nc.sbuf_tensor("w_t", [P, EMB // P, 3, EMB], F32) as g.w_t, \
             nc.sbuf_tensor("x_in", [P, T // P, EMB], F32) as g.x_in:
            stage_sort(nc, g)
            stage_attention(nc, g)
        stage_hash_ffn(nc, g)
    with nc.sbuf_tensor("up_w", [P, WEIGHT_SLOTS, DC * 2 * INTER], F32) as g.up_w, \
         nc.sbuf_tensor("down_w", [IW, WEIGHT_SLOTS, IC * D], F32) as g.down_w:
        stage_dispatch(nc, g)
        stage_experts(nc, g)
    stage_finish(nc, g)


_INS = ["x", "itok_BxS_13_99985", "ctx_2048", "L0_attn_Wq", "L0_attn_Wk", "L0_attn_Wv",
        "L0_ffn_gate", "L0_ffn_gate_up_proj", "L0_ffn_down_proj"]


def kernel(**inputs):
    import numpy as _np
    import concourse.bacc as _bacc
    from concourse import mybir as _mybir
    from concourse.bass_utils import run_bass_kernel_spmd as _run

    nc = _bacc.Bacc("TRN2", target_bir_lowering=False, num_devices=1)
    arrays, args = {}, []
    for name in _INS:
        a = _np.ascontiguousarray(inputs[name])
        arrays[f"in_{name}_dram"] = a
        args.append(nc.dram_tensor(f"in_{name}_dram", a.shape, _mybir.dt.from_np(a.dtype), kind="ExternalInput").ap())
    args.append(nc.dram_tensor("out_0_dram", (B, T, D), _mybir.dt.float32, kind="ExternalOutput").ap())
    decoder_layer(nc, *args)
    r = _run(nc, [arrays], core_ids=[0])
    return r.results[0]["out_0_dram"]
```

```python
from contextlib import ExitStack

import concourse.bass as bass
from concourse import mybir

P = 128
ALU = mybir.AluOpType
ACT = mybir.ActivationFunctionType
AX = mybir.AxisListType
F32 = mybir.dt.float32
F32R = mybir.dt.float32r
BF16 = mybir.dt.bfloat16
I32 = mybir.dt.int32
U32 = mybir.dt.uint32

B, T, D = 4, 512, 512
N_TOK = B * T
TOK_TILES = N_TOK // P
DC = D // P
EPS = 1e-5
HD, EMB = 16, 256

VOCAB, HASHES = 25000, 4
HASH_SPAN = VOCAB // HASHES
SORT_TILES = TOK_TILES + HASHES - 1
SLOTS = SORT_TILES * P

HIGH, LOW = 0, 1
PRODUCTS = ((HIGH, HIGH), (HIGH, LOW), (LOW, HIGH))

EXPERTS, TOP_K, INTER = 32, 4, 192
IC = 2
IW = INTER // IC
GROUP = 4
LEAST_GROUPS = N_TOK * TOP_K // P // GROUP
MOST_GROUPS = -(-(N_TOK * TOP_K // P + EXPERTS - 1) // GROUP)
PLAN = (MOST_GROUPS + 1) * GROUP
WEIGHT_SLOTS = 4


class Tensors:
    pass


def sequence(eng, sem):
    done = [0]

    def link(instruction):
        done[0] += 1
        instruction.then_inc(sem, 1)
        eng.wait_ge(sem, done[0])

    return link


def slots_of_groups(nc, link, w, groups, tiles, ones_sum, ranks):
    v = nc.vector
    flat = "p g t -> p (g t)"
    link(v.memset(w.keep[:], 1.0))
    link(v.memset(w.keep[:, :, 0:1], 0.0))
    for part, ps in ones_sum:
        link(v.tensor_copy(w.sums[:, part], ps))
    link(v.tensor_tensor_scan(w.upto[:].rearrange(flat), w.keep[:].rearrange(flat),
                              w.sums[:].rearrange(flat), 0.0, ALU.mult, ALU.add))
    link(v.tensor_scalar(w.n_tiles_i[:], w.upto[:, :, tiles - 1], P / 2 - 0.5, 1.0 / P, ALU.add, ALU.mult))
    link(v.tensor_copy(w.n_tiles[:], w.n_tiles_i[:]))
    link(v.memset(w.ones_g[:], 1.0))
    link(v.tensor_tensor_scan(w.tiles_end[:], w.ones_g[:], w.n_tiles[:], 0.0, ALU.mult, ALU.add))
    link(v.tensor_tensor(w.first[:], w.tiles_end[:], w.n_tiles[:], ALU.subtract))
    link(v.tensor_scalar(w.first[:], w.first[:], float(P), None, ALU.mult))
    link(v.tensor_tensor(w.slot[:], w.upto[:], w.sums[:], ALU.subtract))
    for part, ps in ranks:
        link(v.tensor_tensor(w.slot[:, part], ps, w.slot[:, part], ALU.add))
    link(v.tensor_tensor(w.slot[:], w.slot[:], w.first[:].unsqueeze(2).to_broadcast([P, groups, tiles]), ALU.add))


def sort_buffers(sb, name, groups, tiles):
    w = Tensors()
    w.keep, w.sums, w.upto, w.slot = (
        sb(f"{name}_{n}", [P, groups, tiles], F32) for n in ("keep", "sums", "upto", "slot"))
    w.n_tiles, w.ones_g, w.tiles_end, w.first = (
        sb(f"{name}_{n}", [P, groups], F32) for n in ("n_tiles", "ones_g", "tiles_end", "first"))
    w.n_tiles_i = sb(f"{name}_n_tiles_i", [P, groups], I32)
    return w


def split_slot(nc, link, tile_of, place_of, tmp_i, slots):
    v = nc.vector
    link(v.tensor_scalar(tmp_i, slots, -(P / 2 - 0.5), 1.0 / P, ALU.add, ALU.mult))
    link(v.tensor_copy(tile_of, tmp_i))
    link(v.scalar_tensor_tensor(out=place_of, in0=tile_of, scalar=-float(P), in1=slots,
                                op0=ALU.mult, op1=ALU.add))


def stage_sort(nc, g):
    count_p, ones, below = g.count_p, g.ones, g.below
    ctx_t = g.ctx_t[LOW]
    with ExitStack() as ctx:
        def sb(name, shape, dt=F32):
            return ctx.enter_context(nc.sbuf_tensor(f"sort_{name}", shape, dt))

        def sem(name):
            return ctx.enter_context(nc.semaphore(f"sort_{name}"))

        ids_i = sb("ids_i", [TOK_TILES, P], I32)
        ids_f = sb("ids_f", [TOK_TILES, P])
        ids = sb("ids", [P, TOK_TILES])
        at_least = sb("at_least", [P, HASHES + 1, TOK_TILES])
        member = sb("member", [P, HASHES, TOK_TILES])
        w = sort_buffers(sb, "hash", HASHES, TOK_TILES)
        picked = sb("picked", [P, HASHES, TOK_TILES])
        tok_i = sb("tok_i", [P, TOK_TILES], I32)
        tile_of = sb("tile_of", [P, TOK_TILES])
        place_of = sb("place_of", [P, TOK_TILES])
        slot_of = sb("slot_of", [P, TOK_TILES])
        at_place = sb("at_place", [P, TOK_TILES, P])
        at_tile = sb("at_tile", [P, TOK_TILES, SORT_TILES])
        token_up = sb("token_up", [P, TOK_TILES])
        w_rows = sb("w_rows", [P, 3, 2, EMB])
        spare_up = sb("spare_up", [P, SORT_TILES])
        empty = sb("empty", [P, SORT_TILES])
        row_up = sb("row_up", [P, SORT_TILES])
        ctx_rows = sb("ctx_rows", [P, HASHES * DC, D])
        plan = sb("plan", [1, SORT_TILES, HASHES])
        plan_f = sb("plan_f", [1, SORT_TILES])
        plan_no = sb("plan_no", [1, SORT_TILES, HASHES])
        ps = ctx.enter_context(nc.psum_tensor("sort_ps", [P, 4, 512], F32))
        ps_ct = ctx.enter_context(nc.psum_tensor("ct_ps", [P, 4, 512], F32))

        ids_in, ctx_in = sem("ids_in"), [sem(f"ctx_in{e}") for e in range(HASHES)]
        matrices_made = sem("matrices_made")
        w_in, x_gate_in, w_turned, w_copied = sem("w_in"), sem("x_gate_in"), sem("w_turned"), sem("w_copied")
        cleared, constants = sem("cleared"), sem("constants")
        ids_float, ids_turned = sem("ids_float"), sem("ids_turned")
        members, ranked, v_chain, v_chain2 = sem("members"), sem("ranked"), sem("v_chain"), sem("v_chain2")
        placed, tabled = sem("placed"), sem("tabled")
        ct_turned, ct_copied = sem("ct_turned"), sem("ct_copied")

        with nc.Block() as block:
            @block.sync
            def _(sp):
                sp.dma_start(ids_i[:], g.tokens.rearrange("b (j p) -> (b j) p", p=P)).then_inc(ids_in, 16)
                for n, w_dram in enumerate((g.wq, g.wk, g.wv)):
                    sp.dma_start(g.w_heads[n].rearrange("(h d) e -> h d e", d=HD), w_dram[:, 0:HD, 0:EMB]).then_inc(w_in, 16)
                sp.dma_start(g.x_in[:], g.x_dram[0, :, 0:EMB].rearrange("(c p) e -> p c e", p=P)).then_inc(x_gate_in, 16)
                sp.wait_ge(w_in, 3 * 16)
                sp.dma_start(w_rows[:], g.w_heads.rearrange("n (h p) e -> p n h e", p=P)).then_inc(w_in, 16)
                for e in range(HASHES):
                    sp.dma_start(ctx_rows[:, e * DC:(e + 1) * DC, :], g.context[e].rearrange("(c p) d -> p c d", p=P)).then_inc(ctx_in[e], 16)
                with nc.allow_non_contiguous_dma(reason="the gate's rows are 32 elements"):
                    sp.dma_start(g.gate[:], g.gate_dram.rearrange("(c p) e -> p c e", p=P)).then_inc(x_gate_in, 16)
                sp.wait_ge(x_gate_in, 2 * 16)

            @block.gpsimd
            def _(pool):
                nc.gpsimd.memset(g.ident[:], 0.0).then_inc(cleared, 1)
                nc.gpsimd.memset(ones[:], 1.0).then_inc(cleared, 1)
                pool.wait_ge(cleared, 2)
                nc.gpsimd.affine_select(out=g.ident[:], in_=g.ident[:], compare_op=ALU.not_equal, fill=1.0,
                                        base=0, pattern=[[-1, P]], channel_multiplier=1).then_inc(matrices_made, 1)
                nc.gpsimd.affine_select(out=below[:], in_=ones[:], compare_op=ALU.is_gt, fill=0.0,
                                        base=0, pattern=[[1, P]], channel_multiplier=-1).then_inc(matrices_made, 1)
                nc.gpsimd.iota(count_p[:], pattern=[[1, P]], base=0, channel_multiplier=0,
                               allow_small_or_imprecise_dtypes=True).then_inc(constants, 1)
                nc.gpsimd.iota(g.count_t[:], pattern=[[1, PLAN]], base=0, channel_multiplier=0,
                               allow_small_or_imprecise_dtypes=True).then_inc(constants, 1)
                nc.gpsimd.iota(token_up[:], pattern=[[P, TOK_TILES]], base=1, channel_multiplier=1,
                               allow_small_or_imprecise_dtypes=True).then_inc(constants, 1)
                nc.gpsimd.iota(spare_up[:], pattern=[[P, SORT_TILES]], base=N_TOK + 1, channel_multiplier=1,
                               allow_small_or_imprecise_dtypes=True).then_inc(constants, 1)
                nc.gpsimd.iota(plan_no[:], pattern=[[1, SORT_TILES], [0, HASHES]], base=0, channel_multiplier=0,
                               allow_small_or_imprecise_dtypes=True).then_inc(constants, 1)
                nc.gpsimd.iota(g.pair_offset[:], pattern=[[N_TOK, TOP_K]], base=0, channel_multiplier=0,
                               allow_small_or_imprecise_dtypes=True)
                nc.gpsimd.iota(g.spare_pair_up[:], pattern=[[P, PLAN]], base=TOP_K * N_TOK + 1, channel_multiplier=1,
                               allow_small_or_imprecise_dtypes=True)

            @block.vector
            def _(dve):
                v = nc.vector
                link = sequence(dve, v_chain)
                dve.wait_ge(ids_in, 16)
                link(v.tensor_scalar(ids_f[:], ids_i[:], float(VOCAB - 1), 0.0, ALU.min, ALU.max))
                v.tensor_copy(ids_f[:], ids_f[:]).then_inc(ids_float, 1)
                dve.wait_ge(ids_turned, 1)
                v.tensor_copy(ids[:], ps[:, 0, 0:TOK_TILES]).then_inc(v_chain, 1)
                dve.wait_ge(v_chain, 2)
                link = sequence(dve, v_chain2)
                link(v.memset(at_least[:, 0, :], 1.0))
                link(v.memset(at_least[:, HASHES, :], 0.0))
                for e in range(1, HASHES):
                    link(v.tensor_scalar(at_least[:, e, :], ids[:], float(e * HASH_SPAN), None, ALU.is_ge))
                v.tensor_tensor(member[:], at_least[:, 0:HASHES, :], at_least[:, 1:HASHES + 1, :],
                                ALU.subtract).then_inc(members, 1)
                dve.wait_ge(ranked, 1)
                shape = ps[:, 1, 0:HASHES * TOK_TILES].rearrange("p (g t) -> p g t", g=HASHES)
                shape2 = ps[:, 2, 0:HASHES * TOK_TILES].rearrange("p (g t) -> p g t", g=HASHES)
                slots_of_groups(nc, link, w, HASHES, TOK_TILES, [(slice(0, HASHES), shape2)], [(slice(0, HASHES), shape)])
                link(v.tensor_tensor(picked[:], w.slot[:], member[:], ALU.mult))
                link(v.tensor_reduce(slot_of[:], picked[:].rearrange("p g t -> p t g"), AX.X, ALU.add))
                split_slot(nc, link, tile_of[:], place_of[:], tok_i[:], slot_of[:])
                dve.wait_ge(constants, 5)
                link(v.tensor_tensor(at_place[:], count_p[:].unsqueeze(1).to_broadcast([P, TOK_TILES, P]),
                                     place_of[:].unsqueeze(2).to_broadcast([P, TOK_TILES, P]), ALU.is_equal))
                link(v.tensor_tensor(at_tile[:], g.count_t[:, 0:SORT_TILES].unsqueeze(1).to_broadcast([P, TOK_TILES, SORT_TILES]),
                                     tile_of[:].unsqueeze(2).to_broadcast([P, TOK_TILES, SORT_TILES]), ALU.is_equal))
                v.tensor_tensor(at_tile[:], at_tile[:], token_up[:].unsqueeze(2).to_broadcast([P, TOK_TILES, SORT_TILES]),
                                ALU.mult).then_inc(placed, 1)
                dve.wait_ge(tabled, 1)
                link(v.tensor_copy(g.slot_token_up[:], ps[:, 3, 0:SORT_TILES]))
                link(v.tensor_scalar(g.slot_full[:], g.slot_token_up[:], 0.5, None, ALU.is_gt))
                link(v.tensor_scalar(g.token_of_slot[:], g.slot_token_up[:], -1.0, 0.0, ALU.add, ALU.max))
                link(v.tensor_scalar(empty[:], g.slot_token_up[:], 0.5, None, ALU.is_lt))
                link(v.tensor_tensor(row_up[:], empty[:], spare_up[:], ALU.mult))
                link(v.tensor_tensor(row_up[:], row_up[:], g.slot_token_up[:], ALU.add))
                link(v.tensor_scalar(g.x2_row_of_slot[:], row_up[:], -1.0, None, ALU.add))
                link(v.tensor_tensor(plan[:], w.tiles_end[0:1, :].unsqueeze(1).to_broadcast([1, SORT_TILES, HASHES]),
                                     plan_no[:], ALU.is_le))
                link(v.tensor_reduce(plan_f[:], plan[:], AX.X, ALU.add))
                link(v.tensor_scalar(g.hash_of_tile[:], plan_f[:], float(HASHES - 1), None, ALU.min))

            @block.scalar
            def _(act):
                for n in range(3 * EMB // P):
                    act.wait_ge(w_turned, n + 1)
                    nc.scalar.copy(g.w_t[:, n % (EMB // P), n // (EMB // P), :], ps_ct[:, n % 4, 0:EMB]).then_inc(w_copied, 1)
                for n in range(HASHES * DC):
                    act.wait_ge(ct_turned, n + 1)
                    e, c = n // DC, n % DC
                    nc.scalar.copy(ctx_t[:, e, c, :].bitcast(F32), ps_ct[:, n % 4, :]).then_inc(ct_copied, 1)

            @block.tensor
            def _(pe):
                pe.wait_ge(matrices_made, 1)
                pe.wait_ge(ids_float, 1)
                pe.transpose(ps[:, 0, 0:TOK_TILES], ids_f[:], g.ident[0:TOK_TILES, 0:TOK_TILES]).then_inc(ids_turned, 1)
                pe.wait_ge(matrices_made, 2)
                pe.wait_ge(members, 1)
                flat = member[:].rearrange("p g t -> p (g t)")
                pe.matmul(ps[:, 1, 0:HASHES * TOK_TILES], below[:], flat, start=True, stop=True)
                pe.matmul(ps[:, 2, 0:HASHES * TOK_TILES], ones[:], flat, start=True, stop=True).then_inc(ranked, 1)
                pe.wait_ge(w_in, 4 * 16)
                W_TURNS = 3 * EMB // P
                for n in range(W_TURNS):
                    which, c = n // (EMB // P), n % (EMB // P)
                    if n >= 4:
                        pe.wait_ge(w_copied, n - 3)
                    for half in range(2):
                        last = pe.transpose(ps_ct[:, n % 4, half * P:(half + 1) * P],
                                            w_rows[:, which, half, c * P:(c + 1) * P], g.ident[:])
                    last.then_inc(w_turned, 1)
                pe.wait_ge(w_copied, W_TURNS)
                for n in range(HASHES * DC):
                    e, c = n // DC, n % DC
                    if n == DC:
                        pe.wait_ge(placed, 1)
                        for t in range(TOK_TILES):
                            last = pe.matmul(ps[:, 3, 0:SORT_TILES], at_place[:, t, :], at_tile[:, t, :],
                                             start=(t == 0), stop=(t == TOK_TILES - 1))
                        last.then_inc(tabled, 1)
                    if c == 0:
                        pe.wait_ge(ctx_in[e], 16)
                    if n >= 4:
                        pe.wait_ge(ct_copied, n - 3)
                    for r in range(DC):
                        last = pe.transpose(ps_ct[:, n % 4, r * P:(r + 1) * P],
                                            ctx_rows[:, e * DC + r, c * P:(c + 1) * P], g.ident[:])
                    last.then_inc(ct_turned, 1)


class Step:

    def __init__(self, tile, buf, lap, unroll):
        self.tile, self.buf, self.lap, self.unroll = tile, buf, lap, unroll

    def at(self, k):
        n = self.buf + k
        return Step(self.tile + k, n % self.unroll, self.lap + n // self.unroll, self.unroll)

    def within(self, count):
        return not isinstance(self.tile, int) or 0 <= self.tile < count

    def after(self, n):
        return not isinstance(self.tile, int) or self.tile >= n


def run_steps(eng, count, unroll, head, tail, body):
    looped = (count - head - tail) // unroll
    for t in range(head):
        body(Step(t, t % unroll, t // unroll, unroll))
    with eng.Fori(0, looped) as i:
        for u in range(unroll):
            body(Step(i * unroll + (head + u), u, i + head // unroll, unroll))
    for t in range(head + looped * unroll, count):
        body(Step(t, t % unroll, t // unroll, unroll))


def hold(eng, g, sem, value):
    if not isinstance(value, int):
        value = eng.to_reg(value)
        eng.wait_ge(g.constant, 1)
    eng.wait_ge(sem, value)


def stage_hash_ffn(nc, g):
    with ExitStack() as ctx:
        def sb(name, shape, dt=F32):
            return ctx.enter_context(nc.sbuf_tensor(f"hash_ffn_{name}", shape, dt))

        def sem(name):
            return ctx.enter_context(nc.semaphore(f"hash_ffn_{name}"))

        def bank(name, n=1):
            return ctx.enter_context(nc.psum_tensor(f"hash_ffn_{name}", [P, n, 512], F32))

        N, U = SORT_TILES, 4
        index = sb("index", [P, U], I32)
        out_index = sb("out_index", [P, U], I32)
        rows = sb("rows", [P, U, D])
        x_t = [sb(f"x_t_{n}", [P, 2, DC, P], F32R) for n in ("high", "low")]
        silu = sb("silu", [P, 2, D])
        h = sb("h", [P, 2, D])
        h_t = [sb(f"h_t_{n}", [P, DC, P], F32R) for n in ("high", "low")]
        total = sb("total", [P, 2, D])
        stats = sb("stats", [P, 6])
        mean_var = sb("mean_var", [P, 2, 2])
        var_eps = sb("var_eps", [P, 2])
        rstd = sb("rstd", [P, 2])
        shift = sb("shift", [P, 2])
        x2 = sb("x2", [P, U, D])
        x2_t = sb("x2_t", [P, DC, P])
        logits = sb("logits", [P, EXPERTS])
        largest = sb("largest", [P, 8])
        largest_at = sb("largest_at", [P, 8], U32)
        absent = sb("absent", [P, SORT_TILES])
        expert_no = sb("expert_no", [P, TOP_K])
        chosen = sb("chosen", [P, TOP_K, EXPERTS])
        member = sb("member", [P, EXPERTS])

        ps_x, ps_h, ps_x2, ps_u, ps_y, ps_l = bank("ps_x"), bank("ps_h"), bank("ps_x2"), bank("ps_u", 2), bank("ps_y", 2), bank("ps_l")
        rows_in = [sem(f"rows_in{u}") for u in range(U)]
        stored = [sem(f"stored{u}") for u in range(U)]
        index_set, out_index_set, x_turned, xt_high, xt_low = (
            sem("index_set"), sem("out_index_set"), sem("x_turned"), sem("xt_high"), sem("xt_low"))
        u_done, silu_done, h_done, h_turned, ht_high, ht_low = (
            sem("u_done"), sem("silu_done"), sem("h_done"), sem("h_turned"), sem("ht_high"), sem("ht_low"))
        y_done, added, stats_done, averaged = sem("y_done"), sem("added"), sem("stats_done"), sem("averaged")
        eps_added, rstd_done, shift_done, x2_done = sem("eps_added"), sem("rstd_done"), sem("shift_done"), sem("x2_done")
        x2_turned, x2t_copied, logits_done = sem("x2_turned"), sem("x2t_copied"), sem("logits_done")
        logits_copied, top_found, top_indexed, top_kept = sem("logits_copied"), sem("top_found"), sem("top_indexed"), sem("top_kept")
        absent_set, numbered, compared, counted = sem("absent_set"), sem("numbered"), sem("compared"), sem("counted")

        final = Step(N - 1, (N - 1) % U, (N - 1) // U, U)

        def steps(eng, body):
            run_steps(eng, N, U, U, 3, body)

        with nc.Block() as block:
            @block.gpsimd
            def _(pool):
                def rstd_of(s):
                    b = s.buf % 2
                    hold(pool, g, averaged, s.tile + 1)
                    nc.gpsimd.tensor_scalar(var_eps[:, b:b + 1], mean_var[:, b, 1:2], EPS, None, ALU.add).then_inc(eps_added, 1)
                    hold(pool, g, eps_added, s.tile + 1)
                    if s.after(2):
                        hold(pool, g, x2_done, s.tile - 1)
                    nc.gpsimd.tensor_tensor(rstd[:, b:b + 1], var_eps[:, b:b + 1], g.minus_half[:], ALU.pow).then_inc(rstd_done, 1)
                    hold(pool, g, rstd_done, s.tile + 1)
                    nc.gpsimd.tensor_scalar(shift[:, b:b + 1], mean_var[:, b, 0:1], rstd[:, b:b + 1], -1.0,
                                            ALU.mult, ALU.mult).then_inc(shift_done, 1)

                def gather(s):
                    if s.after(U):
                        hold(pool, g, added, s.tile - (U - 1))
                    nc.gpsimd.tensor_copy(index[:, s.buf:s.buf + 1], g.token_of_slot[:, bass.ds(s.tile, 1)]).then_inc(index_set, 1)
                    hold(pool, g, index_set, s.tile + 1)
                    nc.gpsimd.indirect_dma_start(
                        out=rows[:, s.buf, :], out_offset=None, in_=g.x1_rows,
                        in_offset=bass.IndirectOffsetOnAxis(ap=index[:, s.buf:s.buf + 1], axis=0),
                    ).then_inc(rows_in[s.buf], 16)

                def store(s):
                    if s.after(U):
                        hold(pool, g, stored[s.buf], s.lap * 16)
                    nc.gpsimd.tensor_copy(out_index[:, s.buf:s.buf + 1], g.x2_row_of_slot[:, bass.ds(s.tile, 1)]).then_inc(out_index_set, 1)
                    hold(pool, g, out_index_set, s.tile + 1)
                    hold(pool, g, x2_done, s.tile + 1)
                    nc.gpsimd.indirect_dma_start(
                        out=g.x2_rows, out_offset=bass.IndirectOffsetOnAxis(ap=out_index[:, s.buf:s.buf + 1], axis=0),
                        in_=x2[:, s.buf, :], in_offset=None,
                    ).then_inc(stored[s.buf], 16)

                pool.wait_ge(g.constant, 1)
                for t in range(3):
                    gather(Step(t, t % U, t // U, U))

                def body(s):
                    if s.at(3).within(N):
                        gather(s.at(3))
                    if s.after(1):
                        rstd_of(s.at(-1))
                        store(s.at(-1))

                steps(pool, body)
                rstd_of(final)
                store(final)
                for u in range(U):
                    pool.wait_ge(stored[u], 16 * len(range(u, N, U)))

            @block.scalar
            def _(act):
                def xt(s):
                    if s.after(2):
                        hold(act, g, u_done, s.tile - 1)
                    hold(act, g, x_turned, s.tile + 1)
                    nc.scalar.copy(x_t[HIGH][:, s.buf % 2].rearrange("p c t -> p (c t)"), ps_x[:, 0, :]).then_inc(xt_high, 1)

                def silu_of(s):
                    if s.after(2):
                        hold(act, g, h_done, s.tile - 1)
                    hold(act, g, u_done, s.tile + 1)
                    nc.scalar.activation(silu[:, s.buf % 2, :], ps_u[:, s.buf % 2, :], ACT.Silu).then_inc(silu_done, 1)

                def ht(s):
                    if s.after(1):
                        hold(act, g, y_done, s.tile)
                    hold(act, g, h_turned, s.tile + 1)
                    nc.scalar.copy(h_t[HIGH][:].rearrange("p c t -> p (c t)"), ps_h[:, 0, :]).then_inc(ht_high, 1)

                def norm_out(s):
                    b = s.buf % 2
                    if s.after(U):
                        hold(act, g, stored[s.buf], s.lap * 16)
                        hold(act, g, x2_turned, s.tile - (U - 1))
                    hold(act, g, shift_done, s.tile + 1)
                    nc.scalar.activation(x2[:, s.buf, :], total[:, b, :], ACT.Identity, bias=shift[:, b:b + 1],
                                         scale=rstd[:, b:b + 1]).then_inc(x2_done, 1)

                def x2t(s):
                    if s.after(1):
                        hold(act, g, logits_done, s.tile)
                    hold(act, g, x2_turned, s.tile + 1)
                    nc.scalar.copy(x2_t[:].rearrange("p c t -> p (c t)"), ps_x2[:, 0, :]).then_inc(x2t_copied, 1)

                first = Step(0, 0, 0, U)
                xt(first)
                xt(first.at(1))
                silu_of(first)

                def body(s):
                    ht(s)
                    if s.after(2):
                        x2t(s.at(-2))
                    if s.at(1).within(N):
                        silu_of(s.at(1))
                    if s.at(2).within(N):
                        xt(s.at(2))
                    if s.after(1):
                        norm_out(s.at(-1))

                steps(act, body)
                x2t(final.at(-1))
                norm_out(final)
                x2t(final)

            @block.vector
            def _(dve):
                v = nc.vector

                def gate(s):
                    if s.after(2):
                        hold(dve, g, h_turned, s.tile - 1)
                    hold(dve, g, silu_done, s.tile + 1)
                    v.tensor_tensor(h[:, s.buf % 2, :], ps_u[:, s.buf % 2, :], silu[:, s.buf % 2, :], ALU.mult).then_inc(h_done, 1)

                def low_part(out, ps, high):
                    return v.tensor_tensor(out.rearrange("p c t -> p (c t)"), ps[:, 0, :],
                                           high.bitcast(F32).rearrange("p c t -> p (c t)"), ALU.subtract)

                def xt(s):
                    b = s.buf % 2
                    if s.after(2):
                        hold(dve, g, u_done, s.tile - 1)
                    hold(dve, g, xt_high, s.tile + 1)
                    low_part(x_t[LOW][:, b], ps_x, x_t[HIGH][:, b]).then_inc(xt_low, 1)

                def ht(s):
                    if s.after(1):
                        hold(dve, g, y_done, s.tile)
                    hold(dve, g, ht_high, s.tile + 1)
                    low_part(h_t[LOW][:], ps_h, h_t[HIGH][:]).then_inc(ht_low, 1)

                def norm_in(s):
                    b = s.buf % 2
                    hold(dve, g, y_done, s.tile + 1)
                    if s.after(2):
                        hold(dve, g, x2_done, s.tile - 1)
                    v.tensor_tensor(total[:, b, :], ps_y[:, b, :], rows[:, s.buf, :], ALU.add).then_inc(added, 1)
                    hold(dve, g, added, s.tile + 1)
                    v.bn_stats(stats[:], total[:, b, :]).then_inc(stats_done, 1)
                    hold(dve, g, stats_done, s.tile + 1)
                    v.bn_aggr(mean_var[:, b, :], stats[:]).then_inc(averaged, 1)

                def top(s):
                    hold(dve, g, logits_done, s.tile + 1)
                    if s.after(1):
                        hold(dve, g, top_kept, s.tile)
                    v.tensor_copy(logits[:], ps_l[:, 0, 0:EXPERTS]).then_inc(logits_copied, 1)
                    hold(dve, g, logits_copied, s.tile + 1)
                    v.max(largest[:], logits[:]).then_inc(top_found, 1)
                    hold(dve, g, top_found, s.tile + 1)
                    v.max_index(largest_at[:], largest[:], logits[:]).then_inc(top_indexed, 1)
                    v.tensor_copy(g.top_logits[:, bass.ds(s.tile, 1), :].rearrange("p a k -> p (a k)"), largest[:])
                    hold(dve, g, top_indexed, s.tile + 1)
                    v.tensor_scalar(expert_no[:], largest_at[:, 0:TOP_K], absent[:, bass.ds(s.tile, 1)], None, ALU.add).then_inc(numbered, 1)
                    hold(dve, g, numbered, s.tile + 1)
                    v.tensor_tensor(chosen[:], g.count_p[:, 0:EXPERTS].unsqueeze(1).to_broadcast([P, TOP_K, EXPERTS]),
                                    expert_no[:].unsqueeze(2).to_broadcast([P, TOP_K, EXPERTS]), ALU.is_equal).then_inc(compared, 1)
                    hold(dve, g, compared, s.tile + 1)
                    v.tensor_reduce(member[:], chosen[:].rearrange("p k e -> p e k"), AX.X, ALU.add).then_inc(counted, 1)
                    v.tensor_copy(g.chosen[:, bass.ds(s.tile, 1)].rearrange("p a k e -> p (a k e)"), chosen[:].rearrange("p k e -> p (k e)"))
                    hold(dve, g, counted, s.tile + 1)
                    v.tensor_copy(g.member[:, :, bass.ds(s.tile, 1)].rearrange("p e a -> p (e a)"), member[:]).then_inc(top_kept, 1)

                v.tensor_scalar(absent[:], g.slot_full[:], -1.0, -1000.0, ALU.add, ALU.mult).then_inc(absent_set, 1)
                dve.wait_ge(absent_set, 1)
                first = Step(0, 0, 0, U)
                xt(first)
                xt(first.at(1))
                gate(first)

                def body(s):
                    ht(s)
                    if s.after(1):
                        norm_in(s.at(-1))
                    if s.at(1).within(N):
                        gate(s.at(1))
                    if s.at(2).within(N):
                        xt(s.at(2))
                    if s.after(3):
                        top(s.at(-3))

                steps(dve, body)
                norm_in(final)
                for t in (-2, -1, 0):
                    top(final.at(t))

            @block.tensor
            def _(pe):
                def turn(source, target, done):
                    for c in range(DC):
                        last = pe.transpose(target[:, 0, c * P:(c + 1) * P], source[:, c * P:(c + 1) * P], g.ident[:])
                    last.then_inc(done, 1)

                def turn_x(s):
                    hold(pe, g, rows_in[s.buf], (s.lap + 1) * 16)
                    if s.after(1):
                        hold(pe, g, xt_low, s.tile)
                    turn(rows[:, s.buf, :], ps_x, x_turned)

                def times_context(s, source, bank_of, done):
                    expert = pe.value_load(g.hash_of_tile[0:1, bass.ds(s.tile, 1)], min_val=0, max_val=HASHES - 1)
                    for c in range(DC):
                        for n, (part, ctx_part) in enumerate(PRODUCTS):
                            last = pe.matmul(bank_of[:, s.buf % 2, :], source[part][:, c, :],
                                             g.ctx_t[ctx_part][:, bass.ds(expert, 1), c, :].rearrange("p a n -> p (a n)"),
                                             start=(c == 0 and n == 0), stop=(c == DC - 1 and n == 2))
                    last.then_inc(done, 1)

                def mm_u(s):
                    if s.after(2):
                        hold(pe, g, h_done, s.tile - 1)
                    hold(pe, g, xt_low, s.tile + 1)
                    times_context(s, [part[:, s.buf % 2] for part in x_t], ps_u, u_done)

                def turn_h(s):
                    hold(pe, g, h_done, s.tile + 1)
                    if s.after(1):
                        hold(pe, g, ht_low, s.tile)
                    turn(h[:, s.buf % 2, :], ps_h, h_turned)

                def mm_y(s):
                    if s.after(2):
                        hold(pe, g, added, s.tile - 1)
                    hold(pe, g, ht_low, s.tile + 1)
                    times_context(s, h_t, ps_y, y_done)

                def turn_x2(s):
                    hold(pe, g, x2_done, s.tile + 1)
                    if s.after(1):
                        hold(pe, g, x2t_copied, s.tile)
                    turn(x2[:, s.buf, :], ps_x2, x2_turned)

                def route(s):
                    if s.after(1):
                        hold(pe, g, logits_copied, s.tile)
                    hold(pe, g, x2t_copied, s.tile + 1)
                    for c in range(DC):
                        last = pe.matmul(ps_l[:, 0, 0:EXPERTS], x2_t[:, c, :], g.gate[:, c, :], start=(c == 0), stop=(c == DC - 1))
                    last.then_inc(logits_done, 1)

                first = Step(0, 0, 0, U)
                turn_x(first)
                turn_x(first.at(1))
                mm_u(first)

                def body(s):
                    turn_h(s)
                    if s.at(1).within(N):
                        mm_u(s.at(1))
                    if s.at(2).within(N):
                        turn_x(s.at(2))
                    mm_y(s)
                    if s.after(2):
                        route(s.at(-2))
                    if s.after(1):
                        turn_x2(s.at(-1))

                steps(pe, body)
                route(final.at(-1))
                turn_x2(final)
                route(final)


def stage_attention(nc, g):
    HEADS = EMB // HD
    EC, QT = EMB // P, T // P
    HG = P // HD
    QUADS = HEADS // 4
    COPIES = 4
    STACKED = COPIES * HD
    VW = 32
    MASKED = -1e30
    SCALE = HD ** -0.5

    with ExitStack() as ctx:
        def sb(name, shape, dt=F32):
            return ctx.enter_context(nc.sbuf_tensor(f"attn_{name}", shape, dt))

        def sem(name):
            return ctx.enter_context(nc.semaphore(f"attn_{name}"))

        def bank(name, n=1):
            return ctx.enter_context(nc.psum_tensor(f"attn_{name}", [P, n, 512], F32))

        N, U = B * QUADS, QUADS
        w_t, x_in = g.w_t, g.x_in
        x_t = sb("x_t", [P, EC, T])
        hi = sb("hi", [P, 2, T], F32R)
        lo = sb("lo", [P, 2, T], F32R)
        qs = sb("qs", [P, 2, HG, T], F32R)
        ks = sb("ks", [P, 2, HG, T], F32R)
        v_one = sb("v_one", [P, 2, QT, HG, VW])
        maxima = sb("maxima", [P, 2, QT, 4])
        neg_max = sb("neg_max", [P, QT, 2, 4], F32R)
        neg_max_t = sb("neg_max_t", [P, T], F32R)
        of_head = sb("of_head", [P, 4, P], F32R)
        head_rows = sb("head_rows", [P, 4])
        exps = sb("exps", [P, 2, 4, T])
        o_t = sb("o_t", [P, T])
        sums_inv = sb("sums_inv", [P, QT, 4])
        o_norm = sb("o_norm", [P, QT, 4, HD])
        res = sb("res", [P, QT, D])
        stats = sb("stats", [P, QT, 6])
        mean_var = sb("mean_var", [P, QT, 2])
        var_eps = sb("var_eps", [P, QT])
        rstd = sb("rstd", [P, QT])
        x1 = sb("x1", [P, QT, D])
        one_f = sb("one_f", [P, 1])
        ident_b = sb("ident_b", [P, P], BF16)
        later_key = sb("later_key", [P, P], BF16)
        earlier_query = sb("earlier_query", [P, P], BF16)
        mask_f = sb("mask_f", [P, 2, P])

        ps_s, ps_t, ps_o, ps_m = bank("ps_s", 2), bank("ps_t", 4), bank("ps_o"), bank("ps_m")

        context_high = sem("context_high")
        x_arrived, res_in = sem("x_arrived"), sem("res_in")
        split_out, cleared, masks_made, constants, rows_set = sem("split_out"), sem("cleared"), sem("masks_made"), sem("constants"), sem("rows_set")
        xt_turned, xt_copied = sem("xt_turned"), sem("xt_copied")
        projected, hi_done, lo_done, v_projected, v_copied = sem("projected"), sem("hi_done"), sem("lo_done"), sem("v_projected"), sem("v_copied")
        q_stacked, k_stacked = [sem(f"q_stacked{i}") for i in range(2)], [sem(f"k_stacked{i}") for i in range(2)]
        s_done, max_done, max_hi, max_lo = sem("s_done"), sem("max_done"), sem("max_hi"), sem("max_lo")
        max_turned, max_copied = sem("max_turned"), sem("max_copied")
        t_done, exp_done, pv_done, o_copied = sem("t_done"), sem("exp_done"), sem("pv_done"), sem("o_copied")
        o_turned, inv_done, o_normed, res_added = sem("o_turned"), sem("inv_done"), sem("o_normed"), sem("res_added")
        stats_done, averaged, eps_added, rstd_done, x1_done, stored = (
            sem("stats_done"), sem("averaged"), sem("eps_added"), sem("rstd_done"), sem("x1_done"), sem("stored"))

        def steps(eng, body):
            run_steps(eng, N, U, U, U, body)

        def group(s):
            return s.lap * 2 + s.buf // 2

        def leads_group(s):
            return s.buf % 2 == 0 and s.at(2).within(N)

        def bank_of(first, n):
            return ps_t[:, n, :] if first else ps_m[:, 0, :]

        def scale_rows(eng, engine, b):
            if not (isinstance(b, int) and b == 0):
                hold(eng, g, stored, b * 16)
            hold(eng, g, rstd_done, b + 1)
            for c in range(QT):
                engine.tensor_scalar(x1[:, c, :], res[:, c, :], mean_var[:, c, 0:1], rstd[:, c:c + 1],
                                     ALU.subtract, ALU.mult).then_inc(x1_done, 1)

        def turns_x(s):
            return s.buf == 1 and s.at(QUADS - 1).within(N)

        PER_S, PER_T = 4 * QT, 2 * QT
        Q, K, V = 0, 1, 2
        X = (0, 1)
        HEADS_TURNED, MAX_TURNED = 4, 7
        LAST_V = 1
        LEAD = [3, 3, 2, 2, 2, 2, 2, 0]

        with nc.Block() as block:
            @block.sync
            def _(sp):
                def load_x(b):
                    hold(sp, g, xt_turned, b * EC)
                    sp.dma_start(x_in[:], g.x_dram[bass.ds(b, 1), :, 0:EMB].rearrange("a (c p) e -> p (a c) e", p=P)).then_inc(x_arrived, 16)

                def load_res(b):
                    if not (isinstance(b, int) and b == 0):
                        hold(sp, g, x1_done, b * QT)
                    sp.dma_start(res[:], g.x_dram[bass.ds(b, 1), :, :].rearrange("a (c p) e -> p (a c) e", p=P)).then_inc(res_in, 16)

                def stack(n, half):
                    if not (isinstance(n, int) and n < 2):
                        hold(sp, g, t_done, (n - 1) * 2 * PER_T)
                    hold(sp, g, hi_done, n * 2 + 2)
                    hold(sp, g, lo_done, n * 2 + 2)
                    for p, part in enumerate((hi, lo)):
                        sp.dma_start(g.split_rows[half, p].rearrange("w r t -> r w t"), part[:].bitcast(F32)).then_inc(split_out, 16)
                    hold(sp, g, split_out, n * 32 + 32)
                    for which, stacked, done in ((0, qs, q_stacked), (1, ks, k_stacked)):
                        for r in range(COPIES):
                            p = (r // 2, r % 2)[which]
                            sp.dma_start(stacked[r * HD:(r + 1) * HD, half, :, :].bitcast(F32),
                                         g.split_rows[half, p, which].rearrange("(h d) t -> d h t", d=HD)).then_inc(done[half], 16)

                def store(b):
                    hold(sp, g, x1_done, b * QT + QT)
                    sp.dma_start(g.x1_rows[bass.ds(b * T, T), :].rearrange("(c p) d -> p c d", p=P), x1[:]).then_inc(stored, 16)

                load_res(0)
                stack(0, 0)

                def body(s):
                    if s.buf == 0 and s.at(U).within(N):
                        load_x(s.lap + 1)
                    if leads_group(s):
                        stack(group(s) + 1, 1 - s.buf // 2)
                    if s.buf == 1 and s.after(U):
                        store(s.lap - 1)
                        load_res(s.lap)

                steps(sp, body)
                store(B - 1)
                sp.wait_ge(stored, 16 * B)

            @block.gpsimd
            def _(pool):
                m = nc.gpsimd
                m.memset(mask_f[:], 0.0).then_inc(cleared, 1)
                m.memset(one_f[:], 1.0).then_inc(cleared, 1)
                m.memset(v_one[:], 0.0).then_inc(cleared, 1)
                pool.wait_ge(cleared, 3)
                m.affine_select(out=mask_f[:, 0, :], in_=mask_f[:, 0, :], compare_op=ALU.is_ge, fill=MASKED, base=0,
                                pattern=[[-1, P]], channel_multiplier=1).then_inc(masks_made, 1)
                m.affine_select(out=mask_f[:, 1, :], in_=mask_f[:, 1, :], compare_op=ALU.is_ge, fill=MASKED, base=0,
                                pattern=[[1, P]], channel_multiplier=-1).then_inc(masks_made, 1)
                m.memset(v_one[:].rearrange("p a c h w -> p (a c h) w")[:, :, HD:HD + 1], 1.0).then_inc(cleared, 1)
                pool.wait_ge(masks_made, 2)
                m.tensor_copy(later_key[:], mask_f[:, 0, :]).then_inc(constants, 1)
                m.tensor_copy(earlier_query[:], mask_f[:, 1, :]).then_inc(constants, 1)
                m.tensor_copy(ident_b[:], g.ident[:]).then_inc(constants, 1)
                pool.wait_ge(cleared, 4)
                pool.sem_inc(constants, 1)

                def add_attention(s):
                    q = s.buf
                    hold(pool, g, o_normed, s.tile + 1)
                    if q == 0:
                        hold(pool, g, res_in, (s.lap + 1) * 16)
                    part = res[:, :, q * 4 * HD:(q + 1) * 4 * HD]
                    m.tensor_tensor(part, part, o_norm[:].rearrange("p c h d -> p c (h d)"), ALU.add).then_inc(res_added, 1)

                def rstd_of(b):
                    hold(pool, g, averaged, b * QT + QT)
                    if not (isinstance(b, int) and b == 0):
                        hold(pool, g, x1_done, b * QT)
                    m.tensor_scalar(var_eps[:], mean_var[:, :, 1], EPS, None, ALU.add).then_inc(eps_added, 1)
                    hold(pool, g, eps_added, b + 1)
                    m.tensor_tensor(rstd[:], var_eps[:], g.minus_half[:].to_broadcast([P, QT]), ALU.pow).then_inc(rstd_done, 1)

                def split_context(s):
                    chunk = lambda part: part[:, bass.ds(s.lap, 1), s.buf, :].rearrange("p a d -> p (a d)")
                    whole = chunk(g.ctx_t[LOW])
                    m.tensor_copy(chunk(g.ctx_t[HIGH]), whole.bitcast(F32)).then_inc(context_high, 1)
                    hold(pool, g, context_high, s.tile + 1)
                    m.tensor_tensor(whole, whole.bitcast(F32), chunk(g.ctx_t[HIGH]).bitcast(F32), ALU.subtract)

                def body(s):
                    split_context(s)
                    if s.after(1):
                        add_attention(s.at(-1))
                        if s.buf == 0:
                            rstd_of(s.lap - 1)
                            scale_rows(pool, m, s.lap - 1)

                steps(pool, body)
                add_attention(Step(N - 1, U - 1, B - 1, U))
                rstd_of(B - 1)

            @block.scalar
            def _(act):
                a = nc.scalar

                def project(n, half, which):
                    if which == V:
                        if not (isinstance(n, int) and n < 2):
                            hold(act, g, pv_done, (n - 1) * 2 * QT)
                        else:
                            act.wait_ge(cleared, 4)
                        hold(act, g, v_projected, n + 1)
                        a.copy(v_one[:, half, :, :, 0:HD], ps_m[:, 0, :].rearrange("p (c h d) -> p c h d", c=QT, d=HD)).then_inc(v_copied, 1)
                        return
                    if not (isinstance(n, int) and n == 0):
                        hold(act, g, split_out, n * 32)
                    hold(act, g, projected, n * 2 + which + 1)
                    a.activation(hi[:, which, :], bank_of(isinstance(n, int) and n == 0, 2 + which), ACT.Copy, scale=SCALE if which == Q else 1.0).then_inc(hi_done, 1)

                def turn_x(b, c):
                    if not (isinstance(b, int) and b == 0):
                        hold(act, g, v_projected, b * 2)
                    hold(act, g, xt_turned, b * EC + c + 1)
                    a.copy(x_t[:, c, :], bank_of(isinstance(b, int) and b == 0, c)).then_inc(xt_copied, 1)

                def copy_max(s):
                    if s.after(1):
                        hold(act, g, t_done, s.tile * PER_T)
                    else:
                        act.wait_ge(rows_set, 3)
                    hold(act, g, max_turned, s.tile + 1)
                    a.copy(neg_max_t[0:8, :], ps_m[0:8, 0, :]).then_inc(max_copied, 1)

                def copy_heads(s):
                    if s.after(1):
                        hold(act, g, o_turned, s.tile)
                    hold(act, g, pv_done, s.tile * QT + QT)
                    a.copy(o_t[:], ps_o[:, 0, :]).then_inc(o_copied, 1)

                def exponentials(s, j):
                    i, pair = j // 2, j % 2
                    w = T - i * P
                    if not (isinstance(s.tile, int) and s.tile == 0 and i < 2):
                        hold(act, g, pv_done, s.tile * QT + i - 1)
                    hold(act, g, t_done, s.tile * PER_T + j + 1)
                    a.activation(exps[:, i % 2, 2 * pair:2 * pair + 2, 0:w], ps_t[:, 2 * pair:2 * pair + 2, 0:w],
                                 ACT.Exp).then_inc(exp_done, 1)

                for c in range(EC):
                    turn_x(0, c)
                for which in (Q, K, V):
                    project(0, 0, which)
                copy_max(Step(0, 0, 0, U))

                def body(s):
                    for j in range(PER_T):
                        if leads_group(s) and j in (Q, K, V):
                            project(group(s) + 1, 1 - s.buf // 2, j)
                        if turns_x(s) and j in X:
                            turn_x(s.lap + 1, X.index(j))
                        if j == LAST_V + 1 and s.after(1):
                            copy_heads(s.at(-1))
                        exponentials(s, j)
                        if j == MAX_TURNED and s.at(1).within(N):
                            copy_max(s.at(1))

                steps(act, body)
                copy_heads(Step(N - 1, U - 1, B - 1, U))

            @block.vector
            def _(dve):
                v = nc.vector
                def split(n, which):
                    hold(dve, g, hi_done, n * 2 + which + 1)
                    v.scalar_tensor_tensor(out=lo[:, which, :], in0=bank_of(isinstance(n, int) and n == 0, 2 + which), scalar=SCALE if which == Q else 1.0,
                                           in1=hi[:, which, :].bitcast(F32), op0=ALU.mult, op1=ALU.subtract).then_inc(lo_done, 1)

                def find_max(s, unit):
                    h, i = unit // QT, unit % QT
                    hold(dve, g, s_done, s.tile * PER_S + unit + 1)
                    v.tensor_reduce(maxima[:, s.buf % 2, i, h:h + 1], ps_s[:, unit % 2, 0:(i + 1) * P], AX.X,
                                    ALU.max).then_inc(max_done, 1)

                def split_max(s):
                    b = s.buf % 2
                    if s.after(1):
                        hold(dve, g, max_turned, s.tile)
                    hold(dve, g, max_done, (s.tile + 1) * PER_S)
                    v.tensor_scalar(neg_max[:, :, 0, :], maxima[:, b], -1.0, None, ALU.mult).then_inc(max_hi, 1)
                    hold(dve, g, max_hi, s.tile + 1)
                    v.scalar_tensor_tensor(out=neg_max[:, :, 1, :], in0=maxima[:, b], scalar=-1.0,
                                           in1=neg_max[:, :, 0, :].bitcast(F32), op0=ALU.mult, op1=ALU.subtract).then_inc(max_lo, 1)

                def norm_heads(s):
                    turned = ps_m[:, 0, :].rearrange("p (c h w) -> p c h w", c=QT, w=VW)
                    if s.after(1):
                        hold(dve, g, res_added, s.tile)
                    hold(dve, g, o_turned, s.tile + 1)
                    v.reciprocal(sums_inv[:], turned[:, :, :, HD]).then_inc(inv_done, 1)
                    hold(dve, g, inv_done, s.tile + 1)
                    v.tensor_tensor(o_norm[:].rearrange("p c h d -> p (c h) d"),
                                    turned[:, :, :, 0:HD].rearrange("p c h d -> p (c h) d"),
                                    sums_inv[:].rearrange("p c h -> p (c h)").unsqueeze(2).to_broadcast([P, QT * 4, HD]),
                                    ALU.mult).then_inc(o_normed, 1)

                def norm_rows(b):
                    hold(dve, g, res_added, b * QUADS + QUADS)
                    for c in range(QT):
                        v.bn_stats(stats[:, c, :], res[:, c, :]).then_inc(stats_done, 1)
                    for c in range(QT):
                        hold(dve, g, stats_done, b * QT + c + 1)
                        v.bn_aggr(mean_var[:, c, :], stats[:, c, :]).then_inc(averaged, 1)

                for which in (Q, K):
                    split(0, which)
                dve.wait_ge(cleared, 4)
                for rows in (qs, ks):
                    v.tensor_scalar(rows[STACKED:P].rearrange("p a h t -> p (a h t)"),
                                    one_f[STACKED:P, 0:1].to_broadcast([P - STACKED, 2 * HG * T]), 0.0, None,
                                    ALU.mult).then_inc(rows_set, 1)
                v.tensor_scalar(neg_max_t[:], one_f[:].to_broadcast([P, T]), 0.0, None, ALU.mult).then_inc(rows_set, 1)
                v.tensor_tensor(head_rows[:], g.ident[:, 0:4], g.ident[:, 4:8], ALU.add).then_inc(rows_set, 1)
                dve.wait_ge(rows_set, 4)
                v.tensor_copy(of_head[:], head_rows[:].unsqueeze(2).to_broadcast([P, 4, P])).then_inc(rows_set, 1)
                for unit in range(PER_S):
                    find_max(Step(0, 0, 0, U), unit)
                split_max(Step(0, 0, 0, U))

                def body(s):
                    for j in range(PER_T):
                        if j == HEADS_TURNED + 1 and s.after(1):
                            norm_heads(s.at(-1))
                        for n in range(max(LEAD[j], 1)):
                            if n < LEAD[j] and s.at(1).within(N):
                                find_max(s.at(1), sum(LEAD[:j]) + n)
                            if n == 0 and leads_group(s) and j in (Q, K):
                                split(group(s) + 1, j)
                    if s.at(1).within(N):
                        split_max(s.at(1))
                    if s.after(1) and s.buf == 0:
                        norm_rows(s.lap - 1)

                steps(dve, body)
                norm_heads(Step(N - 1, U - 1, B - 1, U))
                norm_rows(B - 1)
                scale_rows(dve, v, B - 1)

            @block.tensor
            def _(pe):

                def turn_x(b, c):
                    first = isinstance(b, int) and b == 0
                    if not first and c:
                        hold(pe, g, xt_copied, b * EC + c)
                    elif not first:
                        hold(pe, g, x_arrived, b * 16)
                    for t in range(QT):
                        last = pe.transpose(bank_of(first, c)[:, t * P:(t + 1) * P], x_in[:, t, c * P:(c + 1) * P], g.ident[:])
                    last.then_inc(xt_turned, 1)

                def project(n, half, which):
                    first = isinstance(n, int) and n == 0
                    if which == Q:
                        if half == 0:
                            hold(pe, g, xt_copied, n * EC // 2 + EC)
                    elif not first:
                        hold(pe, g, hi_done, n * 2 + which)
                        hold(pe, g, lo_done, n * 2 + which)
                    if which != V:
                        for c in range(EC):
                            last = pe.matmul(bank_of(first, 2 + which), w_t[:, c, which, half * P:(half + 1) * P], x_t[:, c, :],
                                             start=(c == 0), stop=(c == EC - 1))
                        last.then_inc(projected, 1)
                    else:
                        for t in range(QT):
                            for c in range(EC):
                                last = pe.matmul(ps_m[:, 0, t * P:(t + 1) * P], x_t[:, c, t * P:(t + 1) * P],
                                                 w_t[:, c, 2, half * P:(half + 1) * P], start=(c == 0), stop=(c == EC - 1))
                        last.then_inc(v_projected, 1)

                def first_pass(s, unit):
                    h, i = unit // QT, unit % QT
                    half, head, w = s.buf // 2, (s.buf % 2) * 4 + h, (i + 1) * P
                    out = ps_s[:, unit % 2, 0:w]
                    if unit == 0 and s.buf % 2 == 0:
                        hold(pe, g, q_stacked[half], (s.lap + 1) * COPIES * 16)
                        hold(pe, g, k_stacked[half], (s.lap + 1) * COPIES * 16)
                    if s.after(1) or unit >= 2:
                        hold(pe, g, max_done, s.tile * PER_S + unit - 1)
                    pe.matmul(out, qs[:, half, head, i * P:(i + 1) * P], ks[:, half, head, 0:w], start=True, stop=False)
                    pe.matmul(out[:, i * P:w], ident_b[:], later_key[:], start=False, stop=True).then_inc(s_done, 1)

                def turn_max(s):
                    hold(pe, g, max_lo, s.tile + 1)
                    for i in range(QT):
                        last = pe.transpose(ps_m[0:8, 0, i * P:(i + 1) * P],
                                            neg_max[:, i].rearrange("p a h -> p (a h)").bitcast(F32), g.ident[:])
                    last.then_inc(max_turned, 1)

                def second_pass(s, i, pair, k):
                    half, w = s.buf // 2, T - i * P
                    unit = 2 * i + pair
                    if k == 0 and (s.after(1) or unit >= 2):
                        hold(pe, g, exp_done, s.tile * PER_T + unit - 1)
                    head = (s.buf % 2) * 4 + 2 * pair + k
                    out = ps_t[:, 2 * pair + k, 0:w]
                    pe.matmul(out, ks[:, half, head, i * P:(i + 1) * P], qs[:, half, head, i * P:T], start=True, stop=False)
                    pe.matmul(out[:, 0:P], ident_b[:], earlier_query[:], start=False, stop=False)
                    if unit == 0 and k == 0:
                        hold(pe, g, max_copied, s.tile + 1)
                        if not s.after(1):
                            pe.wait_ge(rows_set, 5)
                    last = pe.matmul(out, of_head[:, 2 * pair + k, :], neg_max_t[:, i * P:T], start=False, stop=True)
                    if k == 1:
                        last.then_inc(t_done, 1)

                def times_v(s, i):
                    half = s.buf // 2
                    if i == 0:
                        if s.buf % 2 == 0:
                            hold(pe, g, v_copied, group(s) + 1)
                        if s.after(1):
                            hold(pe, g, o_copied, s.tile)
                    hold(pe, g, exp_done, s.tile * PER_T + 2 * i + 2)
                    for h in range(4):
                        last = pe.matmul(ps_o[VW * h:VW * (h + 1), 0, i * P:T], v_one[:, half, i, (s.buf % 2) * 4 + h, :],
                                         exps[:, i % 2, h, 0:T - i * P], start=(i == 0), stop=(i == QT - 1), tile_position=(0, VW * h))
                    last.then_inc(pv_done, 1)

                def turn_heads(s):
                    hold(pe, g, o_copied, s.tile + 1)
                    n = s.at(1)
                    if leads_group(n):
                        hold(pe, g, v_copied, group(n) + 2)
                    elif turns_x(n):
                        hold(pe, g, xt_copied, n.lap * EC + 2 * EC)
                    elif n.within(N):
                        hold(pe, g, max_copied, n.tile + 1)
                    for i in range(QT):
                        last = pe.transpose(ps_m[:, 0, i * P:(i + 1) * P], o_t[:, i * P:(i + 1) * P], g.ident[:])
                    last.then_inc(o_turned, 1)

                for c in range(EC):
                    turn_x(0, c)
                for which in (Q, K, V):
                    project(0, 0, which)
                first = Step(0, 0, 0, U)
                pe.wait_ge(constants, 4)
                pe.wait_ge(rows_set, 2)
                for unit in range(PER_S):
                    first_pass(first, unit)
                pe.wait_ge(v_copied, 1)
                turn_max(first)

                def lead(s, j, n):
                    if n < LEAD[j] and s.at(1).within(N):
                        first_pass(s.at(1), sum(LEAD[:j]) + n)

                def body(s):
                    for j in range(PER_T):
                        if j in (Q, X[0]) and (leads_group(s) or turns_x(s)):
                            hold(pe, g, max_copied, s.tile + 1)
                        if leads_group(s) and j in (Q, K, V):
                            project(group(s) + 1, 1 - s.buf // 2, j)
                        if turns_x(s) and j in X:
                            turn_x(s.lap + 1, X.index(j))
                        if j == HEADS_TURNED and s.after(1):
                            turn_heads(s.at(-1))
                        lead(s, j, 0)
                        second_pass(s, j // 2, j % 2, 0)
                        lead(s, j, 1)
                        second_pass(s, j // 2, j % 2, 1)
                        lead(s, j, 2)
                        if j == MAX_TURNED and s.at(1).within(N):
                            if s.after(1):
                                hold(pe, g, o_normed, s.tile)
                            elif leads_group(s):
                                hold(pe, g, v_copied, group(s) + 2)
                            turn_max(s.at(1))
                        if j == LAST_V and s.after(1):
                            times_v(s.at(-1), QT - 1)
                        if j % 2 and j >= 3:
                            times_v(s, j // 2 - 1)

                steps(pe, body)
                final = Step(N - 1, U - 1, B - 1, U)
                times_v(final, QT - 1)
                pe.wait_ge(o_normed, N - 1)
                turn_heads(final)


def load_expert(sp, g, s):
    t = bass.ds(s.tile, 1)
    expert = sp.value_load(g.plan[0:1, 0, t], min_val=0, max_val=EXPERTS - 1)
    is_new = sp.value_load(g.plan[0:1, 1, t], min_val=0, max_val=1)
    slot = sp.value_load(g.plan[0:1, 2, t], min_val=0, max_val=WEIGHT_SLOTS - 1)
    e, b = bass.ds(expert, 1), bass.ds(slot, 1)
    sp.dma_start(g.up_w[:, b, :].rearrange("p a (c f) -> p (a c) f", c=DC),
                 g.up_dram[e, :, :].rearrange("a (c p) f -> p (a c) f", p=P),
                 cond=is_new).then_inc(g.weights_in[s.buf], 16)
    sp.dma_start(g.down_w[:, b, :].rearrange("p a (c n) -> p (a c) n", c=IC),
                 g.down_dram[e, :, :].rearrange("a (c p) n -> p (a c) n", p=IW),
                 cond=is_new).then_inc(g.weights_in[s.buf], 16)


def stage_dispatch(nc, g):
    J, K, E = SORT_TILES, TOP_K, EXPERTS
    U = 4
    with ExitStack() as ctx:
        def sb(name, shape, dt=F32):
            return ctx.enter_context(nc.sbuf_tensor(f"dispatch_{name}", shape, dt))

        def sem(name):
            return ctx.enter_context(nc.semaphore(f"dispatch_{name}"))

        top = g.top_logits[:, :, 0:K]
        shifted = sb("shifted", [P, J, K])
        powers = sb("powers", [P, J, K])
        weight = sb("weight", [P, J, K])
        weight_sum = sb("weight_sum", [P, J])
        w = sort_buffers(sb, "moe", E, J)
        picked = sb("picked", [P, J, K, E])
        pair_slot = sb("pair_slot", [P, J, K])
        tile_of = sb("tile_of", [P, J, K])
        place_of = sb("place_of", [P, J, K])
        tmp_i = sb("tmp_i", [P, J * K], I32)
        hidden = sb("hidden", [P, J])
        at_place = sb("at_place", [P, U, K, P])
        at_tile = sb("at_tile", [P, U, K, PLAN])
        at_tile_row = sb("at_tile_row", [P, U, K, 2, PLAN])
        pair_up = sb("pair_up", [P, J, K])
        row_up = sb("row_up", [P, PLAN])
        empty = sb("empty", [P, PLAN])
        row_of = sb("row_of", [P, PLAN])
        pair_i = sb("pair_i", [P, PLAN], I32)
        end_of = sb("end_of", [E, 1])
        ended = sb("ended", [E, PLAN])
        expert_of = sb("expert_of", [1, PLAN])
        ones_t = sb("ones_t", [1, PLAN])
        changed = sb("changed", [1, PLAN])
        changes = sb("changes", [1, PLAN])
        changes_i = sb("changes_i", [1, PLAN], I32)
        used = sb("used", [1, PLAN])
        n_groups = sb("n_groups", [1, 1])
        half = E // 2
        ps_rank = ctx.enter_context(nc.psum_tensor("ps_rank", [P, 2, 512], F32))
        ps_sum = ctx.enter_context(nc.psum_tensor("ps_sum", [P, 2, 512], F32))
        ps_table = ctx.enter_context(nc.psum_tensor("ps_table", [P, 512], F32))
        ps_ends = ctx.enter_context(nc.psum_tensor("ps_ends", [P, 512], F32))
        ps_plan = ctx.enter_context(nc.psum_tensor("ps_plan", [P, 512], F32))

        v_chain = sem("v_chain")
        shift_ready, exp_ready, summed, ranked = sem("shift_ready"), sem("exp_ready"), sem("summed"), sem("ranked")
        ends_known, ends_turned, ends_compared, ends_counted = sem("ends_known"), sem("ends_turned"), sem("ends_compared"), sem("ends_counted")
        plan_made, tiles_at, places_at = sem("plan_made"), sem("tiles_at"), sem("places_at")
        numbers_at, weights_at = sem("numbers_at"), sem("weights_at")
        table_used, tabled, x2_in = sem("table_used"), sem("tabled"), sem("x2_in")

        with nc.Block() as block:
            @block.sync
            def _(sp):
                for c in range(0, TOK_TILES, 4):
                    sp.dma_start(g.x2_by_token[:, c:c + 4, :],
                                 g.x2_rows[c * P:(c + 4) * P, :].rearrange("(c p) d -> p c d", p=P)).then_inc(x2_in, 16)
                sp.wait_ge(plan_made, 1)
                for t in range(WEIGHT_SLOTS):
                    load_expert(sp, g, Step(t, t, 0, WEIGHT_SLOTS))
                sp.wait_ge(x2_in, TOK_TILES // 4 * 16)

            @block.gpsimd
            def _(pool):
                def number_tiles(s):
                    if s.after(U):
                        hold(pool, g, table_used, s.tile - (U - 1))
                    hold(pool, g, tiles_at, s.tile + 1)
                    number = pair_up[:, bass.ds(s.tile, 1), :].rearrange("p a k -> p (a k)")
                    nc.gpsimd.tensor_tensor(at_tile_row[:, s.buf, :, 0, :], at_tile[:, s.buf],
                                            number.unsqueeze(2).to_broadcast([P, K, PLAN]), ALU.mult).then_inc(numbers_at, 1)

                run_steps(pool, J, U, U, 1, number_tiles)

            @block.scalar
            def _(act):
                act.wait_ge(shift_ready, 1)
                nc.scalar.activation(powers[:], shifted[:], ACT.Exp).then_inc(exp_ready, 1)

                def weigh_tiles(s):
                    if s.after(U):
                        hold(act, g, table_used, s.tile - (U - 1))
                    hold(act, g, tiles_at, s.tile + 1)
                    for k in range(K):
                        last = nc.scalar.activation(at_tile_row[:, s.buf, k, 1, :], at_tile[:, s.buf, k, :], ACT.Copy,
                                                    scale=weight[:, bass.ds(s.tile, 1), k:k + 1].rearrange("p a k -> p (a k)"))
                    last.then_inc(weights_at, 1)

                run_steps(act, J, U, U, 1, weigh_tiles)

            @block.vector
            def _(dve):
                v = nc.vector
                link = sequence(dve, v_chain)
                v.tensor_tensor(shifted[:], top, top[:, :, 0:1].to_broadcast([P, J, K]), ALU.subtract).then_inc(shift_ready, 1)
                link(v.tensor_tensor(pair_up[:], g.pair_offset[:].unsqueeze(1).to_broadcast([P, J, K]),
                                     g.slot_token_up[:].unsqueeze(2).to_broadcast([P, J, K]), ALU.add))
                dve.wait_ge(exp_ready, 1)
                link(v.tensor_reduce(weight_sum[:], powers[:], AX.X, ALU.add))
                link(v.reciprocal(weight_sum[:], weight_sum[:]))
                link(v.tensor_tensor(weight[:], powers[:], weight_sum[:].unsqueeze(2).to_broadcast([P, J, K]), ALU.mult))
                dve.wait_ge(summed, 1)
                dve.wait_ge(ranked, 1)
                halves = lambda ps: [(slice(i * half, (i + 1) * half),
                                      ps[:, i, 0:half * J].rearrange("p (g t) -> p g t", g=half)) for i in range(2)]
                slots_of_groups(nc, link, w, E, J, halves(ps_sum), halves(ps_rank))
                dve.sem_inc(ends_known, 1)
                link(v.tensor_tensor(picked[:], g.chosen[:],
                                     w.slot[:].rearrange("p e j -> p j e").unsqueeze(2).to_broadcast([P, J, K, E]), ALU.mult))
                dve.wait_ge(ends_turned, 1)
                link(v.tensor_copy(end_of[:], ps_ends[0:E, 0:1]))
                v.tensor_scalar(ended[:], g.count_t[0:E, :], end_of[:, 0:1], None, ALU.is_ge).then_inc(ends_compared, 1)
                link(v.tensor_reduce(pair_slot[:], picked[:], AX.X, ALU.add))
                flat = "p j k -> p (j k)"
                split_slot(nc, link, tile_of[:].rearrange(flat), place_of[:].rearrange(flat), tmp_i[:], pair_slot[:].rearrange(flat))
                link(v.tensor_scalar(hidden[:], g.slot_full[:], -1.0, 1000.0, ALU.add, ALU.mult))
                link(v.tensor_tensor(tile_of[:], tile_of[:], hidden[:].unsqueeze(2).to_broadcast([P, J, K]), ALU.add))

                dve.wait_ge(ends_counted, 1)
                link(v.tensor_scalar(expert_of[:], ps_plan[0:1, 0:PLAN], float(E - 1), None, ALU.min))
                link(v.memset(changed[:, 0:1], 1.0))
                link(v.memset(ones_t[:], 1.0))
                link(v.tensor_tensor(changed[:, 1:], expert_of[:, 1:], expert_of[:, 0:PLAN - 1], ALU.not_equal))
                link(v.tensor_tensor_scan(changes[:], ones_t[:], changed[:], -1.0, ALU.mult, ALU.add))
                link(v.tensor_copy(changes_i[:], changes[:]))
                link(v.tensor_scalar(g.plan[:, 2, :], changes_i[:], WEIGHT_SLOTS - 1, None, ALU.bitwise_and))
                link(v.tensor_copy(g.plan[:, 0, :], expert_of[:]))
                link(v.tensor_copy(g.plan[:, 1, :], changed[:]))
                link(v.tensor_scalar(used[:], ps_plan[0:1, 0:PLAN], float(E), None, ALU.is_lt))
                link(v.tensor_copy(g.plan[:, 3, :], used[:]))
                link(v.tensor_reduce(n_groups[:], used[:].rearrange("p (g t) -> p t g", t=GROUP)[:, 0, :], AX.X, ALU.add))
                link(v.tensor_copy(g.n_groups[:], n_groups[:]))
                dve.sem_inc(plan_made, 1)

                def place_pairs(s):
                    if s.after(U):
                        hold(dve, g, table_used, s.tile - (U - 1))
                        hold(dve, g, numbers_at, s.tile - (U - 1))
                        hold(dve, g, weights_at, s.tile - (U - 1))
                    of = lambda x: x[:, bass.ds(s.tile, 1), :].rearrange("p a k -> p (a k)")
                    v.tensor_tensor(at_tile[:, s.buf], g.count_t[:, 0:PLAN].unsqueeze(1).to_broadcast([P, K, PLAN]),
                                    of(tile_of).unsqueeze(2).to_broadcast([P, K, PLAN]), ALU.is_equal).then_inc(tiles_at, 1)
                    v.tensor_tensor(at_place[:, s.buf], g.count_p[:].unsqueeze(1).to_broadcast([P, K, P]),
                                    of(place_of).unsqueeze(2).to_broadcast([P, K, P]), ALU.is_equal).then_inc(places_at, 1)

                run_steps(dve, J, U, U, 1, place_pairs)
                dve.wait_ge(tabled, 1)
                link(v.tensor_copy(row_up[:], ps_table[:, 0:PLAN]))
                link(v.tensor_copy(g.pair_weight[:], ps_table[:, PLAN:2 * PLAN]))
                link(v.tensor_scalar(empty[:], row_up[:], 0.5, None, ALU.is_lt))
                link(v.tensor_scalar(pair_i[:], row_up[:], -1.0, 0.0, ALU.add, ALU.max))
                link(v.tensor_scalar(g.pair_token[:], pair_i[:], N_TOK - 1, None, ALU.bitwise_and))
                link(v.tensor_tensor(empty[:], empty[:], g.spare_pair_up[:], ALU.mult))
                link(v.tensor_tensor(row_of[:], row_up[:], empty[:], ALU.add))
                link(v.tensor_scalar(g.pair_row[:], row_of[:], -1.0, None, ALU.add))

            @block.tensor
            def _(pe):
                for ps, rows, done in ((ps_sum, g.ones, summed), (ps_rank, g.below, ranked)):
                    for i in range(2):
                        member = g.member[:, i * half:(i + 1) * half, :].rearrange("p g t -> p (g t)")
                        last = pe.matmul(ps[:, i, 0:half * J], rows[:], member, start=True, stop=True)
                    last.then_inc(done, 1)
                pe.wait_ge(ends_known, 1)
                pe.transpose(ps_ends[0:E, 0:P], w.tiles_end[:], g.ident[:]).then_inc(ends_turned, 1)
                pe.wait_ge(ends_compared, 1)
                pe.matmul(ps_plan[:, 0:PLAN], g.ones[0:E, :], ended[:], start=True, stop=True).then_inc(ends_counted, 1)

                def add_to_table(s):
                    hold(pe, g, places_at, s.tile + 1)
                    hold(pe, g, numbers_at, s.tile + 1)
                    hold(pe, g, weights_at, s.tile + 1)
                    for k in range(K):
                        first = isinstance(s.tile, int) and s.tile == 0 and k == 0
                        final = isinstance(s.tile, int) and s.tile == J - 1 and k == K - 1
                        last = pe.matmul(ps_table[:, 0:2 * PLAN], at_place[:, s.buf, k, :],
                                         at_tile_row[:, s.buf, k].rearrange("p a t -> p (a t)"), start=first, stop=final)
                    last.then_inc(table_used, 1)
                    if final:
                        pe.wait_ge(table_used, J)
                        pe.sem_inc(tabled, 1)

                run_steps(pe, J, U, U, 1, add_to_table)


def stage_experts(nc, g):
    with ExitStack() as ctx:
        def sb(name, shape, dt=F32):
            return ctx.enter_context(nc.sbuf_tensor(f"experts_{name}", shape, dt))

        def sem(name):
            return ctx.enter_context(nc.semaphore(f"experts_{name}"))

        def bank(name, n=1):
            return ctx.enter_context(nc.psum_tensor(f"experts_{name}", [P, n, 512], F32))

        U = GROUP
        index = sb("index", [P, U], I32)
        out_index = sb("out_index", [P, U], I32)
        rows = sb("rows", [P, U, D])
        x_t = sb("x_t", [P, 2, DC, P])
        silu = sb("silu", [P, 2, INTER])
        h = sb("h", [P, 2, INTER])
        h_t = sb("h_t", [IW, IC, P])
        y = sb("y", [P, U, D])
        ps_x, ps_h, ps_gu, ps_y = bank("ps_x", 2), bank("ps_h", 2), bank("ps_gu", 2), bank("ps_y", 2)

        rows_in = [sem(f"rows_in{u}") for u in range(U)]
        stored = [sem(f"stored{u}") for u in range(U)]
        index_set, out_index_set = sem("index_set"), sem("out_index_set")
        x_turned, xt_copied, gu_done, silu_done = sem("x_turned"), sem("xt_copied"), sem("gu_done"), sem("silu_done")
        h_done, h_turned, ht_copied, y_done, y_scaled = sem("h_done"), sem("h_turned"), sem("ht_copied"), sem("y_done"), sem("y_scaled")

        def steps(eng, body):
            run_steps(eng, LEAST_GROUPS * U, U, U, 0, body)
            with eng.Fori(0, MOST_GROUPS - LEAST_GROUPS) as i:
                tile, lap = i * U + LEAST_GROUPS * U, i + LEAST_GROUPS
                has_pairs = eng.value_load(g.plan[0:1, 3, bass.ds(tile, 1)], min_val=0, max_val=1)
                with eng.If(has_pairs):
                    for u in range(U):
                        body(Step(tile + u, u, lap, U))

        def groups_run(eng):
            return eng.value_load(g.n_groups[0:1, 0:1], min_val=LEAST_GROUPS, max_val=MOST_GROUPS)

        with nc.Block() as block:
            @block.sync
            def _(sp):
                def load(s):
                    hold(sp, g, y_done, s.tile + 1)
                    load_expert(sp, g, s.at(U))

                steps(sp, load)
                groups = groups_run(sp)
                for u in range(U):
                    hold(sp, g, g.weights_in[u], groups * 32 + 32)

            @block.gpsimd
            def _(pool):
                def gather(s):
                    if s.after(U):
                        hold(pool, g, x_turned, s.tile - (U - 1))
                    nc.gpsimd.tensor_copy(index[:, s.buf:s.buf + 1], g.pair_token[:, bass.ds(s.tile, 1)]).then_inc(index_set, 1)
                    hold(pool, g, index_set, s.tile + 1)
                    nc.gpsimd.indirect_dma_start(
                        out=rows[:, s.buf, :], out_offset=None, in_=g.x2_rows[0:N_TOK, :],
                        in_offset=bass.IndirectOffsetOnAxis(ap=index[:, s.buf:s.buf + 1], axis=0),
                    ).then_inc(rows_in[s.buf], 16)

                def store(s):
                    if s.after(U):
                        hold(pool, g, stored[s.buf], s.lap * 16)
                    nc.gpsimd.tensor_copy(out_index[:, s.buf:s.buf + 1], g.pair_row[:, bass.ds(s.tile, 1)]).then_inc(out_index_set, 1)
                    hold(pool, g, out_index_set, s.tile + 1)
                    hold(pool, g, y_scaled, s.tile + 1)
                    nc.gpsimd.indirect_dma_start(
                        out=g.y_rows, out_offset=bass.IndirectOffsetOnAxis(ap=out_index[:, s.buf:s.buf + 1], axis=0),
                        in_=y[:, s.buf, :], in_offset=None,
                    ).then_inc(stored[s.buf], 16)

                for t in range(U):
                    gather(Step(t, t % U, t // U, U))

                def body(s):
                    gather(s.at(U))
                    store(s)

                steps(pool, body)
                groups = groups_run(pool)
                for u in range(U):
                    hold(pool, g, stored[u], groups * 16)
                    hold(pool, g, rows_in[u], groups * 16 + 16)

            @block.scalar
            def _(act):
                def xt(s):
                    b = s.buf % 2
                    if s.after(2):
                        hold(act, g, gu_done, s.tile - 1)
                    hold(act, g, x_turned, s.tile + 1)
                    nc.scalar.copy(x_t[:, b].rearrange("p c t -> p (c t)"), ps_x[:, b, :]).then_inc(xt_copied, 1)

                def silu_of(s):
                    b = s.buf % 2
                    if s.after(2):
                        hold(act, g, h_done, s.tile - 1)
                    hold(act, g, gu_done, s.tile + 1)
                    nc.scalar.activation(silu[:, b, :], ps_gu[:, b, 0:INTER], ACT.Silu).then_inc(silu_done, 1)

                def ht(s):
                    if s.after(1):
                        hold(act, g, y_done, s.tile)
                    hold(act, g, h_turned, s.tile + 1)
                    nc.scalar.copy(h_t[:].rearrange("p c t -> p (c t)"), ps_h[0:IW, s.buf % 2, 0:IC * P]).then_inc(ht_copied, 1)

                first = Step(0, 0, 0, U)
                xt(first)
                silu_of(first)
                xt(first.at(1))

                def body(s):
                    ht(s)
                    silu_of(s.at(1))
                    xt(s.at(2))

                steps(act, body)

            @block.vector
            def _(dve):
                v = nc.vector

                def gate(s):
                    b = s.buf % 2
                    if s.after(2):
                        hold(dve, g, h_turned, s.tile - 1)
                    hold(dve, g, silu_done, s.tile + 1)
                    v.tensor_tensor(h[:, b, :], ps_gu[:, b, INTER:2 * INTER], silu[:, b, :], ALU.mult).then_inc(h_done, 1)

                def scale(s):
                    if s.after(U):
                        hold(dve, g, stored[s.buf], s.lap * 16)
                    hold(dve, g, y_done, s.tile + 1)
                    v.tensor_scalar(y[:, s.buf, :], ps_y[:, s.buf % 2, :], g.pair_weight[:, bass.ds(s.tile, 1)], None,
                                    ALU.mult).then_inc(y_scaled, 1)

                gate(Step(0, 0, 0, U))

                def body(s):
                    gate(s.at(1))
                    scale(s)

                steps(dve, body)

            @block.tensor
            def _(pe):
                def turn_x(s):
                    b = s.buf % 2
                    hold(pe, g, rows_in[s.buf], (s.lap + 1) * 16)
                    if s.after(2):
                        hold(pe, g, xt_copied, s.tile - 1)
                    for c in range(DC):
                        last = pe.transpose(ps_x[:, b, c * P:(c + 1) * P], rows[:, s.buf, c * P:(c + 1) * P], g.ident[:])
                    last.then_inc(x_turned, 1)

                def slot_of(s):
                    return bass.ds(pe.value_load(g.plan[0:1, 2, bass.ds(s.tile, 1)], min_val=0, max_val=WEIGHT_SLOTS - 1), 1)

                def mm_up(s):
                    b = s.buf % 2
                    slot = slot_of(s)
                    if s.after(2):
                        hold(pe, g, h_done, s.tile - 1)
                    hold(pe, g, g.weights_in[s.buf], (s.lap + 1) * 32)
                    hold(pe, g, xt_copied, s.tile + 1)
                    for c in range(DC):
                        last = pe.matmul(ps_gu[:, b, 0:2 * INTER], x_t[:, b, c, :],
                                         g.up_w[:, slot, c * 2 * INTER:(c + 1) * 2 * INTER].rearrange("p a n -> p (a n)"),
                                         start=(c == 0), stop=(c == DC - 1))
                    last.then_inc(gu_done, 1)

                def turn_h(s):
                    b = s.buf % 2
                    hold(pe, g, h_done, s.tile + 1)
                    if s.after(2):
                        hold(pe, g, ht_copied, s.tile - 1)
                    for c in range(IC):
                        last = pe.transpose(ps_h[0:IW, b, c * P:(c + 1) * P], h[:, b, c * IW:(c + 1) * IW], g.ident[:])
                    last.then_inc(h_turned, 1)

                def mm_down(s):
                    b = s.buf % 2
                    slot = slot_of(s)
                    if s.after(2):
                        hold(pe, g, y_scaled, s.tile - 1)
                    hold(pe, g, ht_copied, s.tile + 1)
                    for c in range(IC):
                        last = pe.matmul(ps_y[:, b, :], h_t[:, c, :],
                                         g.down_w[:, slot, c * D:(c + 1) * D].rearrange("p a n -> p (a n)"),
                                         start=(c == 0), stop=(c == IC - 1))
                    last.then_inc(y_done, 1)

                first = Step(0, 0, 0, U)
                turn_x(first)
                mm_up(first)
                turn_x(first.at(1))

                def body(s):
                    turn_h(s)
                    mm_up(s.at(1))
                    turn_x(s.at(2))
                    mm_down(s)

                steps(pe, body)


def stage_finish(nc, g):
    with ExitStack() as ctx:
        def sb(name, shape, dt=F32):
            return ctx.enter_context(nc.sbuf_tensor(f"finish_{name}", shape, dt))

        def sem(name):
            return ctx.enter_context(nc.semaphore(f"finish_{name}"))

        N, U = TOK_TILES, 4
        ys = sb("ys", [P, U, TOP_K, D])
        parts = sb("parts", [P, U, 2, D])
        total = sb("total", [P, U, D])
        stats = sb("stats", [P, U, 6])
        mean_var = sb("mean_var", [P, U, 2])
        var_eps = sb("var_eps", [P, U])
        rstd = sb("rstd", [P, U])
        normed = sb("normed", [P, U, D])
        rows_in = [sem(f"rows_in{u}") for u in range(U)]
        stored = [sem(f"stored{u}") for u in range(U)]
        x2_added, halved, added = sem("x2_added"), sem("halved"), sem("added")
        shift = sb("shift", [P, U])
        stats_done, averaged, eps_added, rstd_done, shift_done, out_done = (
            sem("stats_done"), sem("averaged"), sem("eps_added"), sem("rstd_done"), sem("shift_done"), sem("out_done"))

        def steps(eng, body):
            run_steps(eng, N, U, U, 4, body)

        with nc.Block() as block:
            @block.sync
            def _(sp):
                y_by_token = g.y_rows[0:TOP_K * N_TOK, :].rearrange("(k t) d -> t k d", t=N_TOK)

                def load(s):
                    if s.after(U):
                        hold(sp, g, halved, s.tile - (U - 1))
                    rows = bass.ds(s.tile * P, P)
                    sp.dma_start(ys[:, s.buf], y_by_token[rows, :, :]).then_inc(rows_in[s.buf], 16)

                steps(sp, load)

            @block.scalar
            def _(act):
                def norm_out(s):
                    b = s.buf
                    if s.after(U):
                        hold(act, g, stored[b], s.lap * 16)
                    hold(act, g, shift_done, s.tile + 1)
                    nc.scalar.activation(normed[:, b, :], total[:, b, :], ACT.Identity, bias=shift[:, b:b + 1],
                                         scale=rstd[:, b:b + 1]).then_inc(out_done, 1)
                    hold(act, g, out_done, s.tile + 1)
                    act.dma_start(g.out_rows[bass.ds(s.tile * P, P), :], normed[:, s.buf, :]).then_inc(stored[s.buf], 16)

                steps(act, norm_out)
                for u in range(U):
                    act.wait_ge(stored[u], 16 * len(range(u, N, U)))

            @block.gpsimd
            def _(pool):
                def add(s):
                    b, last = s.buf, TOP_K - 1
                    hold(pool, g, rows_in[b], (s.lap + 1) * 16)
                    x2 = g.x2_by_token[:, bass.ds(s.tile, 1), :].rearrange("p a d -> p (a d)")
                    nc.gpsimd.tensor_tensor(ys[:, b, last, :], ys[:, b, last, :], x2, ALU.add).then_inc(x2_added, 1)

                def rstd_of(s):
                    b = s.buf
                    hold(pool, g, averaged, s.tile + 1)
                    if s.after(U):
                        hold(pool, g, out_done, s.tile - (U - 1))
                    nc.gpsimd.tensor_scalar(var_eps[:, b:b + 1], mean_var[:, b, 1:2], EPS, None, ALU.add).then_inc(eps_added, 1)
                    hold(pool, g, eps_added, s.tile + 1)
                    nc.gpsimd.tensor_tensor(rstd[:, b:b + 1], var_eps[:, b:b + 1], g.minus_half[:], ALU.pow).then_inc(rstd_done, 1)
                    hold(pool, g, rstd_done, s.tile + 1)
                    nc.gpsimd.tensor_scalar(shift[:, b:b + 1], mean_var[:, b, 0:1], rstd[:, b:b + 1], -1.0,
                                            ALU.mult, ALU.mult).then_inc(shift_done, 1)

                add(Step(0, 0, 0, U))

                def body(s):
                    if s.at(1).within(N):
                        add(s.at(1))
                    rstd_of(s)

                steps(pool, body)

            @block.vector
            def _(dve):
                v = nc.vector

                def norm_in(s):
                    b = s.buf
                    half = TOP_K // 2
                    hold(dve, g, x2_added, s.tile + 1)
                    v.tensor_tensor(parts[:, b], ys[:, b, 0:half, :], ys[:, b, half:TOP_K, :], ALU.add).then_inc(halved, 1)
                    hold(dve, g, halved, s.tile + 1)
                    if s.after(U):
                        hold(dve, g, out_done, s.tile - (U - 1))
                    v.tensor_tensor(total[:, b, :], parts[:, b, 0, :], parts[:, b, 1, :], ALU.add).then_inc(added, 1)
                    hold(dve, g, added, s.tile + 1)
                    v.bn_stats(stats[:, b, :], total[:, b, :]).then_inc(stats_done, 1)
                    hold(dve, g, stats_done, s.tile + 1)
                    v.bn_aggr(mean_var[:, b, :], stats[:, b, :]).then_inc(averaged, 1)

                steps(dve, norm_in)


def decoder_layer(nc, x, tokens, context, wq, wk, wv, gate, up, down, out):
    g = Tensors()
    g.x_dram, g.tokens, g.context, g.wq, g.wk, g.wv = x, tokens, context, wq, wk, wv
    g.gate_dram, g.up_dram, g.down_dram = gate, up, down
    g.out_rows = out.rearrange("b t d -> (b t) d")
    g.x1_rows = nc.dram_tensor("x1_rows", (N_TOK, D), F32).ap()
    g.x2_rows = nc.dram_tensor("x2_rows", (N_TOK + SLOTS, D), F32).ap()
    g.y_rows = nc.dram_tensor("y_rows", (TOP_K * N_TOK + PLAN * P, D), F32).ap()
    g.w_heads = nc.dram_tensor("w_heads", (3, EMB, EMB), F32).ap()
    g.split_rows = nc.dram_tensor("split_rows", (2, 2, 2, P, T), F32).ap()

    sb = nc.alloc_sbuf_tensor
    g.ident = sb("ident", [P, P], F32)
    g.ones = sb("ones", [P, P], F32)
    g.below = sb("below", [P, P], F32)
    g.count_p = sb("count_p", [P, P], F32)
    g.count_t = sb("count_t", [P, PLAN], F32)
    g.pair_offset = sb("pair_offset", [P, TOP_K], F32)
    g.spare_pair_up = sb("spare_pair_up", [P, PLAN], F32)
    g.minus_half = sb("minus_half", [P, 1], F32)
    g.gate = sb("gate_w", [P, DC, EXPERTS], F32)
    g.slot_token_up = sb("slot_token_up", [P, SORT_TILES], F32)
    g.x2_row_of_slot = sb("x2_row_of_slot", [P, SORT_TILES], I32)
    g.token_of_slot = sb("token_of_slot", [P, SORT_TILES], I32)
    g.slot_full = sb("slot_full", [P, SORT_TILES], F32)
    g.hash_of_tile = sb("hash_of_tile", [1, SORT_TILES], I32)
    g.top_logits = sb("top_logits", [P, SORT_TILES, 8], F32)
    g.plan = sb("plan", [1, 4, PLAN], I32)
    g.n_groups = sb("n_groups", [1, 1], I32)
    g.pair_weight = sb("pair_weight", [P, PLAN], F32)
    g.pair_row = sb("pair_row", [P, PLAN], I32)
    g.pair_token = sb("pair_token", [P, PLAN], I32)
    g.constant = nc.alloc_semaphore("constant")
    g.weights_in = [nc.alloc_semaphore(f"weights_in{u}") for u in range(WEIGHT_SLOTS)]

    g.ctx_t = tuple(sb(f"ctx_{n}", [P, HASHES, DC, D], F32R) for n in ("high", "low"))
    with nc.Block() as block:
        @block.gpsimd
        def _(pool):
            nc.gpsimd.memset(g.minus_half[:], -0.5).then_inc(g.constant, 1)

    with nc.sbuf_tensor("w_t", [P, EMB // P, 3, EMB], F32) as g.w_t, \
         nc.sbuf_tensor("x_in", [P, T // P, EMB], F32) as g.x_in:
        stage_sort(nc, g)
        stage_attention(nc, g)
    g.chosen = sb("chosen", [P, SORT_TILES, TOP_K, EXPERTS], F32)
    g.member = sb("member", [P, EXPERTS, SORT_TILES], F32)
    stage_hash_ffn(nc, g)
    g.x2_by_token = g.ctx_t[HIGH][:].bitcast(F32).rearrange("p e c d -> p (e c) d")
    with nc.sbuf_tensor("up_w", [P, WEIGHT_SLOTS, DC * 2 * INTER], F32) as g.up_w, \
         nc.sbuf_tensor("down_w", [IW, WEIGHT_SLOTS, IC * D], F32) as g.down_w:
        stage_dispatch(nc, g)
        stage_experts(nc, g)
    stage_finish(nc, g)


_INS = ["x", "itok_BxS_13_99985", "ctx_2048", "L0_attn_Wq", "L0_attn_Wk", "L0_attn_Wv",
        "L0_ffn_gate", "L0_ffn_gate_up_proj", "L0_ffn_down_proj"]


def kernel(**inputs):
    import numpy as _np
    import concourse.bacc as _bacc
    from concourse import mybir as _mybir
    from concourse.bass_utils import run_bass_kernel_spmd as _run

    nc = _bacc.Bacc("TRN2", target_bir_lowering=False, num_devices=1)
    arrays, args = {}, []
    for name in _INS:
        a = _np.ascontiguousarray(inputs[name])
        arrays[f"in_{name}_dram"] = a
        args.append(nc.dram_tensor(f"in_{name}_dram", a.shape, _mybir.dt.from_np(a.dtype), kind="ExternalInput").ap())
    args.append(nc.dram_tensor("out_0_dram", (B, T, D), _mybir.dt.float32, kind="ExternalOutput").ap())
    decoder_layer(nc, *args)
    r = _run(nc, [arrays], core_ids=[0])
    return r.results[0]["out_0_dram"]
```
